# Optimizing a Trainium2 kernel written in Bass

```python
import numpy as np
import jax
import jax.numpy as jnp

def _softmax(x, axis=-1):
    return jax.nn.softmax(x, axis=axis)

def _gelu(x):
    return jax.nn.gelu(x, approximate=True)

def _silu(x):
    return jax.nn.silu(x)

def _sigmoid(x):
    return jax.nn.sigmoid(x)

def _layernorm(x, axis=-1, eps=1e-05):
    m = jnp.mean(x, axis=axis, keepdims=True)
    v = jnp.var(x, axis=axis, keepdims=True)
    return (x - m) / jnp.sqrt(v + eps)

def _scatter_add(tgt, idx, src, axis=0):
    return tgt.at[idx].add(src)

def _segment_sum(src, seg, n):
    return jax.ops.segment_sum(src, seg, n)
kernel_name = 'mk_vit_tower_cls_d1_tok_img1024_r4_2f946e'

def setup_inputs(seed: int=0):
    np.random.seed(seed)
    _w = jnp.asarray

    def _rec_inputs():
        import jax
        import jax.numpy as jnp
        _rk = jax.random.key(seed)
        x = -0.00016672 + 0.999947 * jax.random.normal(jax.random.fold_in(_rk, 1), (64, 3, 96, 96), jnp.float32)
        cls_tok = 0.02 * jax.random.normal(jax.random.fold_in(_rk, 5), (1, 1, 256), jnp.float32)
        return (x, cls_tok)
    x, cls_tok = _rec_inputs()

    def _L0_tok_setup():
        import jax, jax.numpy as jnp
        import numpy as np
        B, C, H, W_IMG = (64, 3, 96, 96)
        P = 16
        EMBED = 256
        PATCH_DIM = C * P * P
        key = jax.random.key(seed)
        k1, k2 = jax.random.split(key)
        x = jax.random.normal(k1, (B, C, H, W_IMG), dtype=jnp.float32)
        W = jax.random.normal(k2, (PATCH_DIM, EMBED), dtype=jnp.float32) * (1.0 / np.sqrt(PATCH_DIM))
        b = jnp.zeros((EMBED,), dtype=jnp.float32)
        return {'x': x, 'W': W, 'b': b}
    _L0_tok_all = _L0_tok_setup()
    _L0_tok_in = {k: v for k, v in _L0_tok_all.items() if k in ('W', 'b')}
    del _L0_tok_all

    def _L0_attn_setup():
        import jax, jax.numpy as jnp
        import numpy as np
        D_MODEL = 256
        NHEAD = 16
        HID = int(D_MODEL * 4.0 * (2.0 / 3.0))
        EPS = 1e-05

        def _ln(x, w, b):
            m = jnp.mean(x, axis=-1, keepdims=True)
            v = jnp.mean((x - m) ** 2, axis=-1, keepdims=True)
            return (x - m) / jnp.sqrt(v + EPS) * w + b
        key = jax.random.key(seed)
        ks = jax.random.split(key, 10)
        w = lambda k, shape: jax.random.normal(k, shape, jnp.float32) * 0.02
        D = D_MODEL
        inp = {'x': jax.random.normal(ks[0], (1, 512, D), jnp.float32), 'norm1_w': jnp.ones((D,), jnp.float32), 'norm1_b': jnp.zeros((D,), jnp.float32), 'wq': w(ks[1], (D, D)), 'bq': jnp.zeros((D,), jnp.float32), 'wk': w(ks[2], (D, D)), 'bk': jnp.zeros((D,), jnp.float32), 'wv': w(ks[3], (D, D)), 'bv': jnp.zeros((D,), jnp.float32), 'wg': w(ks[4], (D, D)), 'bg': jnp.zeros((D,), jnp.float32), 'wo': w(ks[5], (D, D)), 'bo': jnp.zeros((D,), jnp.float32), 'gn_w': jnp.ones((D,), jnp.float32), 'gn_b': jnp.zeros((D,), jnp.float32), 'norm2_w': jnp.ones((D,), jnp.float32), 'norm2_b': jnp.zeros((D,), jnp.float32), 'w_in': w(ks[6], (D, 2 * HID)), 'b_in': jnp.zeros((2 * HID,), jnp.float32), 'w_out': w(ks[7], (HID, D)), 'b_out': jnp.zeros((D,), jnp.float32)}
        return inp
    _L0_attn_all = _L0_attn_setup()
    _L0_attn_in = {k: v for k, v in _L0_attn_all.items() if k in ('norm1_w', 'norm1_b', 'wq', 'bq', 'wk', 'bk', 'wv', 'bv', 'wg', 'bg', 'wo', 'bo', 'gn_w', 'gn_b', 'norm2_w', 'norm2_b', 'w_in', 'b_in', 'w_out', 'b_out')}
    del _L0_attn_all

    def _L0_ffn_setup():
        import jax, jax.numpy as jnp
        import numpy as np
        from jax import lax
        HIDDEN = 256
        INTER = 128
        E = 64
        K = 6
        G = 8
        TG = 4
        NSH = 2
        ISH = INTER * NSH

        def _moe_forward(hidden_states, gate_w, gate_bias, eg_w, eu_w, ed_w, sg_w, su_w, sd_w):
            B, S, H = hidden_states.shape
            x = hidden_states.reshape(-1, H)
            T = x.shape[0]
            shared = jax.nn.silu(x @ sg_w.T) * (x @ su_w.T) @ sd_w.T
            logits = x @ gate_w.T
            scores = jax.nn.sigmoid(logits) + gate_bias
            group_scores = scores.reshape(T, G, E // G).max(axis=-1)
            _, sel_groups = lax.top_k(group_scores, TG)
            group_mask = jnp.zeros((T, G), scores.dtype).at[jnp.arange(T)[:, None], sel_groups].set(1.0)
            mask = jnp.repeat(group_mask, E // G, axis=1)
            masked_scores = scores * mask
            topk_w, topk_i = lax.top_k(masked_scores, K)
            topk_w = topk_w / (topk_w.sum(axis=-1, keepdims=True) + 1e-08)
            comb = jnp.zeros((T, E), x.dtype).at[jnp.arange(T)[:, None], topk_i].add(topk_w)
            h = jax.nn.silu(jnp.einsum('th,eih->eti', x, eg_w)) * jnp.einsum('th,eih->eti', x, eu_w)
            routed = jnp.einsum('eti,ehi,te->th', h, ed_w, comb)
            return (shared + routed).reshape(B, S, H)
        key = jax.random.key(seed)
        ks = jax.random.split(key, 9)
        s = 0.02
        return {'hidden_states': jax.random.normal(ks[0], (1, 256, HIDDEN), jnp.float32), 'gate_w': jax.random.normal(ks[1], (E, HIDDEN), jnp.float32) * s, 'gate_bias': jnp.zeros((E,), jnp.float32), 'eg_w': jax.random.normal(ks[2], (E, INTER, HIDDEN), jnp.float32) * s, 'eu_w': jax.random.normal(ks[3], (E, INTER, HIDDEN), jnp.float32) * s, 'ed_w': jax.random.normal(ks[4], (E, HIDDEN, INTER), jnp.float32) * s, 'sg_w': jax.random.normal(ks[5], (ISH, HIDDEN), jnp.float32) * s, 'su_w': jax.random.normal(ks[6], (ISH, HIDDEN), jnp.float32) * s, 'sd_w': jax.random.normal(ks[7], (HIDDEN, ISH), jnp.float32) * s}
    _L0_ffn_all = _L0_ffn_setup()
    _L0_ffn_in = {k: v for k, v in _L0_ffn_all.items() if k in ('gate_w', 'gate_bias', 'eg_w', 'eu_w', 'ed_w', 'sg_w', 'su_w', 'sd_w')}
    del _L0_ffn_all
    return {'x': x, 'cls_tok': cls_tok, 'L0_tok_W': _L0_tok_in['W'], 'L0_tok_b': _L0_tok_in['b'], 'L0_attn_norm1_w': _L0_attn_in['norm1_w'], 'L0_attn_norm1_b': _L0_attn_in['norm1_b'], 'L0_attn_wq': _L0_attn_in['wq'], 'L0_attn_bq': _L0_attn_in['bq'], 'L0_attn_wk': _L0_attn_in['wk'], 'L0_attn_bk': _L0_attn_in['bk'], 'L0_attn_wv': _L0_attn_in['wv'], 'L0_attn_bv': _L0_attn_in['bv'], 'L0_attn_wg': _L0_attn_in['wg'], 'L0_attn_bg': _L0_attn_in['bg'], 'L0_attn_wo': _L0_attn_in['wo'], 'L0_attn_bo': _L0_attn_in['bo'], 'L0_attn_gn_w': _L0_attn_in['gn_w'], 'L0_attn_gn_b': _L0_attn_in['gn_b'], 'L0_attn_norm2_w': _L0_attn_in['norm2_w'], 'L0_attn_norm2_b': _L0_attn_in['norm2_b'], 'L0_attn_w_in': _L0_attn_in['w_in'], 'L0_attn_b_in': _L0_attn_in['b_in'], 'L0_attn_w_out': _L0_attn_in['w_out'], 'L0_attn_b_out': _L0_attn_in['b_out'], 'L0_ffn_gate_w': _L0_ffn_in['gate_w'], 'L0_ffn_gate_bias': _L0_ffn_in['gate_bias'], 'L0_ffn_eg_w': _L0_ffn_in['eg_w'], 'L0_ffn_eu_w': _L0_ffn_in['eu_w'], 'L0_ffn_ed_w': _L0_ffn_in['ed_w'], 'L0_ffn_sg_w': _L0_ffn_in['sg_w'], 'L0_ffn_su_w': _L0_ffn_in['su_w'], 'L0_ffn_sd_w': _L0_ffn_in['sd_w']}

def reference(x, cls_tok, L0_tok_W, L0_tok_b, L0_attn_norm1_w, L0_attn_norm1_b, L0_attn_wq, L0_attn_bq, L0_attn_wk, L0_attn_bk, L0_attn_wv, L0_attn_bv, L0_attn_wg, L0_attn_bg, L0_attn_wo, L0_attn_bo, L0_attn_gn_w, L0_attn_gn_b, L0_attn_norm2_w, L0_attn_norm2_b, L0_attn_w_in, L0_attn_b_in, L0_attn_w_out, L0_attn_b_out, L0_ffn_gate_w, L0_ffn_gate_bias, L0_ffn_eg_w, L0_ffn_eu_w, L0_ffn_ed_w, L0_ffn_sg_w, L0_ffn_su_w, L0_ffn_sd_w):
    import jax
    import jax.numpy as jnp

    def _L0_tok_ref(x, W, b):
        import jax, jax.numpy as jnp
        import numpy as np
        B, C, H, W_IMG = (64, 3, 96, 96)
        P = 16
        EMBED = 256
        PATCH_DIM = C * P * P
        Bn, Cn, Hn, Wn = x.shape
        gh, gw = (Hn // P, Wn // P)
        patches = x.reshape(Bn, Cn, gh, P, gw, P)
        patches = patches.transpose(0, 2, 4, 1, 3, 5)
        patches = patches.reshape(Bn, gh * gw, Cn * P * P)
        return jnp.einsum('bnd,de->bne', patches, W) + b

    def _L0_attn_ref(x, norm1_w, norm1_b, wq, bq, wk, bk, wv, bv, wg, bg, wo, bo, gn_w, gn_b, norm2_w, norm2_b, w_in, b_in, w_out, b_out):
        import jax, jax.numpy as jnp
        import numpy as np
        D_MODEL = 256
        NHEAD = 16
        HID = int(D_MODEL * 4.0 * (2.0 / 3.0))
        EPS = 1e-05

        def _ln(x, w, b):
            m = jnp.mean(x, axis=-1, keepdims=True)
            v = jnp.mean((x - m) ** 2, axis=-1, keepdims=True)
            return (x - m) / jnp.sqrt(v + EPS) * w + b
        B, S, D = x.shape
        H = NHEAD
        hd = D // H
        xn = _ln(x, norm1_w, norm1_b)
        q = (xn @ wq + bq).reshape(B, S, H, hd).transpose(0, 2, 1, 3)
        k = (xn @ wk + bk).reshape(B, S, H, hd).transpose(0, 2, 1, 3)
        v = (xn @ wv + bv).reshape(B, S, H, hd).transpose(0, 2, 1, 3)
        gamma = 1.0 - jnp.exp2(-5.0 - jnp.arange(H, dtype=jnp.float32))
        n = jnp.arange(S)
        diff = (n[:, None] - n[None, :]).astype(jnp.float32)
        Dmat = jnp.where(diff >= 0, jnp.exp(jnp.log(gamma)[:, None, None] * diff), 0.0)
        scores = jnp.einsum('bhnd,bhmd->bhnm', q, k) * hd ** (-0.5)
        ret = jnp.einsum('bhnm,bhmd->bhnd', scores * Dmat, v)
        ret = ret.transpose(0, 2, 1, 3)
        mu = jnp.mean(ret, axis=-1, keepdims=True)
        var = jnp.mean((ret - mu) ** 2, axis=-1, keepdims=True)
        gn = ((ret - mu) / jnp.sqrt(var + EPS)).reshape(B, S, D) * gn_w + gn_b
        gate = jax.nn.silu(xn @ wg + bg)
        h = gate * gn @ wo + bo
        x = x + h
        x2 = _ln(x, norm2_w, norm2_b)
        uv = x2 @ w_in + b_in
        u, g = jnp.split(uv, 2, axis=-1)
        x = x + (jax.nn.silu(u) * g @ w_out + b_out)
        return x

    def _L0_ffn_ref(hidden_states, gate_w, gate_bias, eg_w, eu_w, ed_w, sg_w, su_w, sd_w):
        import jax, jax.numpy as jnp
        import numpy as np
        from jax import lax
        HIDDEN = 256
        INTER = 128
        E = 64
        K = 6
        G = 8
        TG = 4
        NSH = 2
        ISH = INTER * NSH

        def _moe_forward(hidden_states, gate_w, gate_bias, eg_w, eu_w, ed_w, sg_w, su_w, sd_w):
            B, S, H = hidden_states.shape
            x = hidden_states.reshape(-1, H)
            T = x.shape[0]
            shared = jax.nn.silu(x @ sg_w.T) * (x @ su_w.T) @ sd_w.T
            logits = x @ gate_w.T
            scores = jax.nn.sigmoid(logits) + gate_bias
            group_scores = scores.reshape(T, G, E // G).max(axis=-1)
            _, sel_groups = lax.top_k(group_scores, TG)
            group_mask = jnp.zeros((T, G), scores.dtype).at[jnp.arange(T)[:, None], sel_groups].set(1.0)
            mask = jnp.repeat(group_mask, E // G, axis=1)
            masked_scores = scores * mask
            topk_w, topk_i = lax.top_k(masked_scores, K)
            topk_w = topk_w / (topk_w.sum(axis=-1, keepdims=True) + 1e-08)
            comb = jnp.zeros((T, E), x.dtype).at[jnp.arange(T)[:, None], topk_i].add(topk_w)
            h = jax.nn.silu(jnp.einsum('th,eih->eti', x, eg_w)) * jnp.einsum('th,eih->eti', x, eu_w)
            routed = jnp.einsum('eti,ehi,te->th', h, ed_w, comb)
            return (shared + routed).reshape(B, S, H)
        return _moe_forward(hidden_states, gate_w, gate_bias, eg_w, eu_w, ed_w, sg_w, su_w, sd_w)
    h = _L0_tok_ref(x, L0_tok_W, L0_tok_b)
    h = jnp.concatenate([jnp.broadcast_to(cls_tok, (h.shape[0], 1, h.shape[2])), h], axis=1)
    h = h + _L0_attn_ref(_layernorm(h, axis=-1), L0_attn_norm1_w, L0_attn_norm1_b, L0_attn_wq, L0_attn_bq, L0_attn_wk, L0_attn_bk, L0_attn_wv, L0_attn_bv, L0_attn_wg, L0_attn_bg, L0_attn_wo, L0_attn_bo, L0_attn_gn_w, L0_attn_gn_b, L0_attn_norm2_w, L0_attn_norm2_b, L0_attn_w_in, L0_attn_b_in, L0_attn_w_out, L0_attn_b_out)
    h = h + _L0_ffn_ref(_layernorm(h, axis=-1), L0_ffn_gate_w, L0_ffn_gate_bias, L0_ffn_eg_w, L0_ffn_eu_w, L0_ffn_ed_w, L0_ffn_sg_w, L0_ffn_su_w, L0_ffn_sd_w)
    return h

_drawn_inputs = setup_inputs


def setup_inputs(seed=0):
    import zlib

    import numpy as np

    out = dict(_drawn_inputs(seed))
    spreads = {'L0_tok_b': (0.0, 0.1),
     'L0_attn_norm1_w': (1.0, 0.6),
     'L0_attn_norm1_b': (0.0, 0.8),
     'L0_attn_bq': (0.0, 0.8),
     'L0_attn_bk': (0.0, 0.656),
     'L0_attn_bv': (0.0, 0.724),
     'L0_attn_bg': (0.0, 0.8),
     'L0_attn_bo': (0.0, 0.1),
     'L0_attn_gn_w': (1.0, 0.6),
     'L0_attn_gn_b': (0.0, 0.8),
     'L0_attn_norm2_w': (1.0, 0.6),
     'L0_attn_norm2_b': (0.0, 0.8),
     'L0_attn_b_in': (0.0, 0.8),
     'L0_attn_b_out': (0.0, 0.1),
     'L0_ffn_gate_bias': (0.0, 0.8)}
    factors = {'L0_attn_w_in': 3.204,
     'L0_attn_w_out': 3.165,
     'L0_ffn_gate_w': 8.0,
     'L0_ffn_eg_w': 8.0,
     'L0_ffn_eu_w': 8.0,
     'L0_ffn_ed_w': 8.0,
     'L0_ffn_sg_w': 5.67,
     'L0_ffn_su_w': 6.305,
     'L0_ffn_sd_w': 4.864}
    for name, (base, spread) in spreads.items():
        noise = np.random.default_rng([zlib.crc32(name.encode()), seed]).standard_normal(out[name].shape)
        drawn = base * np.exp(spread * noise) if base else spread * noise
        out[name] = jnp.asarray(drawn.astype(out[name].dtype))
    for name, factor in factors.items():
        out[name] = (out[name] * factor).astype(out[name].dtype)
    return out
```

```python
from contextlib import ExitStack

import concourse.bass as bass
from concourse import mybir

F32 = mybir.dt.float32
BF16 = mybir.dt.bfloat16
I32 = mybir.dt.int32
U32 = mybir.dt.uint32
ALU = mybir.AluOpType
ACT = mybir.ActivationFunctionType
AX = mybir.AxisListType

SEQS, SEQ, D = 64, 37, 256
PER = 3
TP = PER * SEQ
NT = 22
NPAIR = NT // 2
TALL = NT * TP
KP = 6
NH, HD = 16, 16
HID, HM, NM = 682, 114, 6
MS = [HM] * (NM - 1) + [HID - HM * (NM - 1)]
NE, TOPK, NG, TOPG = 64, 6, 8, 4
EG = NE // NG
SLOT_BLOCKS = -(-TALL // 128)
UNROLL = 6
NBLK = (TALL * TOPK + NE * 127) // 128
NBLK = -(-NBLK // UNROLL) * UNROLL
TAB_BLOCKS = NE * SLOT_BLOCKS + 128
TKT = TAB_BLOCKS // 128
EPS = 1e-5
RSTD, MEAN, BOTH = 0, 1, 6

VEC = {}
_at = 0
for _name, _w in (("n1w", 2), ("n1b", 2), ("bq", 2), ("bk", 2), ("bg", 2), ("gnw", 2), ("gnb", 2),
                  ("n2w", 2), ("n2b", 2), ("b_u", NM), ("b_g", NM)):
    VEC[_name] = _at
    _at += _w
NVEC = _at
ROWS = ("bv", "bo", "b_out")


def later(t, k):
    return not isinstance(t, int) or t >= k


def build(nc, a, out):
    with ExitStack() as ctx:
        def sb(name, shape, dt=F32):
            return ctx.enter_context(nc.sbuf_tensor(name, shape, dt))

        def sem(name):
            return ctx.enter_context(nc.semaphore(name))

        x_rows = nc.dram_tensor("x_rows", (TALL, D), F32, kind="Internal").ap()
        slot_token = nc.dram_tensor("slot_token", (TAB_BLOCKS * 128, 1), F32, kind="Internal").ap()
        y_rows = nc.dram_tensor("y_rows", (NBLK * 128, D), F32, kind="Internal").ap()

        h = sb("h", [TP, NT, D])
        x = sb("x", [TP, NT, D])
        cen = sb("cen", [TP, NT, D])
        gateT = sb("gateT", [128, 2, TALL])
        st = sb("st", [TP, NT, 6])
        gvar = sb("gvar", [TP, NT, NH])
        grs = sb("grs", [TP, NT, NH])
        rs = sb("rs", [TP, 8, NT])
        half = sb("half", [TP, NT])

        w_tok = sb("w_tok", [128, KP, D])
        wqk = sb("wqk", [128, 2, 4, D])
        wo = sb("wo", [128, 2, D])
        w_in = sb("w_in", [128, 2, 2 * HID])
        w_out = sb("w_out", [HM, NM, D])
        sgu = sb("sgu", [128, 2, 2, D])
        sdw = sb("sdw", [128, 2, D])
        gw = sb("gw", [128, 2, NE])
        vec = sb("vec", [128, NVEC])
        rows = sb("rows", [TP, len(ROWS), D])
        pos = sb("pos", [TP, D])
        gbias = sb("gbias", [TP, NE])
        decay = sb("decay", [TP, NH, TP])
        hmask = sb("hmask", [128, 8])
        ident = sb("ident", [128, 128])
        tri = sb("tri", [TP, TP])
        trib = sb("trib", [TP, TP], BF16)
        onesb = sb("onesb", [TP, 128], BF16)
        io64 = sb("io64", [TP, NE])
        ebase = sb("ebase", [TP, NE])
        jcol = sb("jcol", [128, TKT])
        tid = sb("tid", [TP, NT])

        xn = [sb(f"xn{u}", [TP, D]) for u in range(2)]
        xT = sb("xT", [128, 2, 2 * TP])
        qT = [sb(f"qT{u}", [128, 2, TP]) for u in range(2)]
        kT = [sb(f"kT{u}", [128, 2, TP]) for u in range(2)]
        qm = [sb(f"qm{u}", [128, NH, TP]) for u in range(2)]
        vv = [sb(f"vv{u}", [TP, D]) for u in range(2)]
        ss = [sb(f"ss{u}", [TP, NH, TP]) for u in range(2)]
        gsum = [sb(f"gsum{u}", [TP, NH]) for u in range(2)]
        gsq = sb("gsq", [TP, D])
        q0, q1 = (qm[u][:, :, :].rearrange("p a b -> p (a b)") for u in range(2))
        pat = [q0[:, u * KP * TP:(u + 1) * KP * TP].rearrange("p (k t) -> p k t", k=KP) for u in range(2)]
        tab_zero = q1[:, 0:TAB_BLOCKS]
        su = [q1[:, u * 2 * TP:(u + 1) * 2 * TP] for u in range(2)]
        hT = q0[:, 0:NM * 2 * TP].rearrange("p (j t) -> p j t", j=NM)
        gx = [qT[u] for u in range(2)]
        gh = [kT[u] for u in range(2)]
        sc = [sb(f"sc{u}", [TP, NE]) for u in range(2)]
        gmx = sb("gmx", [TP, NG])
        top = sb("top", [TP, 8])
        idx = sb("idx", [TP, 8], U32)
        idf = sb("idf", [TP, 8])
        geq = sb("geq", [TP, TOPG, NG])
        gsel = sb("gsel", [TP, NG])
        msc = sb("msc", [TP, NE])
        etop = [sb(f"etop{u}", [TP, 8]) for u in range(2)]
        ss0 = ss[0][:, :, :].rearrange("p a b -> p (a b)")
        oh, prod = (ss0[:, u * TOPK * NE:(u + 1) * TOPK * NE].rearrange("p (k e) -> p k e", k=TOPK) for u in range(2))
        sel = [sb(f"sel{u}", [TP, NE], BF16) for u in range(2)]
        selsum = sb("selsum", [TP, NT + 1, NE], BF16)
        smap = sb("smap", [TP, NE])
        slf = sb("slf", [TP, TOPK])
        slot = sb("slot", [TP, NT, TOPK])
        chosen = sb("chosen", [TP, NT, TOPK])
        yrow = sb("yrow", [TP, NT, TOPK], I32)
        shift = sb("shift", [TP, NE])
        slc = [sb(f"slc{u}", [TP, TOPK], I32) for u in range(2)]
        tic = [sb(f"tic{u}", [TP, 1]) for u in range(2)]
        wk = sb("wk", [TP, NT, TOPK])
        wsum = sb("wsum", [TP, 2])
        nbf = sb("nbf", [128, NE])
        nbi = sb("nbi", [128, NE], I32)
        bend = sb("bend", [128, NE])
        ones64 = sb("ones64", [128, NE])
        le = sb("le", [128, 2, NE])
        lb = sb("lb", [128, 2, NE])
        bcol = sb("bcol", [128, 2])
        ecol = sb("ecol", [128, 2])
        scol = sb("scol", [128, 2])
        vb = q0[:, 444:956].rearrange("p (a b) -> p a b", a=4)
        rowf = q0[:, 956:1468].rearrange("p (a b) -> p a b", a=2)
        rowi = sb("rowi", [1, 2, 256], I32)
        blk_idx = sb("blk_idx", [128, NBLK], I32)

        w_in_f = w_in[:, :, :].rearrange("p a b -> p (a b)")
        wqk_f = wqk[:, :, :, :].rearrange("p a b c -> p (a b c)")
        w_tok_f = w_tok[:, :, :].rearrange("p a b -> p (a b)")
        moe_w = [w_in_f[:, q * 768:(q + 1) * 768] for q in range(3)] + [w_tok_f[:, 0:768]]
        moe_w += [q1[:, q * 768:(q + 1) * 768] for q in range(2)]
        xg = [wqk_f[:, q * D:(q + 1) * D] for q in range(UNROLL)]
        xgT = [wqk_f[:, (6 + q) * D:(7 + q) * D].rearrange("p (a b) -> p a b", a=2) for q in range(2)]
        ys = [q0[:, 888 + q * D:888 + (q + 1) * D] for q in range(2)]
        sg, hb = ([w_tok_f[:, 768 + (2 * j + q) * 128:896 + (2 * j + q) * 128] for q in range(2)] for j in range(2))
        icol = [sb(f"icol{q}", [128, 1], I32) for q in range(UNROLL)]
        tab = q1[:, 0:TKT * 128].rearrange("p (k c) -> p k c", k=TKT)
        choose = [q0[:, 222 * u:222 * u + NBLK] for u in range(2)]
        arena = cen[:, :, :].rearrange("p a b -> p (a b)")
        cg = [arena[:, u * TOPK * D:(u + 1) * TOPK * D].rearrange("p (k n) -> p k n", k=TOPK) for u in range(2)]
        sh_s = [q0[:, u * 4 * TP:(u + 1) * 4 * TP].rearrange("p (a b) -> p a b", a=2) for u in range(2)]

        bank = [ctx.enter_context(nc.psum_tensor(f"bank{i}", [128, 512], F32)) for i in range(8)]

        S = {}
        for name in ("consts", "weights", "posrow", "table_zero", "table_cleared", "setup",
                     "embedded", "h_ready", "h_stats", "pool_step", "norms_ready",
                     "xn_ready", "x0_ready", "x0b_ready", "xnT_done", "xT_ready", "qk_done", "gate_done",
                     "v_done", "qk_read", "gate_read", "qm0_ready", "qm1_ready", "scores_done", "mask_done",
                     "v_ready", "av_done", "head_sum", "cen_ready", "head_sq", "gvar_ready",
                     "grs_step", "grs_ready", "gn_ready", "gnT_done", "gx_ready", "gh_ready", "wo_done", "x1_ready",
                     "x1_stats", "hx_step", "hx_ready", "rs2_ready",
                     "x2_ready", "x2T_done", "x2T_ready", "u_done", "g_done", "su_ready", "hid_ready", "mlp_done",
                     "h1_ready", "h1_stats", "rs3_ready",
                     "xf_ready", "xfT_done", "xfT_ready", "xf_kept", "logits_done", "sig_ready",
                     "r1", "r2", "r3", "r4", "r5", "r6", "r7", "r8", "r9", "r10", "r11", "r12", "r13",
                     "sel_ready", "pos_done", "slots_ready", "wk_ready", "tid_copied", "r14", "r15", "r16",
                     "count_done", "tb", "vb_ready", "rows_done", "rows_ready", "choose_ready", "choose_used",
                     "idx_done", "idx_ready", "tab_loaded",
                     "icol_first", "icol_ready", "xgT_done", "xgT_ready", "gu_done", "sg_ready", "hb_ready", "y_done", "ys_ready", "sh_done", "sh_silu", "sh_ready", "sd_done", "acc_ready",
                     "ci_ready", "yrow_step", "yrow_ready", "combined", "acc_step"):
            S[name] = sem(name)
        pat_loaded = [sem(f"pat_loaded{u}") for u in range(2)]
        xf_stored = [sem(f"xf_stored{u}") for u in range(2)]
        scattered = [sem(f"scattered{u}") for u in range(2)]
        w_loaded = [sem(f"w_loaded{q}") for q in range(UNROLL)]
        gathered = [sem(f"gathered{q}") for q in range(UNROLL)]
        y_stored = [sem(f"y_stored{q}") for q in range(2)]
        cg_loaded = [sem(f"cg_loaded{u}") for u in range(2)]
        out_stored = [sem(f"out_stored{u}") for u in range(2)]

        def col(name, j=0, n=128):
            return vec[0:n, VEC[name] + j:VEC[name] + j + 1]

        def row(name):
            return rows[:, ROWS.index(name), :]

        def bc(ap, axis, n):
            return ap.unsqueeze(axis).to_broadcast([*ap.shape[:axis], n, *ap.shape[axis:]])

        NCONST, NWEIGHT = 16, 0
        consts = [(ident[:, :], a["c_ident"]), (vec[:, :], a["c_vec"]), (hmask[:, :], a["c_hmask"]),
                  (tri[:, :], a["c_tri"]), (decay[:, :, :].rearrange("p a b -> p (a b)"), a["c_decay"]),
                  (io64[:, :], a["c_io64"].partition_broadcast(TP)), (ebase[:, :], a["c_ebase"].partition_broadcast(TP)),
                  (bcol[:, :], a["c_bcol"]), (jcol[:, :], a["c_jcol"]), (tid[:, :], a["c_tid"]),
                  (gbias[:, :], a["gate_bias"].partition_broadcast(TP)),
                  (row("bv"), a["bv"].partition_broadcast(TP)), (row("bo"), a["bo"].partition_broadcast(TP)),
                  (row("b_out"), a["b_out"].partition_broadcast(TP))]
        kpn = "(k p) n -> p k n"
        weights = [(wqk[:, :, j, :], a[n].rearrange(kpn, p=128)) for j, n in enumerate(("wq", "wk", "wg", "wv"))]
        weights += [(wo[:, :, :], a["wo"].rearrange(kpn, p=128)), (w_in[:, :, :], a["w_in"].rearrange(kpn, p=128)),
                    (w_out[:, 0:NM - 1, :], a["w_out"][0:HM * (NM - 1), :].rearrange(kpn, p=HM)),
                    (w_out[0:MS[-1], NM - 1, :], a["w_out"][HM * (NM - 1):HID, :]),
                    (sgu[:, :, 0, :], a["sgT"].rearrange(kpn, p=128)), (sgu[:, :, 1, :], a["suT"].rearrange(kpn, p=128)),
                    (sdw[:, :, :], a["sdT"].rearrange(kpn, p=128)), (gw[:, :, :], a["gateT"].rearrange(kpn, p=128))]

        def settle(eng):
            eng.wait_ge(S["setup"], 4)

        def pairs(eng, lo, hi, step):
            with eng.Fori(lo, hi) as i:
                for u in range(2):
                    step(2 * i + u, u, i)

        def all_tiles(eng, step):
            step(0, 0, 0)
            step(1, 1, 0)
            pairs(eng, 1, NPAIR, step)

        def skewed(eng, step):
            for s in range(-2, 2):
                step(s, s % 2)
            pairs(eng, 1, NPAIR - 1, lambda t, u, n: step(t, u))
            for s in range(NT - 2, NT + 1):
                step(s, s % 2)

        block = ctx.enter_context(nc.Block())

        @block.sync
        def _(sp):
            sp.dma_start(w_tok[:, :, :], a["w_tok"].rearrange(kpn, p=128)).then_inc(S["posrow"], 16)
            sp.dma_start(pos[:, :], a["b_tok"].partition_broadcast(TP)).then_inc(S["posrow"], 16)

            def load_patches(t, u, n):
                if later(t, 2):
                    sp.wait_ge(S["embedded"], t - 1)
                sp.dma_start(pat[u][:, :, :].rearrange("p k t -> p (k t)"),
                             a["patches"][bass.ds(t, 1), :, :].rearrange("a p n -> p (a n)")).then_inc(pat_loaded[u], 16)

            for u in range(2):
                load_patches(u, u, 0)
            sp.wait_ge(S["posrow"], 32)
            for s in range(PER):
                sp.dma_start(pos[s * SEQ:s * SEQ + 1, :], a["cls"]).then_inc(S["posrow"], 16)
            with sp.Fori(1, NPAIR) as i:
                for u in range(2):
                    load_patches(2 * i + u, u, i)
            sp.wait_ge(S["table_zero"], 1)
            sp.dma_start(slot_token.rearrange("(p n) a -> p (n a)", p=128), tab_zero).then_inc(S["table_cleared"], 16)

            def store_xf(t, u, n=0):
                sp.wait_ge(S["xf_ready"], t + 1)
                sp.dma_start(x_rows[bass.ds(t * TP, TP), :], xn[u][:, :]).then_inc(xf_stored[u], 16)
            pairs(sp, 0, NPAIR, store_xf)
            for u in range(2):
                sp.wait_ge(scattered[u], 16 * TOPK * NPAIR)
            sp.wait_ge(S["mlp_done"], NT)
            sp.dma_start(tab, slot_token.rearrange("(k p c) a -> p k (c a)", p=128, c=128)).then_inc(S["tab_loaded"], 16)

            sp.wait_ge(S["rows_ready"], 1)

            def load_w(b, q):
                if later(b, UNROLL):
                    sp.wait_ge(S["y_done"], b - UNROLL + 1)
                e = sp.value_load(rowi[0:1, 0, bass.ds(b, 1)], min_val=0, max_val=NE - 1)
                sp.dma_start(moe_w[q][:, :], a["moe"][bass.ds(e, 1), :, :].rearrange("a p n -> p (a n)")).then_inc(w_loaded[q], 16)

            def store_y(b, q):
                sp.wait_ge(S["ys_ready"], b + 1)
                sp.dma_start(y_rows[bass.ds(b * 128, 128), :], ys[q % 2][:, :]).then_inc(y_stored[q % 2], 16)

            for b in range(UNROLL):
                if b == 4:
                    sp.wait_ge(S["idx_ready"], 1)
                load_w(b, b)
            with sp.Fori(0, NBLK // UNROLL - 1) as i:
                for q in range(UNROLL):
                    store_y(UNROLL * i + q, q)
                    load_w(UNROLL * i + q + UNROLL, q)
            for q in range(UNROLL):
                store_y(NBLK - UNROLL + q, q)

            def store_out(t, u, n=TP):
                sp.wait_ge(S["combined"], t + 1)
                sp.dma_start(out[bass.ds(t * TP, n), :], h[0:n, t, :]).then_inc(out_stored[u], 16)
            pairs(sp, 0, NPAIR - 1, lambda t, u, n: store_out(t, u))
            store_out(NT - 2, 0)
            store_out(NT - 1, 1, SEQS * SEQ - (NT - 1) * TP)
            for u in range(2):
                sp.wait_ge(out_stored[u], 16 * NPAIR)

        @block.gpsimd
        def _(pool):
            pool.memset(half[:, :], -0.5).then_inc(S["setup"], 1)
            pool.memset(selsum[:, 0, :], 0.0).then_inc(S["setup"], 1)
            pool.memset(onesb[:, :], 1.0).then_inc(S["setup"], 1)
            pool.memset(ones64[:, :], 1.0).then_inc(S["setup"], 1)
            pool.memset(tab_zero, 0.0).then_inc(S["table_zero"], 1)

            chain = [0]

            def do(ins):
                ins.then_inc(S["pool_step"], 1)
                chain[0] += 1
                pool.wait_ge(S["pool_step"], chain[0])

            def norm_factors(var):
                n, t0, t1 = D // 2, rs[:, 2, :], rs[:, 3, :]
                do(pool.tensor_tensor(t0, st[:, :, 1], st[:, :, 4], ALU.add))
                do(pool.tensor_scalar(rs[:, MEAN, :], t0, 0.5, None, ALU.mult))
                do(pool.tensor_tensor(t0, st[:, :, 1], st[:, :, 4], ALU.subtract))
                do(pool.tensor_tensor(t1, t0, t0, ALU.mult))
                do(pool.tensor_scalar(t0, t1, n / 2.0, None, ALU.mult))
                do(pool.tensor_tensor(t1, st[:, :, 2], st[:, :, 5], ALU.add))
                do(pool.tensor_tensor(t0, t0, t1, ALU.add))
                do(pool.tensor_scalar(var, t0, 1.0 / D, None, ALU.mult))
                do(pool.tensor_scalar(t1, var, EPS, None, ALU.add))
                do(pool.tensor_tensor(rs[:, RSTD, :], t1, half[:, 0:NT], ALU.pow))

            pool.wait_ge(S["h_stats"], NT)
            pool.wait_ge(S["setup"], 4)
            norm_factors(rs[:, 4, :])
            do(pool.tensor_tensor(rs[:, 2, :], rs[:, RSTD, :], rs[:, RSTD, :], ALU.mult))
            do(pool.tensor_tensor(rs[:, 3, :], rs[:, 4, :], rs[:, 2, :], ALU.mult))
            do(pool.tensor_scalar(rs[:, 4, :], rs[:, 3, :], EPS, None, ALU.add))
            do(pool.tensor_tensor(rs[:, 5, :], rs[:, 4, :], half[:, 0:NT], ALU.pow))
            pool.tensor_tensor(rs[:, BOTH, :], rs[:, 5, :], rs[:, RSTD, :], ALU.mult).then_inc(S["norms_ready"], 1)

            pool.wait_ge(S["weights"], 16 * (len(weights) + len(consts)))
            pool.wait_ge(S["table_cleared"], 16)

            def mask_queries(t, u):
                pool.wait_ge(S["qk_read"], t + 1)
                if later(t, 2):
                    pool.wait_ge(S["scores_done"], 4 * (t - 1))
                pool.tensor_tensor(qm[u][:, 8:16, :], bc(qT[u][:, 1, :], 1, 8), bc(hmask[:, :], 2, TP),
                                   ALU.mult).then_inc(S["qm1_ready"], 1)

            def residual_bias(t, u):
                settle(pool)
                pool.wait_ge(S["x0_ready"], t + 1)
                pool.tensor_tensor(x[:, t, :], x[:, t, :], row("bo"), ALU.add).then_inc(S["x0b_ready"], 1)

            def head_factors(t, u):
                settle(pool)
                pool.wait_ge(S["gvar_ready"], t + 1)
                pool.tensor_tensor(gvar[:, t, :], grs[:, t, :], half[:, 0:NH], ALU.pow).then_inc(S["grs_ready"], 1)

            def stage2(s, u):
                loop = not isinstance(s, int)
                if loop or 0 <= s + 1 < NT:
                    mask_queries(s + 1, 1 - u)
                if loop or s + 2 < NT:
                    residual_bias(s + 2, u)
                if loop or 0 <= s - 2 < NT:
                    head_factors(s - 2, u)
            skewed(pool, stage2)
            head_factors(NT - 1, 1)

            pool.wait_ge(S["gate_read"], NT)

            def gate_heads(t, u):
                pool.wait_ge(S["gx_ready"], t + 1)
                settle(pool)
                if later(t, 2):
                    pool.wait_ge(S["wo_done"], t - 1)
                pool.tensor_tensor(gh[u][:, :, :], gx[u][:, :, :], gateT[:, :, bass.ds(t * TP, TP)],
                                   ALU.mult).then_inc(S["gh_ready"], 1)

            def mlp_residual(t, u):
                settle(pool)
                pool.wait_ge(S["x1_ready"], t + 1)
                pool.tensor_tensor(h[:, t, :], h[:, t, :], x[:, t, :], ALU.add).then_inc(S["hx_step"], 1)
                settle(pool)
                pool.wait_ge(S["hx_step"], t + 1)
                pool.tensor_tensor(h[:, t, :], h[:, t, :], row("b_out"), ALU.add).then_inc(S["hx_ready"], 1)

            def stage3(t, u, n=0):
                gate_heads(t, u)
                if later(t, 1):
                    mlp_residual(t - 1, 1 - u)
            all_tiles(pool, stage3)
            mlp_residual(NT - 1, 1)

            pool.wait_ge(S["x1_stats"], NT)
            norm_factors(rs[:, 4, :])
            pool.engine_nop().then_inc(S["rs2_ready"], 1)
            pool.wait_ge(S["h1_stats"], NT)
            pool.wait_ge(S["x2_ready"], NT)
            norm_factors(rs[:, 4, :])
            pool.engine_nop().then_inc(S["rs3_ready"], 1)

            pool.wait_ge(S["table_cleared"], 16)

            def scatter(t, u, n=0):
                pool.wait_ge(S["xfT_ready"], t + 1)
                pool.tensor_copy(gateT[:, :, bass.ds(t * TP, TP)], gx[u][:, :, :]).then_inc(S["xf_kept"], 1)
                if later(t, 2):
                    pool.wait_ge(scattered[u], 16 * TOPK * n)
                pool.wait_ge(S["slots_ready"], t + 1)
                pool.tensor_copy(slc[u][:, :], slot[:, t, :])
                pool.tensor_copy(tic[u][:, :], tid[:, bass.ds(t, 1)]).then_inc(S["tid_copied"], 1)
                settle(pool)
                pool.wait_ge(S["tid_copied"], t + 1)
                for k in range(TOPK):
                    pool.indirect_dma_start(slot_token, bass.IndirectOffsetOnAxis(ap=slc[u][:, k:k + 1], axis=0),
                                            tic[u][:, :], None).then_inc(scattered[u], 16)
            all_tiles(pool, scatter)

            pool.wait_ge(S["idx_ready"], 1)
            for u in range(2):
                pool.wait_ge(xf_stored[u], 16 * NPAIR)

            def gather(b, q, n):
                if later(b, UNROLL):
                    pool.wait_ge(gathered[q], 16 * n)
                    pool.wait_ge(S["xgT_done"], b - UNROLL + 1)
                first = not later(b, UNROLL)
                pool.tensor_copy(icol[q][:, :], blk_idx[:, bass.ds(b, 1)]).then_inc(S["icol_first" if first else "icol_ready"], 1)
                if first:
                    pool.wait_ge(S["icol_first"], b + 1)
                else:
                    settle(pool)
                    pool.wait_ge(S["icol_ready"], b - UNROLL + 1)
                pool.indirect_dma_start(xg[q][:, :], None, x_rows, bass.IndirectOffsetOnAxis(ap=icol[q][:, 0:1], axis=0)
                                        ).then_inc(gathered[q], 16)
            for q in range(UNROLL):
                gather(q, q, 0)
            with pool.Fori(1, NBLK // UNROLL) as i:
                for q in range(UNROLL):
                    gather(UNROLL * i + q, q, i)

            for q in range(2):
                pool.wait_ge(y_stored[q], 16 * NBLK // 2)

            def collect(t, u, n=0):
                if later(t, 2):
                    pool.wait_ge(cg_loaded[u], 16 * TOPK * n)
                    pool.wait_ge(S["combined"], t - 1)
                pool.wait_ge(S["yrow_ready"], t + 1)
                pool.tensor_copy(slc[u][:, :], yrow[:, t, :]).then_inc(S["ci_ready"], 1)
                settle(pool)
                pool.wait_ge(S["ci_ready"], t + 1)
                for k in range(TOPK):
                    pool.indirect_dma_start(cg[u][:, k, :], None, y_rows,
                                            bass.IndirectOffsetOnAxis(ap=slc[u][:, k:k + 1], axis=0)).then_inc(cg_loaded[u], 16)
            all_tiles(pool, collect)

        @block.scalar
        def _(act):
            for dst, src in consts + weights:
                act.dma_start(dst, src).then_inc(S["weights"], 16)
            act.wait_ge(S["weights"], 16 * (len(weights) + len(consts)))

            def turned(t, u):
                act.wait_ge(S["xnT_done"], t + 1)
                if later(t, 1):
                    act.wait_ge(S["v_done"], t)
                for k in range(2):
                    ins = act.activation(xT[:, k, 0:TP], bank[4][:, k * TP:(k + 1) * TP], ACT.Identity,
                                         bias=col("n1b", k), scale=col("n1w", k))
                ins.then_inc(S["xT_ready"], 1)

            def projected(t, u):
                act.wait_ge(S["qk_done"], t + 1)
                if later(t, 2):
                    act.wait_ge(S["qm0_ready"], t - 1)
                    act.wait_ge(S["qm1_ready"], t - 1)
                    act.wait_ge(S["scores_done"], 4 * (t - 1))
                for k in range(2):
                    act.activation(qT[u][:, k, :], bank[5][:, k * TP:(k + 1) * TP], ACT.Identity, bias=col("bq", k))
                for k in range(2):
                    ins = act.activation(kT[u][:, k, :], bank[5][:, (2 + k) * TP:(3 + k) * TP], ACT.Identity, bias=col("bk", k))
                ins.then_inc(S["qk_read"], 1)
                act.wait_ge(S["gate_done"], t + 1)
                for k in range(2):
                    ins = act.activation(gateT[:, k, bass.ds(t * TP, TP)], bank[4][:, k * TP:(k + 1) * TP], ACT.Silu, bias=col("bg", k))
                ins.then_inc(S["gate_read"], 1)

            def stage2(s, u):
                loop = not isinstance(s, int)
                if loop or 0 <= s + 1 < NT:
                    projected(s + 1, 1 - u)
                if loop or s + 2 < NT:
                    turned(s + 2, u)
            skewed(act, stage2)

            def heads_turned(t, u, n=0):
                act.wait_ge(S["gnT_done"], t + 1)
                if later(t, 2):
                    act.wait_ge(S["gh_ready"], t - 1)
                for k in range(2):
                    ins = act.activation(gx[u][:, k, :], bank[u][:, k * TP:(k + 1) * TP], ACT.Identity,
                                         bias=col("gnb", k), scale=col("gnw", k))
                ins.then_inc(S["gx_ready"], 1)
            all_tiles(act, heads_turned)

            def x2_turned(i):
                act.wait_ge(S["x2T_done"], 2 * i + 2)
                if later(i, 1):
                    act.wait_ge(S["g_done"], NM * i)
                for u in range(2):
                    for k in range(2):
                        ins = act.activation(xT[:, k, u * TP:(u + 1) * TP], bank[4 + u][:, k * TP:(k + 1) * TP],
                                             ACT.Identity, bias=col("n2b", k), scale=col("n2w", k))
                ins.then_inc(S["x2T_ready"], 1)

            def hidden(i):
                for j, m in enumerate(MS):
                    act.wait_ge(S["u_done"], NM * i + j + 1)
                    if later(i, 1) or j >= 2:
                        act.wait_ge(S["hid_ready"], NM * i + j - 1)
                    act.activation(su[j % 2][0:m, :], bank[j % 2][0:m, 0:2 * TP], ACT.Silu,
                                   bias=col("b_u", j, m)).then_inc(S["su_ready"], 1)
            x2_turned(0)
            hidden(0)
            with act.Fori(1, NPAIR) as i:
                x2_turned(i)
                hidden(i)

            def xf_turned(t, u, n=0):
                act.wait_ge(S["xfT_done"], t + 1)
                if later(t, 2):
                    act.wait_ge(S["xf_kept"], t - 1)
                    act.wait_ge(S["logits_done"], t - 1)
                act.activation(gx[u][:, :, :].rearrange("p a b -> p (a b)"), bank[u][:, 0:2 * TP], ACT.Copy).then_inc(S["xfT_ready"], 1)
                act.wait_ge(S["logits_done"], t + 1)
                if later(t, 2):
                    act.wait_ge(S["r1"], t - 1)
                act.activation(sc[u][:, :], bank[2 + u][0:TP, 0:NE], ACT.Sigmoid).then_inc(S["sig_ready"], 1)
            all_tiles(act, xf_turned)

            def rows_turned(b, p):
                act.wait_ge(S["xgT_done"], b + 1)
                if later(b, 2):
                    act.wait_ge(S["gu_done"], b - 1)
                act.activation(xgT[p][:, :, :].rearrange("p a b -> p (a b)"), bank[p][:, 0:256], ACT.Copy).then_inc(S["xgT_ready"], 1)

            def gate_silu(b, p):
                act.wait_ge(S["gu_done"], b + 1)
                if later(b, 2):
                    act.wait_ge(S["hb_ready"], b - 1)
                act.activation(sg[p][:, :], bank[2 + p][:, 0:128], ACT.Silu).then_inc(S["sg_ready"], 1)

            rows_turned(0, 0)
            rows_turned(1, 1)
            for b in range(2):
                gate_silu(b, b)
                rows_turned(b + 2, b)
            with act.Fori(1, NBLK // 2 - 1) as i:
                for u in range(2):
                    gate_silu(2 * i + u, u)
                    rows_turned(2 * i + u + 2, u)
            gate_silu(NBLK - 2, 0)
            gate_silu(NBLK - 1, 1)

            def shared_silu(i):
                act.wait_ge(S["sh_done"], i + 1)
                if later(i, 1):
                    act.wait_ge(S["sh_ready"], i)
                act.activation(sh_s[0][:, :, :].rearrange("p a b -> p (a b)"), bank[0][:, 0:4 * TP], ACT.Silu).then_inc(S["sh_silu"], 1)
            shared_silu(0)
            with act.Fori(1, NPAIR) as i:
                shared_silu(i)

        @block.tensor
        def _(pe):
            def mm(out_, lhsT, rhs, start, stop):
                return pe.matmul(out_, lhsT, rhs, start=start, stop=stop)

            pe.wait_ge(S["posrow"], 32)

            def embed(t, u, n):
                pe.wait_ge(pat_loaded[u], 16 * (n + 1))
                if later(t, 2):
                    pe.wait_ge(S["h_ready"], t - 1)
                for k in range(KP):
                    ins = mm(bank[u][0:TP, 0:D], pat[u][:, k, :], w_tok[:, k, :], k == 0, k == KP - 1)
                ins.then_inc(S["embedded"], 1)
            embed(0, 0, 0)
            embed(1, 1, 0)
            with pe.Fori(1, NPAIR) as i:
                for u in range(2):
                    embed(2 * i + u, u, i)

            pe.wait_ge(S["weights"], 16 * (len(weights) + len(consts)))

            def turn_norm(t, u):
                pe.wait_ge(S["xn_ready"], t + 1)
                if later(t, 1):
                    pe.wait_ge(S["gate_read"], t)
                for k in range(2):
                    ins = pe.transpose(bank[4][:, k * TP:(k + 1) * TP], xn[u][:, k * 128:(k + 1) * 128], ident[0:TP, 0:TP])
                ins.then_inc(S["xnT_done"], 1)

            def project(t, u):
                pe.wait_ge(S["xT_ready"], t + 1)
                if later(t, 1):
                    pe.wait_ge(S["qk_read"], t)
                for j in range(2):
                    for m in range(2):
                        for k in range(2):
                            ins = mm(bank[5][:, (2 * j + m) * TP:(2 * j + m + 1) * TP], wqk[:, k, j, m * 128:(m + 1) * 128],
                                     xT[:, k, 0:TP], k == 0, k == 1)
                ins.then_inc(S["qk_done"], 1)
                for m in range(2):
                    for k in range(2):
                        ins = mm(bank[4][:, m * TP:(m + 1) * TP], wqk[:, k, 2, m * 128:(m + 1) * 128], xT[:, k, 0:TP], k == 0, k == 1)
                ins.then_inc(S["gate_done"], 1)
                if later(t, 1):
                    pe.wait_ge(S["v_ready"], t)
                for k in range(2):
                    ins = mm(bank[6][0:TP, 0:D], xT[:, k, 0:TP], wqk[:, k, 3, :], k == 0, k == 1)
                ins.then_inc(S["v_done"], 1)

            def scores(t, u):
                pe.wait_ge(S["qm0_ready"], t + 1)
                pe.wait_ge(S["qm1_ready"], t + 1)
                for j in range(4):
                    if later(t, 1):
                        pe.wait_ge(S["mask_done"], 4 * t - 3 + j)
                    mm(bank[j][0:TP, 0:4 * TP], kT[u][:, j // 2, :], qm[u][:, 4 * j:4 * j + 4, :].rearrange("p a b -> p (a b)"),
                       True, True).then_inc(S["scores_done"], 1)

            def retain(t, u):
                pe.wait_ge(S["mask_done"], 4 * t + 4)
                pe.wait_ge(S["v_ready"], t + 1)
                if later(t, 1):
                    pe.wait_ge(S["cen_ready"], t)
                for n in range(NH):
                    ins = mm(bank[7][0:TP, n * HD:(n + 1) * HD], ss[u][:, n, :], vv[u][:, n * HD:(n + 1) * HD], True, True)
                ins.then_inc(S["av_done"], 1)

            def stage2(s, u):
                loop = not isinstance(s, int)
                if loop or 0 <= s + 1 < NT:
                    project(s + 1, 1 - u)
                if loop or 0 <= s < NT:
                    scores(s, u)
                if loop or 0 <= s - 1 < NT:
                    retain(s - 1, 1 - u)
                if loop or s + 2 < NT:
                    turn_norm(s + 2, u)
            skewed(pe, stage2)

            pe.wait_ge(S["gate_read"], NT)
            pe.wait_ge(S["qk_read"], NT)

            def turn_heads(t, u):
                pe.wait_ge(S["gn_ready"], t + 1)
                if later(t, 2):
                    pe.wait_ge(S["gx_ready"], t - 1)
                for k in range(2):
                    ins = pe.transpose(bank[u][:, k * TP:(k + 1) * TP], xn[u][:, k * 128:(k + 1) * 128], ident[0:TP, 0:TP])
                ins.then_inc(S["gnT_done"], 1)

            def attn_out(t, u):
                pe.wait_ge(S["gh_ready"], t + 1)
                if later(t, 2):
                    pe.wait_ge(S["x1_ready"], t - 1)
                for k in range(2):
                    ins = mm(bank[2 + u][0:TP, 0:D], gh[u][:, k, :], wo[:, k, :], k == 0, k == 1)
                ins.then_inc(S["wo_done"], 1)

            turn_heads(0, 0)
            turn_heads(1, 1)
            attn_out(0, 0)
            turn_heads(2, 0)
            attn_out(1, 1)
            with pe.Fori(1, NPAIR - 1) as i:
                for u in range(2):
                    turn_heads(2 * i + u + 1, 1 - u)
                    attn_out(2 * i + u, u)
            turn_heads(NT - 1, 1)
            attn_out(NT - 2, 0)
            attn_out(NT - 1, 1)

            def turn_x2(i):
                for u in range(2):
                    pe.wait_ge(S["x2_ready"], 2 * i + u + 1)
                    if u == 0 and later(i, 1):
                        pe.wait_ge(S["x2T_ready"], i)
                    for k in range(2):
                        ins = pe.transpose(bank[4 + u][:, k * TP:(k + 1) * TP], xn[u][:, k * 128:(k + 1) * 128], ident[0:TP, 0:TP])
                    ins.then_inc(S["x2T_done"], 1)

            def mlp_in(i):
                pe.wait_ge(S["x2T_ready"], i + 1)
                for j, m in enumerate(MS):
                    for s, (done, free) in enumerate((("u_done", "su_ready"), ("g_done", "hid_ready"))):
                        if later(i, 1) or j >= 2:
                            pe.wait_ge(S[free], NM * i + j - 1)
                        for k in range(2):
                            at = s * HID + j * HM
                            ins = mm(bank[2 * s + j % 2][0:m, 0:2 * TP], w_in[:, k, at:at + m], xT[:, k, :], k == 0, k == 1)
                        ins.then_inc(S[done], 1)

            def mlp_out(i):
                pe.wait_ge(S["hid_ready"], NM * (i + 1))
                for u in range(2):
                    if later(i, 1):
                        pe.wait_ge(S["h1_ready"], 2 * i + u - 1)
                    for j, m in enumerate(MS):
                        ins = mm(bank[6 + u][0:TP, 0:D], hT[0:m, j, u * TP:(u + 1) * TP], w_out[0:m, j, :], j == 0, j == NM - 1)
                    ins.then_inc(S["mlp_done"], 1)

            pe.wait_ge(S["x1_ready"], NT)
            turn_x2(0)
            mlp_in(0)
            turn_x2(1)
            mlp_out(0)
            with pe.Fori(1, NPAIR - 1) as i:
                mlp_in(i)
                turn_x2(i + 1)
                mlp_out(i)
            mlp_in(NPAIR - 1)
            mlp_out(NPAIR - 1)

            def turn_xf(t, u):
                pe.wait_ge(S["xf_ready"], t + 1)
                if later(t, 2):
                    pe.wait_ge(S["xfT_ready"], t - 1)
                for k in range(2):
                    ins = pe.transpose(bank[u][:, k * TP:(k + 1) * TP], xn[u][:, k * 128:(k + 1) * 128], ident[0:TP, 0:TP])
                ins.then_inc(S["xfT_done"], 1)

            def route(t, u):
                pe.wait_ge(S["xfT_ready"], t + 1)
                if later(t, 2):
                    pe.wait_ge(S["sig_ready"], t - 1)
                for k in range(2):
                    ins = mm(bank[2 + u][0:TP, 0:NE], gx[u][:, k, :], gw[:, k, :], k == 0, k == 1)
                ins.then_inc(S["logits_done"], 1)

            def place(t, u):
                pe.wait_ge(S["sel_ready"], t + 1)
                if later(t, 2):
                    pe.wait_ge(S["slots_ready"], t - 1)
                mm(bank[4 + u][0:TP, 0:NE], trib[:, :], sel[u][:, :], True, False)
                mm(bank[4 + u][0:TP, 0:NE], onesb[:, 0:TP], selsum[:, t, :], False, True).then_inc(S["pos_done"], 1)

            pe.wait_ge(S["xf_ready"], 1)
            turn_xf(0, 0)
            route(0, 0)
            turn_xf(1, 1)
            place(0, 0)
            route(1, 1)
            turn_xf(2, 0)
            place(1, 1)
            with pe.Fori(1, NPAIR - 1) as i:
                for u in range(2):
                    route(2 * i + u, u)
                    turn_xf(2 * i + u + 1, 1 - u)
                    place(2 * i + u, u)
            route(NT - 2, 0)
            turn_xf(NT - 1, 1)
            place(NT - 2, 0)
            route(NT - 1, 1)
            place(NT - 1, 1)

            pe.wait_ge(S["r16"], NT)
            mm(bank[6][:, 0:NE], onesb[:, :], selsum[:, NT, :], True, True).then_inc(S["count_done"], 1)
            pe.wait_ge(S["vb_ready"], 1)
            for q in range(4):
                ins = mm(bank[7][:, q * 128:(q + 1) * 128], vb[:, q, :], ident[:, :], True, True)
            ins.then_inc(S["rows_done"], 1)
            pe.wait_ge(S["tab_loaded"], 16)
            for k in range(TKT):
                pe.wait_ge(S["choose_ready"], k + 1)
                mm(bank[6][:, 0:NBLK], tab[:, k, :], choose[k % 2], k == 0, k == TKT - 1).then_inc(S["choose_used"], 1)

            def turn_rows(b, q, p, n):
                pe.wait_ge(gathered[q], 16 * (n + 1))
                if later(b, 2):
                    pe.wait_ge(S["xgT_ready"], b - 1)
                for k in range(2):
                    ins = pe.transpose(bank[p][:, k * 128:(k + 1) * 128], xg[q][:, k * 128:(k + 1) * 128], ident[:, :])
                ins.then_inc(S["xgT_done"], 1)

            def gate_up(b, q, p, n):
                pe.wait_ge(w_loaded[q], 16 * (n + 1))
                pe.wait_ge(S["xgT_ready"], b + 1)
                if later(b, 2):
                    pe.wait_ge(S["hb_ready"], b - 1)
                for s in range(2):
                    for k in range(2):
                        at = k * 256 + s * 128
                        ins = mm(bank[2 + p][:, s * 128:(s + 1) * 128], moe_w[q][:, at:at + 128], xgT[p][:, k, :], k == 0, k == 1)
                ins.then_inc(S["gu_done"], 1)

            def down(b, q, p):
                pe.wait_ge(S["hb_ready"], b + 1)
                if later(b, 2):
                    pe.wait_ge(S["ys_ready"], b - 1)
                mm(bank[6 + p][:, 0:256], hb[p][:, :], moe_w[q][:, 512:768], True, True).then_inc(S["y_done"], 1)

            def stage6(i, q, first=False, ahead=True):
                b, p, m = UNROLL * i + q, q % 2, (q - 1) % UNROLL
                gate_up(b, q, p, i)
                if ahead:
                    turn_rows(b + 2, (q + 2) % UNROLL, p, i + (q + 2) // UNROLL)
                if not first:
                    down(b - 1, m, 1 - p)

            pe.wait_ge(S["idx_ready"], 1)
            turn_rows(0, 0, 0, 0)
            turn_rows(1, 1, 1, 0)
            for q in range(UNROLL):
                stage6(0, q, first=q == 0)
            with pe.Fori(1, NBLK // UNROLL - 1) as i:
                for q in range(UNROLL):
                    stage6(i, q)
            for q in range(UNROLL):
                stage6(NBLK // UNROLL - 1, q, ahead=q < UNROLL - 2)
            down(NBLK - 1, UNROLL - 1, 1)

            pe.wait_ge(S["ys_ready"], NBLK)
            pe.wait_ge(S["xf_kept"], NT)

            def shared_in(i):
                for s in range(2):
                    if later(i, 1):
                        pe.wait_ge(S["sh_silu" if s == 0 else "sh_ready"], i)
                    for m in range(2):
                        for k in range(2):
                            ins = mm(bank[s][:, m * 2 * TP:(m + 1) * 2 * TP], sgu[:, k, s, m * 128:(m + 1) * 128],
                                     gateT[:, k, bass.ds(i * 2 * TP, 2 * TP)], k == 0, k == 1)
                ins.then_inc(S["sh_done"], 1)

            def shared_out(i):
                pe.wait_ge(S["sh_ready"], i + 1)
                for u in range(2):
                    if later(i, 1):
                        pe.wait_ge(S["acc_ready"], 2 * i + u - 1)
                    for k in range(2):
                        ins = mm(bank[2 + u][0:TP, 0:D], sh_s[1][:, k, u * TP:(u + 1) * TP], sdw[:, k, :], k == 0, k == 1)
                    ins.then_inc(S["sd_done"], 1)
            shared_in(0)
            shared_out(0)
            with pe.Fori(1, NPAIR) as i:
                shared_in(i)
                shared_out(i)

        @block.vector
        def _(dve):
            dve.wait_ge(S["posrow"], 16 * (2 + PER))

            def embedded(t, u, n=0):
                dve.wait_ge(S["embedded"], t + 1)
                dve.tensor_tensor(h[:, t, :], bank[u][0:TP, 0:D], pos[:, :], ALU.add).then_inc(S["h_ready"], 1)
                dve.wait_ge(S["h_ready"], t + 1)
                dve.bn_stats(st[:, t, :], h[:, t, :]).then_inc(S["h_stats"], 1)
            pairs(dve, 0, NPAIR, embedded)

            dve.wait_ge(S["table_cleared"], 16)
            dve.wait_ge(S["norms_ready"], 1)
            dve.wait_ge(S["weights"], 16 * (len(weights) + len(consts)))
            dve.tensor_copy(trib[:, :], tri[:, :]).then_inc(S["setup"], 1)

            def normed(t, u):
                dve.tensor_scalar(x[:, t, :], h[:, t, :], rs[:, MEAN, bass.ds(t, 1)], rs[:, RSTD, bass.ds(t, 1)],
                                  ALU.subtract, ALU.mult).then_inc(S["x0_ready"], 1)
                if later(t, 2):
                    dve.wait_ge(S["xnT_done"], t - 1)
                dve.tensor_scalar(xn[u][:, :], h[:, t, :], rs[:, MEAN, bass.ds(t, 1)], rs[:, BOTH, bass.ds(t, 1)],
                                  ALU.subtract, ALU.mult).then_inc(S["xn_ready"], 1)

            def mask_queries(t, u, n=0):
                dve.wait_ge(S["qk_read"], t + 1)
                if later(t, 2):
                    dve.wait_ge(S["scores_done"], 4 * (t - 1))
                dve.tensor_tensor(qm[u][:, 0:8, :], bc(qT[u][:, 0, :], 1, 8), bc(hmask[:, :], 2, TP),
                                  ALU.mult).then_inc(S["qm0_ready"], 1)

            def decay_scores(t, u):
                if later(t, 2):
                    dve.wait_ge(S["av_done"], t - 1)
                for j in range(4):
                    dve.wait_ge(S["scores_done"], 4 * t + j + 1)
                    dve.tensor_tensor(ss[u][:, 4 * j:4 * j + 4, :], bank[j][0:TP, 0:4 * TP].rearrange("p (a b) -> p a b", a=4),
                                      decay[:, 4 * j:4 * j + 4, :], ALU.mult).then_inc(S["mask_done"], 1)

            def values(t, u):
                dve.wait_ge(S["v_done"], t + 1)
                if later(t, 2):
                    dve.wait_ge(S["av_done"], t - 1)
                dve.tensor_tensor(vv[u][:, :], bank[6][0:TP, 0:D], row("bv"), ALU.add).then_inc(S["v_ready"], 1)

            def centre(t, u):
                heads = bank[7][0:TP, 0:D].rearrange("p (n d) -> p n d", n=NH)
                cen_t = cen[:, t, :].rearrange("p (n d) -> p n d", n=NH)
                dve.wait_ge(S["av_done"], t + 1)
                if later(t, 2):
                    dve.wait_ge(S["cen_ready"], t - 1)
                dve.tensor_reduce(gsum[u][:, :], heads, AX.X, ALU.add).then_inc(S["head_sum"], 1)
                dve.wait_ge(S["head_sum"], t + 1)
                dve.scalar_tensor_tensor(cen_t, bc(gsum[u][:, :], 2, HD), -1.0 / HD, heads, ALU.mult, ALU.add).then_inc(S["cen_ready"], 1)
                dve.wait_ge(S["cen_ready"], t + 1)
                if later(t, 1):
                    dve.wait_ge(S["gvar_ready"], t)
                dve.tensor_tensor(gsq[:, :], cen[:, t, :], cen[:, t, :], ALU.mult).then_inc(S["head_sq"], 1)
                dve.wait_ge(S["head_sq"], t + 1)
                if later(t, 2):
                    dve.wait_ge(S["gvar_ready"], t - 1)
                dve.tensor_reduce(gsum[u][:, :], gsq[:, :].rearrange("p (n d) -> p n d", n=NH), AX.X, ALU.add).then_inc(S["grs_step"], 1)
                dve.wait_ge(S["grs_step"], t + 1)
                dve.tensor_scalar(grs[:, t, :], gsum[u][:, :], 1.0 / HD, EPS, ALU.mult, ALU.add).then_inc(S["gvar_ready"], 1)

            def stage2(s, u):
                loop = not isinstance(s, int)
                if loop or 0 <= s + 1 < NT:
                    mask_queries(s + 1, 1 - u)
                if loop or 0 <= s < NT:
                    decay_scores(s, u)
                if loop or s + 2 < NT:
                    normed(s + 2, u)
                if loop or 0 <= s + 1 < NT:
                    values(s + 1, 1 - u)
                if loop or 0 <= s - 1 < NT:
                    centre(s - 1, 1 - u)
            skewed(dve, stage2)

            dve.wait_ge(S["grs_ready"], NT)
            dve.wait_ge(S["x0b_ready"], NT)

            def group_normed(t, u):
                dve.wait_ge(S["gnT_done"], t - 1) if later(t, 2) else None
                dve.tensor_tensor(xn[u][:, :].rearrange("p (n d) -> p n d", n=NH), cen[:, t, :].rearrange("p (n d) -> p n d", n=NH),
                                  gvar[:, t, :].unsqueeze(2).to_broadcast([TP, NH, HD]), ALU.mult).then_inc(S["gn_ready"], 1)

            def attended(t, u):
                dve.wait_ge(S["wo_done"], t + 1)
                dve.tensor_tensor(x[:, t, :], bank[2 + u][0:TP, 0:D], x[:, t, :], ALU.add).then_inc(S["x1_ready"], 1)
                dve.wait_ge(S["x1_ready"], t + 1)
                dve.bn_stats(st[:, t, :], x[:, t, :]).then_inc(S["x1_stats"], 1)

            group_normed(0, 0)
            group_normed(1, 1)
            attended(0, 0)
            group_normed(2, 0)
            attended(1, 1)
            with dve.Fori(1, NPAIR - 1) as i:
                for u in range(2):
                    group_normed(2 * i + u + 1, 1 - u)
                    attended(2 * i + u, u)
            group_normed(NT - 1, 1)
            attended(NT - 2, 0)
            attended(NT - 1, 1)

            dve.wait_ge(S["rs2_ready"], 1)
            dve.wait_ge(S["hx_ready"], NT)
            dve.wait_ge(S["gnT_done"], NT)

            def x2_normed(i):
                for u in range(2):
                    t = 2 * i + u
                    if later(i, 1):
                        dve.wait_ge(S["x2T_done"], 2 * i + u - 1)
                    dve.tensor_scalar(xn[u][:, :], x[:, t, :], rs[:, MEAN, bass.ds(t, 1)], rs[:, RSTD, bass.ds(t, 1)],
                                      ALU.subtract, ALU.mult).then_inc(S["x2_ready"], 1)

            def hidden(i):
                if later(i, 1):
                    dve.wait_ge(S["mlp_done"], 2 * i)
                for j, m in enumerate(MS):
                    dve.wait_ge(S["g_done"], NM * i + j + 1)
                    dve.wait_ge(S["su_ready"], NM * i + j + 1)
                    dve.scalar_tensor_tensor(hT[0:m, j, :], bank[2 + j % 2][0:m, 0:2 * TP], col("b_g", j, m),
                                             su[j % 2][0:m, :], ALU.add, ALU.mult
                                             ).then_inc(S["hid_ready"], 1)

            def mlp_added(i):
                for u in range(2):
                    t = 2 * i + u
                    dve.wait_ge(S["mlp_done"], t + 1)
                    dve.tensor_tensor(h[:, t, :], bank[6 + u][0:TP, 0:D], h[:, t, :], ALU.add).then_inc(S["h1_ready"], 1)
                    dve.wait_ge(S["h1_ready"], t + 1)
                    dve.bn_stats(st[:, t, :], h[:, t, :]).then_inc(S["h1_stats"], 1)
            x2_normed(0)
            x2_normed(1)
            hidden(0)
            mlp_added(0)
            with dve.Fori(1, NPAIR - 1) as i:
                x2_normed(i + 1)
                hidden(i)
                mlp_added(i)
            hidden(NPAIR - 1)
            mlp_added(NPAIR - 1)

            dve.wait_ge(S["rs3_ready"], 1)
            dve.wait_ge(S["setup"], 5)
            dve.wait_ge(S["x2T_done"], NT)

            def last_norm(t, u, n=0):
                if later(t, 2):
                    dve.wait_ge(S["xfT_done"], t - 1)
                    dve.wait_ge(xf_stored[u], 16 * n)
                dve.tensor_scalar(xn[u][:, :], h[:, t, :], rs[:, MEAN, bass.ds(t, 1)], rs[:, RSTD, bass.ds(t, 1)],
                                  ALU.subtract, ALU.mult).then_inc(S["xf_ready"], 1)

            def choose_experts(t, u):
                def do(ins, name):
                    ins.then_inc(S[name], 1)
                    if name in ("r2", "r3", "r8", "r9"):
                        settle(dve)
                    dve.wait_ge(S[name], t + 1)
                dve.wait_ge(S["sig_ready"], t + 1)
                do(dve.tensor_tensor(msc[:, :], sc[u][:, :], gbias[:, :], ALU.add), "r1")
                grouped = msc[:, :].rearrange("p (g e) -> p g e", g=NG)
                do(dve.tensor_reduce(gmx[:, :], grouped, AX.X, ALU.max), "r2")
                do(dve.max(top[:, :], gmx[:, :]), "r3")
                do(dve.max_index(idx[:, :], top[:, :], gmx[:, :]), "r4")
                do(dve.tensor_copy(idf[:, :], idx[:, :]), "r5")
                do(dve.tensor_tensor(geq[:, :, :], bc(io64[:, 0:NG], 1, TOPG), bc(idf[:, 0:TOPG], 2, NG), ALU.is_equal), "r6")
                do(dve.tensor_reduce(gsel[:, :], geq[:, :, :].rearrange("p k g -> p g k"), AX.X, ALU.add), "r7")
                if later(t, 2):
                    dve.wait_ge(S["wk_ready"], t - 1)
                do(dve.tensor_tensor(grouped, grouped, bc(gsel[:, :], 2, EG), ALU.mult), "r8")
                do(dve.max(etop[u][:, :], msc[:, :]), "r9")
                do(dve.max_index(idx[:, :], etop[u][:, :], msc[:, :]), "r10")
                do(dve.tensor_copy(idf[:, :], idx[:, :]), "r11")
                dve.tensor_copy(chosen[:, t, :], idf[:, 0:TOPK])
                do(dve.tensor_tensor(oh[:, :, :], bc(io64[:, :], 1, TOPK), bc(idf[:, 0:TOPK], 2, NE), ALU.is_equal), "r12")
                if later(t, 2):
                    dve.wait_ge(S["pos_done"], t - 1)
                dve.tensor_reduce(smap[:, :], oh[:, :, :].rearrange("p k e -> p e k"), AX.X, ALU.add).then_inc(S["r13"], 1)
                dve.wait_ge(S["r13"], t + 1)
                dve.tensor_copy(sel[u][:, :], smap[:, :]).then_inc(S["sel_ready"], 1)
                dve.tensor_tensor(selsum[:, t + 1, :], selsum[:, t, :], smap[:, :], ALU.add).then_inc(S["r16"], 1)
                do(dve.tensor_reduce(wsum[:, 0:1], etop[u][:, 0:TOPK], AX.X, ALU.add), "r14")
                do(dve.tensor_scalar(wsum[:, 1:2], wsum[:, 0:1], 1e-8, None, ALU.add), "tb")
                do(dve.reciprocal(wsum[:, 0:1], wsum[:, 1:2]), "acc_step")
                dve.tensor_scalar(wk[:, t, :], etop[u][:, 0:TOPK], wsum[:, 0:1], None, ALU.mult).then_inc(S["wk_ready"], 1)
                dve.wait_ge(S["pos_done"], t + 1)
                dve.wait_ge(S["r16"], t + 1)
                dve.tensor_tensor(smap[:, :], bank[4 + u][0:TP, 0:NE], ebase[:, :], ALU.add).then_inc(S["r15"], 1)
                dve.wait_ge(S["r15"], 3 * t + 1)
                dve.tensor_tensor(prod[:, :, :], oh[:, :, :], bc(smap[:, :], 1, TOPK), ALU.mult).then_inc(S["r15"], 1)
                dve.wait_ge(S["r15"], 3 * t + 2)
                dve.tensor_reduce(slf[:, :], prod[:, :, :], AX.X, ALU.add).then_inc(S["r15"], 1)
                dve.wait_ge(S["r15"], 3 * t + 3)
                dve.tensor_copy(slot[:, t, :], slf[:, :]).then_inc(S["slots_ready"], 1)
                dve.wait_ge(S["slots_ready"], t + 1)

            last_norm(0, 0)
            last_norm(1, 1)
            choose_experts(0, 0)
            last_norm(2, 0, 1)
            choose_experts(1, 1)
            with dve.Fori(1, NPAIR - 1) as i:
                for u in range(2):
                    last_norm(2 * i + u + 1, 1 - u, i + u)
                    choose_experts(2 * i + u, u)
            last_norm(NT - 1, 1, NPAIR - 1)
            choose_experts(NT - 2, 0)
            choose_experts(NT - 1, 1)

            n_tb = [NT]

            def do(ins):
                ins.then_inc(S["tb"], 1)
                n_tb[0] += 1
                dve.wait_ge(S["tb"], n_tb[0])
            dve.wait_ge(S["count_done"], 1)
            do(dve.tensor_scalar(nbf[:, :], bank[6][:, 0:NE], 127.0, None, ALU.add))
            do(dve.tensor_copy(nbi[:, :], nbf[:, :]))
            do(dve.tensor_scalar(nbi[:, :], nbi[:, :], 7, None, ALU.arith_shift_right))
            do(dve.tensor_copy(nbf[:, :], nbi[:, :]))
            do(dve.tensor_tensor_scan(bend[:, :], ones64[:, :], nbf[:, :], 0.0, ALU.mult, ALU.add))
            do(dve.tensor_tensor(shift[:, :], bend[0:TP, :], nbf[0:TP, :], ALU.subtract))
            do(dve.scalar_tensor_tensor(shift[:, :], shift[:, :], 128.0, ebase[:, :], ALU.mult, ALU.subtract))
            for j in range(2):
                do(dve.tensor_scalar(le[:, j, :], bend[:, :], bcol[:, j:j + 1], None, ALU.is_le))
                do(dve.tensor_tensor(lb[:, j, :], le[:, j, :], bend[:, :], ALU.mult))
            do(dve.tensor_reduce(ecol[:, :], le[:, :, :], AX.X, ALU.add))
            do(dve.tensor_reduce(scol[:, :], lb[:, :, :], AX.X, ALU.max))
            do(dve.tensor_tensor(scol[:, :], bcol[:, :], scol[:, :], ALU.subtract))
            do(dve.scalar_tensor_tensor(scol[:, :], ecol[:, :], float(SLOT_BLOCKS), scol[:, :], ALU.mult, ALU.add))
            do(dve.tensor_scalar(ecol[:, :], ecol[:, :], float(NE - 1), None, ALU.min))
            for j in range(2):
                do(dve.tensor_copy(vb[:, j, :], ecol[:, j:j + 1].to_broadcast([128, 128])))
                do(dve.tensor_copy(vb[:, 2 + j, :], scol[:, j:j + 1].to_broadcast([128, 128])))
            dve.engine_nop().then_inc(S["vb_ready"], 1)
            dve.wait_ge(S["rows_done"], 1)
            do(dve.tensor_copy(rowf[:, :, :].rearrange("p a b -> p (a b)"), bank[7][:, :]))
            dve.tensor_copy(rowi[0:1, :, :], rowf[0:1, :, :]).then_inc(S["rows_ready"], 1)
            dve.wait_ge(S["mlp_done"], NT)
            for k in range(TKT):
                if k >= 2:
                    dve.wait_ge(S["choose_used"], k - 1)
                dve.tensor_scalar(choose[k % 2], rowf[:, 1, 0:NBLK], jcol[:, k:k + 1], None, ALU.is_equal).then_inc(S["choose_ready"], 1)
            dve.wait_ge(S["choose_used"], TKT)
            dve.tensor_copy(blk_idx[:, :], bank[6][:, 0:NBLK]).then_inc(S["idx_ready"], 1)

            def product(b, p):
                dve.wait_ge(S["sg_ready"], b + 1)
                if later(b, 2):
                    dve.wait_ge(S["y_done"], b - 1)
                dve.tensor_tensor(hb[p][:, :], bank[2 + p][:, 128:256], sg[p][:, :], ALU.mult).then_inc(S["hb_ready"], 1)

            def rows_out(b, p, n):
                dve.wait_ge(S["y_done"], b + 1)
                if later(b, 2):
                    dve.wait_ge(y_stored[p], 16 * n)
                dve.tensor_copy(ys[p][:, :], bank[6 + p][:, 0:256]).then_inc(S["ys_ready"], 1)

            product(0, 0)
            for b in range(1, 4):
                product(b, b % 2)
                rows_out(b - 1, (b - 1) % 2, (b - 1) // 2)
            with dve.Fori(2, NBLK // 2) as i:
                for u in range(2):
                    product(2 * i + u, u)
                    rows_out(2 * i + u - 1, 1 - u, i + (u - 1))
            rows_out(NBLK - 1, 1, NBLK // 2 - 1)

            def shared_product(i):
                dve.wait_ge(S["sh_silu"], i + 1)
                if later(i, 1):
                    dve.wait_ge(S["sd_done"], 2 * i)
                dve.tensor_tensor(sh_s[1][:, :, :].rearrange("p a b -> p (a b)"), bank[1][:, 0:4 * TP],
                                  sh_s[0][:, :, :].rearrange("p a b -> p (a b)"), ALU.mult).then_inc(S["sh_ready"], 1)

            def result_rows(t, u, n=0):
                dve.tensor_tensor(oh[:, :, :], bc(io64[:, :], 1, TOPK), bc(chosen[:, t, :], 2, NE), ALU.is_equal).then_inc(S["yrow_step"], 1)
                dve.wait_ge(S["yrow_step"], 3 * t + 1)
                dve.tensor_tensor(prod[:, :, :], oh[:, :, :], bc(shift[:, :], 1, TOPK), ALU.mult).then_inc(S["yrow_step"], 1)
                dve.wait_ge(S["yrow_step"], 3 * t + 2)
                dve.tensor_reduce(slf[:, :], prod[:, :, :], AX.X, ALU.add).then_inc(S["yrow_step"], 1)
                dve.wait_ge(S["yrow_step"], 3 * t + 3)
                dve.tensor_tensor(yrow[:, t, :], slf[:, :], slot[:, t, :], ALU.add).then_inc(S["yrow_ready"], 1)

            def combine(t, u, n):
                dve.wait_ge(S["sd_done"], t + 1)
                dve.tensor_tensor(h[:, t, :], bank[2 + u][0:TP, 0:D], h[:, t, :], ALU.add).then_inc(S["acc_ready"], 1)
                dve.wait_ge(S["acc_ready"], t + 1)
                dve.wait_ge(cg_loaded[u], 16 * TOPK * (n + 1))
                for k in range(TOPK):
                    ins = dve.scalar_tensor_tensor(h[:, t, :], cg[u][:, k, :], wk[:, t, k:k + 1], h[:, t, :], ALU.mult, ALU.add)
                    if k < TOPK - 1:
                        ins.then_inc(S["acc_step"], 1)
                        dve.wait_ge(S["acc_step"], NT + (TOPK - 1) * t + k + 1)
                ins.then_inc(S["combined"], 1)
            result_rows(0, 0)
            result_rows(1, 1)
            shared_product(0)
            for u in range(2):
                result_rows(2 + u, u)
                combine(u, u, 0)
            with dve.Fori(1, NPAIR - 1) as i:
                shared_product(i)
                for u in range(2):
                    result_rows(2 * i + 2 + u, u)
                    combine(2 * i + u, u, i)
            shared_product(NPAIR - 1)
            combine(NT - 2, 0, NPAIR - 1)
            combine(NT - 1, 1, NPAIR - 1)


def kernel(**inputs):
    import numpy as np
    import concourse.bacc as bacc
    from concourse.bass_utils import run_bass_kernel_spmd

    g = {k: np.asarray(v) for k, v in inputs.items()}
    at, ff = "L0_attn_", "L0_ffn_"
    p = g["x"].reshape(SEQS, 3, 6, 16, 6, 16).transpose(0, 2, 4, 1, 3, 5).reshape(SEQS, 36, KP * 128)
    full = np.zeros((NT * PER, SEQ, KP * 128), np.float32)
    full[:SEQS, 1:] = p
    patches = full.reshape(NT, TP, KP, 128).transpose(0, 3, 2, 1).reshape(NT, 128, KP * TP)

    vec = np.zeros((128, NVEC), np.float32)
    for name, key in (("n1w", "norm1_w"), ("n1b", "norm1_b"), ("bq", "bq"), ("bk", "bk"), ("bg", "bg"),
                      ("gnw", "gn_w"), ("gnb", "gn_b"), ("n2w", "norm2_w"), ("n2b", "norm2_b")):
        vec[:, VEC[name]:VEC[name] + 2] = g[at + key].reshape(2, 128).T
    for s, name in enumerate(("b_u", "b_g")):
        for j, m in enumerate(MS):
            vec[:m, VEC[name] + j] = g[at + "b_in"][s * HID + j * HM:s * HID + j * HM + m]
    eg, eu, ed = (g[ff + n] for n in ("eg_w", "eu_w", "ed_w"))
    gu = np.stack([eg.transpose(0, 2, 1), eu.transpose(0, 2, 1)], 2).reshape(NE, 2, 128, 256).transpose(0, 2, 1, 3)
    moe = np.concatenate([gu.reshape(NE, 128, 512), ed.transpose(0, 2, 1)], 2)

    gamma = (1.0 - np.exp2(-5.0 - np.arange(NH, dtype=np.float32))).astype(np.float32)
    key, query = np.arange(TP)[:, None, None], np.arange(TP)[None, None, :]
    diff = (query - key).astype(np.float32)
    same = (key // SEQ == query // SEQ) & (diff >= 0)
    decay = np.where(same, np.exp(np.log(gamma)[None, :, None] * np.maximum(diff, 0)) * np.float32(HD ** -0.5), 0)
    p128 = np.arange(128)
    arrays = {
        "patches": patches, "w_tok": g["L0_tok_W"], "b_tok": g["L0_tok_b"], "cls": g["cls_tok"].reshape(1, D),
        "wq": g[at + "wq"], "wk": g[at + "wk"], "wg": g[at + "wg"], "wv": g[at + "wv"], "wo": g[at + "wo"],
        "bv": g[at + "bv"], "bo": g[at + "bo"], "b_out": g[at + "b_out"],
        "w_in": g[at + "w_in"], "w_out": g[at + "w_out"],
        "sgT": g[ff + "sg_w"].T, "suT": g[ff + "su_w"].T, "sdT": g[ff + "sd_w"].T, "gateT": g[ff + "gate_w"].T,
        "gate_bias": g[ff + "gate_bias"], "moe": moe, "c_vec": vec,
        "c_ident": np.eye(128), "c_hmask": (p128[:, None] // HD == np.arange(8)[None]),
        "c_tri": np.triu(np.ones((TP, TP)), 1), "c_decay": decay.reshape(TP, NH * TP),
        "c_io64": np.arange(NE), "c_ebase": np.arange(NE) * SLOT_BLOCKS * 128,
        "c_bcol": p128[:, None] + np.array([[0, 128]]), "c_jcol": p128[:, None] + 128 * np.arange(TKT)[None],
        "c_tid": np.arange(TP)[:, None] + TP * np.arange(NT)[None],
    }
    arrays = {n: np.ascontiguousarray(v, dtype=np.float32) for n, v in arrays.items()}

    nc = bacc.Bacc("TRN2", target_bir_lowering=False, num_devices=1)
    aps = {n: nc.dram_tensor(f"in_{n}", v.shape, mybir.dt.from_np(v.dtype), kind="ExternalInput").ap() for n, v in arrays.items()}
    out = nc.dram_tensor("out_0", (SEQS * SEQ, D), F32, kind="ExternalOutput").ap()
    build(nc, aps, out)
    r = run_bass_kernel_spmd(nc, [{f"in_{n}": v for n, v in arrays.items()}], core_ids=[0])
    return r.results[0]["out_0"].reshape(SEQS, SEQ, D)
```

```python
from contextlib import ExitStack

import concourse.bass as bass
from concourse import mybir

F32 = mybir.dt.float32
BF16 = mybir.dt.bfloat16
I32 = mybir.dt.int32
U32 = mybir.dt.uint32
ALU = mybir.AluOpType
ACT = mybir.ActivationFunctionType
AX = mybir.AxisListType

SEQS, SEQ, D = 64, 37, 256
PER = 3
TP = PER * SEQ
NT = 22
NPAIR = NT // 2
TALL = NT * TP
KP = 6
NH, HD = 16, 16
HID, HM, NM = 682, 114, 6
MS = [HM] * (NM - 1) + [HID - HM * (NM - 1)]
NE, TOPK, NG, TOPG = 64, 6, 8, 4
EG = NE // NG
SLOT_BLOCKS = -(-TALL // 128)
UNROLL = 6
NBLK = (TALL * TOPK + NE * 127) // 128
NBLK = -(-NBLK // UNROLL) * UNROLL
TAB_BLOCKS = NE * SLOT_BLOCKS + 128
EPS = 1e-5
PATS = 4
FIRST = 16
RSTD, MEAN, BOTH = 0, 1, 6
CHOICE_STEPS, SLOT_STEPS = 14, 3

VEC = {}
_at = 0
for _name, _w in (("n1w", 2), ("n1b", 2), ("bq", 2), ("bk", 2), ("bg", 2), ("gnw", 2), ("gnb", 2),
                  ("n2w", 2), ("n2b", 2), ("b_u", NM), ("b_g", NM)):
    VEC[_name] = _at
    _at += _w
NVEC = _at
ROWS = ("bv", "bo", "b_out")


def later(t, k):
    return not isinstance(t, int) or t >= k


def build(nc, a, out):
    with ExitStack() as ctx:
        def sb(name, shape, dt=F32):
            return ctx.enter_context(nc.sbuf_tensor(name, shape, dt))

        def sem(name):
            return ctx.enter_context(nc.semaphore(name))

        x_rows = nc.dram_tensor("x_rows", (TALL, D), F32, kind="Internal").ap()
        slot_token = nc.dram_tensor("slot_token", (TAB_BLOCKS * 128, 1), F32, kind="Internal").ap()
        y_rows = nc.dram_tensor("y_rows", (NBLK * 128, D), F32, kind="Internal").ap()

        h = sb("h", [TP, NT, D])
        x = sb("x", [TP, NT, D])
        cen = sb("cen", [TP, NT, D])
        gateT = sb("gateT", [128, 2, TALL])
        st = sb("st", [TP, NT, 6])
        gvar = sb("gvar", [TP, NT, NH])
        grs = sb("grs", [TP, NT, NH])
        rs = sb("rs", [TP, 7, NT])
        half = sb("half", [TP, NT])

        w_tok = sb("w_tok", [128, KP, D])
        wqk = sb("wqk", [128, 2, 4, D])
        wo = sb("wo", [128, 2, D])
        w_in = sb("w_in", [128, 2, 2 * HID])
        w_out = sb("w_out", [HM, NM, D])
        sgu = sb("sgu", [128, 2, 2, D])
        sdw = sb("sdw", [128, 2, D])
        gw = sb("gw", [128, 2, NE])
        vec = sb("vec", [128, NVEC])
        rows = sb("rows", [TP, len(ROWS), D])
        pos = sb("pos", [TP, D])
        gbias = sb("gbias", [TP, NE])
        decay = sb("decay", [TP, NH, TP])
        hmask = sb("hmask", [128, 8])
        ident = sb("ident", [128, 128])
        tri = sb("tri", [TP, TP])
        trib = sb("trib", [TP, TP], BF16)
        onesb = sb("onesb", [TP, 128], BF16)
        io64 = sb("io64", [TP, NE])
        ebase = sb("ebase", [TP, NE])
        tid = sb("tid", [TP, NT])

        xn = [sb(f"xn{u}", [TP, D]) for u in range(2)]
        xT = sb("xT", [128, 2, 2 * TP])
        qT = [sb(f"qT{u}", [128, 2, TP]) for u in range(2)]
        kT = [sb(f"kT{u}", [128, 2, TP]) for u in range(2)]
        qm = [sb(f"qm{u}", [128, NH, TP]) for u in range(2)]
        vv = [sb(f"vv{u}", [TP, D]) for u in range(2)]
        ss = [sb(f"ss{u}", [TP, NH, TP]) for u in range(2)]
        gsum = [sb(f"gsum{u}", [TP, NH]) for u in range(2)]
        gsq = sb("gsq", [TP, D])
        q0, q1 = (qm[u][:, :, :].rearrange("p a b -> p (a b)") for u in range(2))
        pat = [gateT[:, :, :].rearrange("p a b -> p (a b)")[:, u * KP * TP:(u + 1) * KP * TP].rearrange("p (k t) -> p k t", k=KP)
               for u in range(PATS)]
        tab_zero = q1[:, 0:TAB_BLOCKS]
        su = [q1[:, u * 2 * TP:(u + 1) * 2 * TP] for u in range(2)]
        hT = q0[:, 0:NM * 2 * TP].rearrange("p (j t) -> p j t", j=NM)
        st_x, st_h = (sb(f"st_{n}", [TP, 2, 6]) for n in "xh")
        mv_x, mv_h = (sb(f"mv_{n}", [TP, 2, 2]) for n in "xh")
        rstd_x, rstd_h = (sb(f"rstd_{n}", [TP, 2, 2]) for n in "xh")
        ss0, ss1 = (ss[u][:, :, :].rearrange("p a b -> p (a b)") for u in range(2))
        x2, xf, gn = (ss1[:, j * 2 * D:(j + 1) * 2 * D].rearrange("p (a n) -> p a n", a=2) for j in range(3))
        xfT, gx, gh = (q1[:, j * 4 * TP:(j + 1) * 4 * TP].rearrange("p (k t) -> p k t", k=2) for j in (1, 2, 3))
        eps = sb("eps", [TP, 2])
        sig = sb("sig", [TP, 2, NE])
        sc = sb("sc", [TP, 2, NE])
        gmax = sb("gmax", [TP, 2, NG])
        top = sb("top", [TP, 2, 8])
        idx = sb("idx", [TP, 2, 8], U32)
        idf = sb("idf", [TP, 2, 8])
        geq = sb("geq", [TP, 2, TOPG, NG])
        gsel = sb("gsel", [TP, 2, NG])
        etop = sb("etop", [TP, 2, 8])
        oh, prod = (ss0[:, u * 2 * TOPK * NE:(u + 1) * 2 * TOPK * NE].rearrange("p (a k e) -> p a k e", a=2, k=TOPK) for u in range(2))
        sel = sb("sel", [TP, 2, NE], BF16)
        selsum = sb("selsum", [TP, NT + 1, NE], BF16)
        smap = sb("smap", [TP, 2, NE])
        slf = sb("slf", [TP, 2, TOPK])
        slot = sb("slot", [TP, NT, TOPK])
        chosen = sb("chosen", [TP, NT, TOPK])
        yrow = sb("yrow", [TP, NT, TOPK], I32)
        shift = sb("shift", [TP, NE])
        slc = [sb(f"slc{u}", [TP, TOPK], I32) for u in range(2)]
        tic = [sb(f"tic{u}", [TP, 1]) for u in range(2)]
        wk = sb("wk", [TP, NT, TOPK])
        wsum = sb("wsum", [TP, 3, 2])
        nbf = sb("nbf", [128, NE])
        nbi = sb("nbi", [128, NE], I32)
        bend = sb("bend", [128, NE])
        ones64 = sb("ones64", [128, NE])
        le = sb("le", [128, 2, NE])
        lb = sb("lb", [128, 2, NE])
        bcol = sb("bcol", [128, 2])
        ecol = sb("ecol", [128, 2])
        scol = sb("scol", [128, 2])
        scol_i = sb("scol_i", [128, 2], I32)
        vb, blk_rows = (q0[:, j * 256:(j + 1) * 256].rearrange("p (a b) -> p a b", a=2) for j in range(2))
        rowi = sb("rowi", [1, 256], I32)
        blk_idx = sb("blk_idx", [128, NBLK], I32)

        w_in_f = w_in[:, :, :].rearrange("p a b -> p (a b)")
        wqk_f = wqk[:, :, :, :].rearrange("p a b c -> p (a b c)")
        w_tok_f = w_tok[:, :, :].rearrange("p a b -> p (a b)")
        moe_w = [w_in_f[:, q * 768:(q + 1) * 768] for q in range(3)] + [w_tok_f[:, 0:768]]
        moe_w += [q1[:, q * 768:(q + 1) * 768] for q in range(2)]
        xg = [wqk_f[:, q * D:(q + 1) * D] for q in range(UNROLL)]
        xgT = [wqk_f[:, (6 + q) * D:(7 + q) * D].rearrange("p (a b) -> p a b", a=2) for q in range(2)]
        ys = [q0[:, 888 + q * D:888 + (q + 1) * D] for q in range(2)]
        sg, hb = ([w_tok_f[:, 768 + (2 * j + q) * 128:896 + (2 * j + q) * 128] for q in range(2)] for j in range(2))
        icol = [sb(f"icol{q}", [128, 1], I32) for q in range(UNROLL)]
        arena = cen[:, :, :].rearrange("p a b -> p (a b)")
        cg = [arena[:, u * TOPK * D:(u + 1) * TOPK * D].rearrange("p (k n) -> p k n", k=TOPK) for u in range(2)]
        sh_s = [q0[:, u * 4 * TP:(u + 1) * 4 * TP].rearrange("p (a b) -> p a b", a=2) for u in range(2)]

        bank = [ctx.enter_context(nc.psum_tensor(f"bank{i}", [128, 512], F32)) for i in range(8)]

        S = {}
        for name in ("consts", "weights", "posrow", "table_zero", "table_cleared", "setup",
                     "embedded", "h_ready", "h_stats", "pool_step", "norms_ready",
                     "xn_ready", "x0_ready", "x0b_ready", "hb_out", "xnT_done", "xT_ready", "qk_done", "gate_done",
                     "v_done", "qk_read", "gate_read", "qm0_ready", "qm1_ready", "scores_done", "mask_done",
                     "v_ready", "av_done", "head_sum", "cen_ready", "head_sq", "gvar_ready",
                     "grs_step", "grs_ready", "gn_ready", "gnT_done", "gx_ready", "gh_ready", "wo_done", "x1_ready",
                     "x1_stats", "x1_moments", "hx_ready", "rs2_step", "rs2_ready",
                     "x2_ready", "x2T_done", "x2T_ready", "in_done", "su_ready", "hid_ready", "mlp_done",
                     "h1_ready", "h1_stats", "h1_moments", "rs3_step", "rs3_ready",
                     "xf_ready", "xfT_done", "xfT_ready", "xf_kept", "logits_done", "sig_ready",
                     "choice_step", "gmax_ready", "top_ready", "masked_ready", "etop_ready", "sel_ready", "pos_done", "slot_step", "slots_ready",
                     "count_done", "tb", "blocks_ready", "vb_ready", "row_done", "rows_ready",
                     "block_rows", "block_rows_turned", "idx_ready",
                     "icol_first", "icol_ready", "xgT_done", "xgT_ready", "gu_done", "sg_ready", "hb_ready", "y_done", "ys_ready", "sh_done", "sh_silu", "sh_ready", "sd_done", "acc_ready",
                     "ci_ready", "yrow_step", "yrow_ready", "combined", "acc_step"):
            S[name] = sem(name)
        pat_loaded = [sem(f"pat_loaded{u}") for u in range(PATS)]
        xf_stored = sem("xf_stored")
        indices_ready = [sem(f"indices_ready{u}") for u in range(2)]
        scattered = [sem(f"scattered{u}") for u in range(2)]
        w_loaded = [sem(f"w_loaded{q}") for q in range(UNROLL)]
        gathered = [sem(f"gathered{q}") for q in range(UNROLL)]
        y_stored = [sem(f"y_stored{q}") for q in range(2)]
        cg_loaded = [sem(f"cg_loaded{u}") for u in range(2)]
        out_stored = [sem(f"out_stored{u}") for u in range(2)]

        def col(name, j=0, n=128):
            return vec[0:n, VEC[name] + j:VEC[name] + j + 1]

        def row(name):
            return rows[:, ROWS.index(name), :]

        def bc(ap, axis, n):
            return ap.unsqueeze(axis).to_broadcast([*ap.shape[:axis], n, *ap.shape[axis:]])

        NCONST, NWEIGHT = 16, 0
        consts = [(ident[:, :], a["c_ident"]), (vec[:, :], a["c_vec"]), (hmask[:, :], a["c_hmask"]),
                  (tri[:, :], a["c_tri"]), (decay[:, :, :].rearrange("p a b -> p (a b)"), a["c_decay"]),
                  (io64[:, :], a["c_io64"].partition_broadcast(TP)), (ebase[:, :], a["c_ebase"].partition_broadcast(TP)),
                  (bcol[:, :], a["c_bcol"]), (tid[:, :], a["c_tid"]),
                  (gbias[:, :], a["gate_bias"].partition_broadcast(TP)),
                  (row("bv"), a["bv"].partition_broadcast(TP)), (row("bo"), a["bo"].partition_broadcast(TP)),
                  (row("b_out"), a["b_out"].partition_broadcast(TP))]
        kpn = "(k p) n -> p k n"
        weights = [(wqk[:, :, j, :], a[n].rearrange(kpn, p=128)) for j, n in enumerate(("wq", "wk", "wg", "wv"))]
        weights += [(wo[:, :, :], a["wo"].rearrange(kpn, p=128)), (w_in[:, :, :], a["w_in"].rearrange(kpn, p=128)),
                    (w_out[:, 0:NM - 1, :], a["w_out"][0:HM * (NM - 1), :].rearrange(kpn, p=HM)),
                    (w_out[0:MS[-1], NM - 1, :], a["w_out"][HM * (NM - 1):HID, :]),
                    (sgu[:, :, 0, :], a["sgT"].rearrange(kpn, p=128)), (sgu[:, :, 1, :], a["suT"].rearrange(kpn, p=128)),
                    (sdw[:, :, :], a["sdT"].rearrange(kpn, p=128)), (gw[:, :, :], a["gateT"].rearrange(kpn, p=128))]

        def settle(eng):
            eng.wait_ge(S["setup"], 4)

        def pairs(eng, lo, hi, step):
            with eng.Fori(lo, hi) as i:
                for u in range(2):
                    step(2 * i + u, u, i)

        def all_tiles(eng, step):
            step(0, 0, 0)
            step(1, 1, 0)
            pairs(eng, 1, NPAIR, step)

        def has(s, k):
            return not isinstance(s, int) or 0 <= s + k < NPAIR

        def tower(eng, step, lo=2, end=NPAIR - 1, hi=NPAIR + 2):
            for s in range(-1, lo):
                step(s)
            with eng.Fori(lo, end) as s:
                step(s)
            for s in range(end, hi):
                step(s)

        def skewed(eng, step, before_loop=lambda: None):
            for s in range(-2, 4):
                step(s, s % 2)
            before_loop()
            pairs(eng, 2, NPAIR - 1, lambda t, u, n: step(t, u))
            for s in range(NT - 2, NT + 2):
                step(s, s % 2)

        block = ctx.enter_context(nc.Block())

        @block.sync
        def _(sp):
            sp.dma_start(w_tok[:, :, :], a["w_tok"].rearrange(kpn, p=128)).then_inc(S["posrow"], 16)
            sp.dma_start(pos[:, :], a["b_tok"].partition_broadcast(TP)).then_inc(S["posrow"], 16)

            def load_patches(t, u, n):
                if later(t, PATS):
                    sp.wait_ge(S["embedded"], t - PATS + 1)
                sp.dma_start(pat[u].rearrange("p k t -> p (k t)"),
                             a["patches"][bass.ds(t, 1), :, :].rearrange("a p n -> p (a n)")).then_inc(pat_loaded[u], 16)

            for u in range(PATS):
                load_patches(u, u, 0)
            sp.wait_ge(S["posrow"], 32)
            for s in range(PER):
                sp.dma_start(pos[s * SEQ:s * SEQ + 1, :], a["cls"]).then_inc(S["posrow"], 16)
            with sp.Fori(1, NT // PATS) as i:
                for u in range(PATS):
                    load_patches(PATS * i + u, u, i)
            for t in range(NT // PATS * PATS, NT):
                load_patches(t, t % PATS, t // PATS)
            sp.wait_ge(S["table_zero"], 1)
            sp.dma_start(slot_token.rearrange("(p n) a -> p (n a)", p=128), tab_zero).then_inc(S["table_cleared"], 16)

            with sp.Fori(0, NPAIR) as q:
                sp.wait_ge(S["xf_ready"], q + 1)
                sp.dma_start(x_rows[bass.ds(q * 2 * TP, 2 * TP), :].rearrange("(a p) n -> p a n", a=2), xf).then_inc(xf_stored, 16)
            sp.wait_ge(S["rows_ready"], 1)

            def load_w(b, q):
                if later(b, UNROLL):
                    sp.wait_ge(S["y_done"], b - UNROLL + 1)
                e = sp.value_load(rowi[0:1, bass.ds(b, 1)], min_val=0, max_val=NE - 1)
                sp.dma_start(moe_w[q][:, :], a["moe"][bass.ds(e, 1), :, :].rearrange("a p n -> p (a n)")).then_inc(w_loaded[q], 16)

            def store_y(b, q):
                sp.wait_ge(S["ys_ready"], b + 1)
                sp.dma_start(y_rows[bass.ds(b * 128, 128), :], ys[q % 2][:, :]).then_inc(y_stored[q % 2], 16)

            for b in range(UNROLL):
                load_w(b, b)
            with sp.Fori(0, NBLK // UNROLL - 1) as i:
                for q in range(UNROLL):
                    store_y(UNROLL * i + q, q)
                    load_w(UNROLL * i + q + UNROLL, q)
            for q in range(UNROLL):
                store_y(NBLK - UNROLL + q, q)

            def store_out(t, u, n=TP):
                sp.wait_ge(S["combined"], t + 1)
                sp.dma_start(out[bass.ds(t * TP, n), :], h[0:n, t, :]).then_inc(out_stored[u], 16)
            pairs(sp, 0, NPAIR - 1, lambda t, u, n: store_out(t, u))
            store_out(NT - 2, 0)
            store_out(NT - 1, 1, SEQS * SEQ - (NT - 1) * TP)
            for u in range(2):
                sp.wait_ge(out_stored[u], 16 * NPAIR)

        @block.gpsimd
        def _(pool):
            pool.memset(half[:, :], -0.5).then_inc(S["setup"], 1)
            pool.memset(selsum[:, 0, :], 0.0).then_inc(S["setup"], 1)
            pool.memset(eps[:, :], EPS)
            pool.memset(onesb[:, :], 1.0).then_inc(S["setup"], 1)
            pool.memset(ones64[:, :], 1.0).then_inc(S["setup"], 1)
            pool.memset(tab_zero, 0.0).then_inc(S["table_zero"], 1)

            chain = [0]

            def do(ins):
                ins.then_inc(S["pool_step"], 1)
                chain[0] += 1
                pool.wait_ge(S["pool_step"], chain[0])

            def first_norms(lo, hi):
                mean, r, both, t0, t1, var, t2 = (rs[:, j, lo:hi] for j in (MEAN, RSTD, BOTH, 2, 3, 4, 5))
                s6 = st[:, lo:hi, :]
                pool.tensor_tensor(t0, s6[:, :, 1], s6[:, :, 4], ALU.add)
                pool.tensor_tensor(t2, s6[:, :, 2], s6[:, :, 5], ALU.add)
                do(pool.tensor_tensor(t1, s6[:, :, 1], s6[:, :, 4], ALU.subtract))
                pool.tensor_scalar(mean, t0, 0.5, None, ALU.mult)
                do(pool.tensor_tensor(var, t1, t1, ALU.mult))
                do(pool.tensor_scalar(t0, var, D / 4.0, None, ALU.mult))
                do(pool.tensor_tensor(t1, t0, t2, ALU.add))
                do(pool.tensor_scalar(var, t1, 1.0 / D, None, ALU.mult))
                do(pool.tensor_scalar(t1, var, EPS, None, ALU.add))
                do(pool.tensor_tensor(r, t1, half[:, lo:hi], ALU.pow))
                do(pool.tensor_tensor(t0, r, r, ALU.mult))
                do(pool.tensor_tensor(t1, var, t0, ALU.mult))
                do(pool.tensor_scalar(t0, t1, EPS, None, ALU.add))
                do(pool.tensor_tensor(t2, t0, half[:, lo:hi], ALU.pow))
                pool.tensor_tensor(both, t2, r, ALU.mult).then_inc(S["norms_ready"], 1)

            pool.wait_ge(S["setup"], 4)
            pool.wait_ge(S["h_stats"], FIRST)
            first_norms(0, FIRST)
            pool.wait_ge(S["h_stats"], NT)
            first_norms(FIRST, NT)

            pool.wait_ge(S["weights"], 16 * (len(weights) + len(consts)))
            pool.wait_ge(S["table_cleared"], 16)

            def mask_queries(t, u):
                pool.wait_ge(S["qk_read"], t + 1)
                if later(t, 2):
                    pool.wait_ge(S["scores_done"], 4 * (t - 1))
                pool.tensor_tensor(qm[u][:, 8:16, :], bc(qT[u][:, 1, :], 1, 8), bc(hmask[:, :], 2, TP),
                                   ALU.mult).then_inc(S["qm1_ready"], 1)

            def residual_bias(t, u):
                settle(pool)
                pool.wait_ge(S["x0_ready"], t + 1)
                pool.tensor_tensor(x[:, t, :], x[:, t, :], row("bo"), ALU.add).then_inc(S["x0b_ready"], 1)
                settle(pool)
                pool.wait_ge(S["xn_ready"], t + 1)
                pool.tensor_tensor(h[:, t, :], h[:, t, :], row("b_out"), ALU.add).then_inc(S["hb_out"], 1)

            def head_factors(t, u):
                settle(pool)
                pool.wait_ge(S["gvar_ready"], t + 1)
                pool.tensor_tensor(gvar[:, t, :], grs[:, t, :], half[:, 0:NH], ALU.pow).then_inc(S["grs_ready"], 1)

            def stage2(s, u):
                loop = not isinstance(s, int)
                if loop or 0 <= s + 1 < NT:
                    mask_queries(s + 1, 1 - u)
                if loop or s + 2 < NT:
                    residual_bias(s + 2, u)
                if loop or 0 <= s - 2 < NT:
                    head_factors(s - 2, u)
            skewed(pool, stage2)

            def factors(mv, rstd, i, moments, step, ready):
                pool.wait_ge(S[moments], i + 1)
                pool.tensor_tensor(rstd[:, 0, :], mv[:, :, 1], eps[:, :], ALU.add).then_inc(S[step], 1)
                pool.wait_ge(S[step], i + 1)
                pool.tensor_tensor(rstd[:, 1, :], rstd[:, 0, :], half[:, 0:2], ALU.pow).then_inc(S[ready], 1)

            def scatter(n, u):
                if later(n, 1):
                    pool.wait_ge(scattered[u], 16 * TOPK * n)
                pool.wait_ge(S["slots_ready"], n + 1)
                pool.tensor_copy(slc[u][:, :], slot[:, 2 * n + u, :])
                pool.tensor_copy(tic[u][:, :], tid[:, bass.ds(2 * n + u, 1)]).then_inc(indices_ready[u], 1)
                settle(pool)
                pool.wait_ge(indices_ready[u], n + 1)
                for k in range(TOPK):
                    pool.indirect_dma_start(slot_token, bass.IndirectOffsetOnAxis(ap=slc[u][:, k:k + 1], axis=0),
                                            tic[u][:, :], None).then_inc(scattered[u], 16)

            def stages35(s):
                if has(s, -1):
                    factors(mv_h, rstd_h, s - 1, "h1_moments", "rs3_step", "rs3_ready")
                if has(s, -4):
                    scatter(s - 4, 1)
                if has(s, 1):
                    factors(mv_x, rstd_x, s + 1, "x1_moments", "rs2_step", "rs2_ready")
                if has(s, -3):
                    scatter(s - 3, 0)
            pool.wait_ge(S["grs_ready"], NT)
            tower(pool, stages35, lo=4, hi=NPAIR + 4)

            pool.wait_ge(S["blocks_ready"], 1)
            pool.wait_ge(S["mlp_done"], NPAIR)
            for u in range(2):
                pool.wait_ge(scattered[u], 16 * TOPK * NPAIR)
            for j in range(2):
                pool.indirect_dma_start(blk_rows[:, j, :], None, slot_token.rearrange("(b c) a -> b (c a)", c=128),
                                        bass.IndirectOffsetOnAxis(ap=scol_i[:, j:j + 1], axis=0)).then_inc(S["block_rows"], 16)

            pool.wait_ge(S["idx_ready"], 1)
            pool.wait_ge(xf_stored, 16 * NPAIR)

            def gather(b, q, n):
                if later(b, UNROLL):
                    pool.wait_ge(gathered[q], 16 * n)
                    pool.wait_ge(S["xgT_done"], b - UNROLL + 1)
                first = not later(b, UNROLL)
                pool.tensor_copy(icol[q][:, :], blk_idx[:, bass.ds(b, 1)]).then_inc(S["icol_first" if first else "icol_ready"], 1)
                if first:
                    pool.wait_ge(S["icol_first"], b + 1)
                else:
                    settle(pool)
                    pool.wait_ge(S["icol_ready"], b - UNROLL + 1)
                pool.indirect_dma_start(xg[q][:, :], None, x_rows, bass.IndirectOffsetOnAxis(ap=icol[q][:, 0:1], axis=0)
                                        ).then_inc(gathered[q], 16)
            for q in range(UNROLL):
                gather(q, q, 0)
            with pool.Fori(1, NBLK // UNROLL) as i:
                for q in range(UNROLL):
                    gather(UNROLL * i + q, q, i)

            for q in range(2):
                pool.wait_ge(y_stored[q], 16 * NBLK // 2)

            def collect(t, u, n=0):
                if later(t, 2):
                    pool.wait_ge(cg_loaded[u], 16 * TOPK * n)
                    pool.wait_ge(S["combined"], t - 1)
                pool.wait_ge(S["yrow_ready"], t + 1)
                pool.tensor_copy(slc[u][:, :], yrow[:, t, :]).then_inc(S["ci_ready"], 1)
                settle(pool)
                pool.wait_ge(S["ci_ready"], t + 1)
                for k in range(TOPK):
                    pool.indirect_dma_start(cg[u][:, k, :], None, y_rows,
                                            bass.IndirectOffsetOnAxis(ap=slc[u][:, k:k + 1], axis=0)).then_inc(cg_loaded[u], 16)
            all_tiles(pool, collect)

        @block.scalar
        def _(act):
            for dst, src in consts + weights:
                act.dma_start(dst, src).then_inc(S["weights"], 16)
            act.wait_ge(S["weights"], 16 * (len(weights) + len(consts)))

            def turned(t, u):
                act.wait_ge(S["xnT_done"], t + 1)
                if later(t, 1):
                    act.wait_ge(S["v_done"], t)
                for k in range(2):
                    ins = act.activation(xT[:, k, 0:TP], bank[3][:, k * TP:(k + 1) * TP], ACT.Identity,
                                         bias=col("n1b", k), scale=col("n1w", k))
                ins.then_inc(S["xT_ready"], 1)

            def projected(t, u):
                act.wait_ge(S["qk_done"], t + 1)
                if later(t, 2):
                    act.wait_ge(S["qm0_ready"], t - 1)
                    act.wait_ge(S["qm1_ready"], t - 1)
                    act.wait_ge(S["scores_done"], 4 * (t - 1))
                for k in range(2):
                    act.activation(qT[u][:, k, :], bank[5][:, k * TP:(k + 1) * TP], ACT.Identity, bias=col("bq", k))
                for k in range(2):
                    ins = act.activation(kT[u][:, k, :], bank[5][:, (2 + k) * TP:(3 + k) * TP], ACT.Identity, bias=col("bk", k))
                ins.then_inc(S["qk_read"], 1)
                act.wait_ge(S["gate_done"], t + 1)
                for k in range(2):
                    ins = act.activation(gateT[:, k, bass.ds(t * TP, TP)], bank[4][:, k * TP:(k + 1) * TP], ACT.Silu, bias=col("bg", k))
                ins.then_inc(S["gate_read"], 1)

            def stage2(s, u):
                loop = not isinstance(s, int)
                if loop or 0 <= s + 1 < NT:
                    projected(s + 1, 1 - u)
                if loop or s + 2 < NT:
                    turned(s + 2, u)
            skewed(act, stage2)

            def turned(dst, src, scale, bias):
                for k in range(2):
                    ins = act.activation(dst[:, k, :], src[:, k * 2 * TP:(k + 1) * 2 * TP], ACT.Identity,
                                         bias=col(bias, k), scale=col(scale, k))
                return ins

            def heads_turned(p):
                act.wait_ge(S["gnT_done"], p + 1)
                if later(p, 1):
                    act.wait_ge(S["gh_ready"], p)
                turned(gx, bank[5], "gnw", "gnb").then_inc(S["gx_ready"], 1)

            def x2_turned(p):
                act.wait_ge(S["x2T_done"], p + 1)
                if later(p, 1):
                    act.wait_ge(S["in_done"], NM * p)
                turned(xT, bank[5], "n2w", "n2b").then_inc(S["x2T_ready"], 1)

            def hidden(i, j):
                m = MS[j]
                act.wait_ge(S["in_done"], NM * i + j + 1)
                if later(i, 1) or j >= 2:
                    act.wait_ge(S["hid_ready"], NM * i + j - 1)
                act.activation(su[j % 2][0:m, :], bank[j % 3][0:m, 0:2 * TP], ACT.Silu,
                               bias=col("b_u", j, m)).then_inc(S["su_ready"], 1)

            def xf_turned(q):
                act.wait_ge(S["xfT_done"], q + 1)
                if later(q, 1):
                    act.wait_ge(S["logits_done"], q)
                act.activation(xfT.rearrange("p a b -> p (a b)"), bank[7][:, 0:4 * TP], ACT.Copy).then_inc(S["xfT_ready"], 1)
                act.activation(gateT[:, :, bass.ds(q * 2 * TP, 2 * TP)], bank[7][:, 0:4 * TP].rearrange("p (k t) -> p k t", k=2),
                               ACT.Copy).then_inc(S["xf_kept"], 1)

            def scored(q):
                act.wait_ge(S["logits_done"], q + 1)
                if later(q, 1):
                    act.wait_ge(S["choice_step"], CHOICE_STEPS * (q - 1) + 1)
                act.activation(sig[:, :, :].rearrange("p a b -> p (a b)"), bank[4][0:TP, 0:2 * NE], ACT.Sigmoid).then_inc(S["sig_ready"], 1)

            def stages35(s):
                if has(s, 0):
                    hidden(s, 0)
                if has(s, 1):
                    heads_turned(s + 1)
                if has(s, 0):
                    hidden(s, 1)
                    hidden(s, 2)
                if has(s, -1):
                    xf_turned(s - 1)
                if has(s, 0):
                    for j in range(3, NM):
                        hidden(s, j)
                if has(s, 1):
                    x2_turned(s + 1)
                if has(s, -1):
                    scored(s - 1)
            tower(act, stages35, hi=NPAIR + 1)

            def rows_turned(b, p):
                act.wait_ge(S["xgT_done"], b + 1)
                if later(b, 2):
                    act.wait_ge(S["gu_done"], b - 1)
                act.activation(xgT[p][:, :, :].rearrange("p a b -> p (a b)"), bank[p][:, 0:256], ACT.Copy).then_inc(S["xgT_ready"], 1)

            def gate_silu(b, p):
                act.wait_ge(S["gu_done"], b + 1)
                if later(b, 2):
                    act.wait_ge(S["hb_ready"], b - 1)
                act.activation(sg[p][:, :], bank[2 + p][:, 0:128], ACT.Silu).then_inc(S["sg_ready"], 1)

            rows_turned(0, 0)
            rows_turned(1, 1)
            for b in range(2):
                gate_silu(b, b)
                rows_turned(b + 2, b)
            with act.Fori(1, NBLK // 2 - 1) as i:
                for u in range(2):
                    gate_silu(2 * i + u, u)
                    rows_turned(2 * i + u + 2, u)
            gate_silu(NBLK - 2, 0)
            gate_silu(NBLK - 1, 1)

            def shared_silu(i):
                act.wait_ge(S["sh_done"], i + 1)
                if later(i, 1):
                    act.wait_ge(S["sh_ready"], i)
                act.activation(sh_s[0][:, :, :].rearrange("p a b -> p (a b)"), bank[0][:, 0:4 * TP], ACT.Silu).then_inc(S["sh_silu"], 1)
            shared_silu(0)
            with act.Fori(1, NPAIR) as i:
                shared_silu(i)

        @block.tensor
        def _(pe):
            def mm(out_, lhsT, rhs, start, stop):
                return pe.matmul(out_, lhsT, rhs, start=start, stop=stop)

            pe.wait_ge(S["posrow"], 32)

            def embed(t, u, n):
                pe.wait_ge(pat_loaded[u], 16 * (n + 1))
                if later(t, 2):
                    pe.wait_ge(S["h_ready"], t - 1)
                for k in range(KP):
                    ins = mm(bank[u % 2][0:TP, 0:D], pat[u][:, k, :], w_tok[:, k, :], k == 0, k == KP - 1)
                ins.then_inc(S["embedded"], 1)
            for t in range(PATS):
                embed(t, t, 0)
            with pe.Fori(1, NT // PATS) as i:
                for u in range(PATS):
                    embed(PATS * i + u, u, i)
            for t in range(NT // PATS * PATS, NT):
                embed(t, t % PATS, t // PATS)

            pe.wait_ge(S["weights"], 16 * (len(weights) + len(consts)))

            def turn_norm(t, u):
                pe.wait_ge(S["xn_ready"], t + 1)
                if later(t, 1):
                    pe.wait_ge(S["xT_ready"], t)
                for k in range(2):
                    ins = pe.transpose(bank[3][:, k * TP:(k + 1) * TP], xn[u][:, k * 128:(k + 1) * 128], ident[0:TP, 0:TP])
                ins.then_inc(S["xnT_done"], 1)

            def project(t, u):
                pe.wait_ge(S["xT_ready"], t + 1)
                if later(t, 1):
                    pe.wait_ge(S["qk_read"], t)
                for j in range(2):
                    for m in range(2):
                        for k in range(2):
                            ins = mm(bank[5][:, (2 * j + m) * TP:(2 * j + m + 1) * TP], wqk[:, k, j, m * 128:(m + 1) * 128],
                                     xT[:, k, 0:TP], k == 0, k == 1)
                ins.then_inc(S["qk_done"], 1)
                if later(t, 1):
                    pe.wait_ge(S["gate_read"], t)
                for m in range(2):
                    for k in range(2):
                        ins = mm(bank[4][:, m * TP:(m + 1) * TP], wqk[:, k, 2, m * 128:(m + 1) * 128], xT[:, k, 0:TP], k == 0, k == 1)
                ins.then_inc(S["gate_done"], 1)
                if later(t, 1):
                    pe.wait_ge(S["v_ready"], t)
                for k in range(2):
                    ins = mm(bank[6][0:TP, 0:D], xT[:, k, 0:TP], wqk[:, k, 3, :], k == 0, k == 1)
                ins.then_inc(S["v_done"], 1)

            def scores(t, u, j):
                if j == 0:
                    pe.wait_ge(S["qm0_ready"], t + 1)
                    pe.wait_ge(S["qm1_ready"], t + 1)
                    if later(t, 1):
                        pe.wait_ge(S["mask_done"], 4 * t)
                if j == 3:
                    pe.wait_ge(S["mask_done"], 4 * t + 1)
                mm(bank[j % 3][0:TP, 0:4 * TP], kT[u][:, j // 2, :], qm[u][:, 4 * j:4 * j + 4, :].rearrange("p a b -> p (a b)"),
                   True, True).then_inc(S["scores_done"], 1)

            def retain(t, u, j):
                pe.wait_ge(S["mask_done"], 4 * t + j + 1)
                if j == 0:
                    pe.wait_ge(S["v_ready"], t + 1)
                    if later(t, 1):
                        pe.wait_ge(S["cen_ready"], t)
                for n in range(4 * j, 4 * j + 4):
                    ins = mm(bank[7][0:TP, n * HD:(n + 1) * HD], ss[u][:, n, :], vv[u][:, n * HD:(n + 1) * HD], True, True)
                if j == 3:
                    ins.then_inc(S["av_done"], 1)

            def stage2(s, u):
                loop = not isinstance(s, int)
                if loop or 0 <= s + 1 < NT:
                    project(s + 1, 1 - u)
                if loop or s + 2 < NT:
                    turn_norm(s + 2, u)
                for j in range(4):
                    if loop or 0 <= s < NT:
                        scores(s, u, j)
                    if loop or 0 <= s - 1 < NT:
                        retain(s - 1, 1 - u, j)
            skewed(pe, stage2)

            pe.wait_ge(S["gate_read"], NT)
            pe.wait_ge(S["qk_read"], NT)
            pe.wait_ge(S["cen_ready"], NT)

            def turn(dst, src):
                for k in range(2):
                    for u in range(2):
                        at = (2 * k + u) * TP
                        ins = pe.transpose(dst[:, at:at + TP], src[:, u, k * 128:(k + 1) * 128], ident[0:TP, 0:TP])
                return ins

            def turn_heads(p):
                pe.wait_ge(S["gn_ready"], p + 1)
                if later(p, 1):
                    pe.wait_ge(S["x2T_ready"], p)
                turn(bank[5], gn).then_inc(S["gnT_done"], 1)

            def attn_out(p):
                pe.wait_ge(S["gh_ready"], p + 1)
                if later(p, 1):
                    pe.wait_ge(S["x1_ready"], p)
                for u in range(2):
                    for k in range(2):
                        ins = mm(bank[6][0:TP, u * D:(u + 1) * D], gh[:, k, u * TP:(u + 1) * TP], wo[:, k, :], k == 0, k == 1)
                ins.then_inc(S["wo_done"], 1)

            def turn_x2(p):
                pe.wait_ge(S["x2_ready"], p + 1)
                turn(bank[5], x2).then_inc(S["x2T_done"], 1)

            def mlp_in(i, j):
                m = MS[j]
                if j == 0:
                    pe.wait_ge(S["x2T_ready"], i + 1)
                if later(i, 1) or j >= 3:
                    pe.wait_ge(S["hid_ready"], NM * i + j - 2)
                for s in range(2):
                    for k in range(2):
                        at = s * HID + j * HM
                        ins = mm(bank[j % 3][0:m, s * 2 * TP:(s + 1) * 2 * TP], w_in[:, k, at:at + m], xT[:, k, :], k == 0, k == 1)
                ins.then_inc(S["in_done"], 1)

            def mlp_out(i, u):
                if u == 0 and later(i, 1):
                    pe.wait_ge(S["h1_ready"], i)
                for j, m in enumerate(MS):
                    if u == 0:
                        pe.wait_ge(S["hid_ready"], NM * i + j + 1)
                    ins = mm(bank[3][0:TP, u * D:(u + 1) * D], hT[0:m, j, u * TP:(u + 1) * TP], w_out[0:m, j, :], j == 0, j == NM - 1)
                if u == 1:
                    ins.then_inc(S["mlp_done"], 1)

            def turn_xf(q):
                pe.wait_ge(S["xf_ready"], q + 1)
                if later(q, 2):
                    pe.wait_ge(S["slot_step"], SLOT_STEPS * (q - 2) + 1)
                turn(bank[7], xf).then_inc(S["xfT_done"], 1)

            def route(q):
                if later(q, 1):
                    pe.wait_ge(S["sig_ready"], q)
                pe.wait_ge(S["xfT_ready"], q + 1)
                for u in range(2):
                    for k in range(2):
                        ins = mm(bank[4][0:TP, u * NE:(u + 1) * NE], xfT[:, k, u * TP:(u + 1) * TP], gw[:, k, :], k == 0, k == 1)
                ins.then_inc(S["logits_done"], 1)

            def place(q):
                pe.wait_ge(S["sel_ready"], q + 1)
                pe.wait_ge(S["xf_kept"], (q + 2) if later(q, NPAIR) else min(q + 2, NPAIR))
                for u in range(2):
                    at = u * NE
                    mm(bank[7][0:TP, at:at + NE], trib[:, :], sel[:, u, :], True, False)
                    ins = mm(bank[7][0:TP, at:at + NE], onesb[:, 0:TP], selsum[:, 2 * q + u, :], False, True)
                ins.then_inc(S["pos_done"], 1)

            def stages35(s):
                if has(s, 0):
                    mlp_in(s, 0)
                if has(s, -3):
                    place(s - 3)
                if has(s, 1):
                    turn_heads(s + 1)
                if has(s, 0):
                    mlp_in(s, 1)
                    mlp_in(s, 2)
                if has(s, 1):
                    attn_out(s + 1)
                if has(s, -1):
                    turn_xf(s - 1)
                if has(s, 0):
                    for j in range(3, NM):
                        mlp_in(s, j)
                if has(s, -1):
                    route(s - 1)
                if has(s, 0):
                    mlp_out(s, 0)
                if has(s, 1):
                    turn_x2(s + 1)
                if has(s, 0):
                    mlp_out(s, 1)
            tower(pe, stages35, lo=3, hi=NPAIR + 3)

            pe.wait_ge(S["sel_ready"], NPAIR)
            mm(bank[6][:, 0:NE], onesb[:, :], selsum[:, NT, :], True, True).then_inc(S["count_done"], 1)
            pe.wait_ge(S["vb_ready"], 1)
            for j in range(2):
                ins = mm(bank[7][:, j * 128:(j + 1) * 128], vb[:, j, :], ident[:, :], True, True)
            ins.then_inc(S["row_done"], 1)
            pe.wait_ge(S["block_rows"], 32)
            for j in range(2):
                ins = pe.transpose(bank[6][:, j * 128:(j + 1) * 128], blk_rows[:, j, :], ident[:, :])
            ins.then_inc(S["block_rows_turned"], 1)

            def turn_rows(b, q, p, n):
                pe.wait_ge(gathered[q], 16 * (n + 1))
                if later(b, 2):
                    pe.wait_ge(S["xgT_ready"], b - 1)
                for k in range(2):
                    ins = pe.transpose(bank[p][:, k * 128:(k + 1) * 128], xg[q][:, k * 128:(k + 1) * 128], ident[:, :])
                ins.then_inc(S["xgT_done"], 1)

            def gate_up(b, q, p, n):
                pe.wait_ge(w_loaded[q], 16 * (n + 1))
                pe.wait_ge(S["xgT_ready"], b + 1)
                if later(b, 2):
                    pe.wait_ge(S["hb_ready"], b - 1)
                for s in range(2):
                    for k in range(2):
                        at = k * 256 + s * 128
                        ins = mm(bank[2 + p][:, s * 128:(s + 1) * 128], moe_w[q][:, at:at + 128], xgT[p][:, k, :], k == 0, k == 1)
                ins.then_inc(S["gu_done"], 1)

            def down(b, q, p):
                pe.wait_ge(S["hb_ready"], b + 1)
                if later(b, 2):
                    pe.wait_ge(S["ys_ready"], b - 1)
                mm(bank[6 + p][:, 0:256], hb[p][:, :], moe_w[q][:, 512:768], True, True).then_inc(S["y_done"], 1)

            def stage6(i, q, first=False, ahead=True):
                b, p, m = UNROLL * i + q, q % 2, (q - 1) % UNROLL
                gate_up(b, q, p, i)
                if ahead:
                    turn_rows(b + 2, (q + 2) % UNROLL, p, i + (q + 2) // UNROLL)
                if not first:
                    down(b - 1, m, 1 - p)

            pe.wait_ge(S["idx_ready"], 1)
            turn_rows(0, 0, 0, 0)
            turn_rows(1, 1, 1, 0)
            for q in range(UNROLL):
                stage6(0, q, first=q == 0)
            with pe.Fori(1, NBLK // UNROLL - 1) as i:
                for q in range(UNROLL):
                    stage6(i, q)
            for q in range(UNROLL):
                stage6(NBLK // UNROLL - 1, q, ahead=q < UNROLL - 2)
            down(NBLK - 1, UNROLL - 1, 1)

            pe.wait_ge(S["ys_ready"], NBLK)
            pe.wait_ge(S["xf_kept"], NPAIR)

            def shared_in(i):
                for s in range(2):
                    if later(i, 1):
                        pe.wait_ge(S["sh_silu" if s == 0 else "sh_ready"], i)
                    for m in range(2):
                        for k in range(2):
                            ins = mm(bank[s][:, m * 2 * TP:(m + 1) * 2 * TP], sgu[:, k, s, m * 128:(m + 1) * 128],
                                     gateT[:, k, bass.ds(i * 2 * TP, 2 * TP)], k == 0, k == 1)
                ins.then_inc(S["sh_done"], 1)

            def shared_out(i):
                pe.wait_ge(S["sh_ready"], i + 1)
                for u in range(2):
                    if later(i, 1):
                        pe.wait_ge(S["acc_ready"], 2 * i + u - 1)
                    for k in range(2):
                        ins = mm(bank[2 + u][0:TP, 0:D], sh_s[1][:, k, u * TP:(u + 1) * TP], sdw[:, k, :], k == 0, k == 1)
                    ins.then_inc(S["sd_done"], 1)
            shared_in(0)
            shared_out(0)
            with pe.Fori(1, NPAIR) as i:
                shared_in(i)
                shared_out(i)

        @block.vector
        def _(dve):
            dve.wait_ge(S["posrow"], 16 * (2 + PER))

            def embedded(t, u, n=0):
                dve.wait_ge(S["embedded"], t + 1)
                dve.tensor_tensor(h[:, t, :], bank[u][0:TP, 0:D], pos[:, :], ALU.add).then_inc(S["h_ready"], 1)
                dve.wait_ge(S["h_ready"], t + 1)
                dve.bn_stats(st[:, t, :], h[:, t, :]).then_inc(S["h_stats"], 1)
            pairs(dve, 0, NPAIR, embedded)

            dve.wait_ge(S["table_cleared"], 16)
            dve.wait_ge(S["norms_ready"], 1)
            dve.wait_ge(S["weights"], 16 * (len(weights) + len(consts)))
            dve.tensor_copy(trib[:, :], tri[:, :]).then_inc(S["setup"], 1)

            def normed(t, u):
                dve.tensor_scalar(x[:, t, :], h[:, t, :], rs[:, MEAN, bass.ds(t, 1)], rs[:, RSTD, bass.ds(t, 1)],
                                  ALU.subtract, ALU.mult).then_inc(S["x0_ready"], 1)
                if later(t, 2):
                    dve.wait_ge(S["xnT_done"], t - 1)
                dve.tensor_scalar(xn[u][:, :], h[:, t, :], rs[:, MEAN, bass.ds(t, 1)], rs[:, BOTH, bass.ds(t, 1)],
                                  ALU.subtract, ALU.mult).then_inc(S["xn_ready"], 1)

            def mask_queries(t, u, n=0):
                dve.wait_ge(S["qk_read"], t + 1)
                if later(t, 2):
                    dve.wait_ge(S["scores_done"], 4 * (t - 1))
                dve.tensor_tensor(qm[u][:, 0:8, :], bc(qT[u][:, 0, :], 1, 8), bc(hmask[:, :], 2, TP),
                                  ALU.mult).then_inc(S["qm0_ready"], 1)

            def decay_scores(t, u):
                if later(t, 2):
                    dve.wait_ge(S["av_done"], t - 1)
                for j in range(4):
                    dve.wait_ge(S["scores_done"], 4 * t + j + 1)
                    dve.tensor_tensor(ss[u][:, 4 * j:4 * j + 4, :], bank[j % 3][0:TP, 0:4 * TP].rearrange("p (a b) -> p a b", a=4),
                                      decay[:, 4 * j:4 * j + 4, :], ALU.mult).then_inc(S["mask_done"], 1)

            def values(t, u):
                dve.wait_ge(S["v_done"], t + 1)
                if later(t, 2):
                    dve.wait_ge(S["av_done"], t - 1)
                dve.tensor_tensor(vv[u][:, :], bank[6][0:TP, 0:D], row("bv"), ALU.add).then_inc(S["v_ready"], 1)

            def centre(t, u):
                heads = bank[7][0:TP, 0:D].rearrange("p (n d) -> p n d", n=NH)
                cen_t = cen[:, t, :].rearrange("p (n d) -> p n d", n=NH)
                dve.wait_ge(S["av_done"], t + 1)
                if later(t, 2):
                    dve.wait_ge(S["cen_ready"], t - 1)
                dve.tensor_reduce(gsum[u][:, :], heads, AX.X, ALU.add).then_inc(S["head_sum"], 1)
                dve.wait_ge(S["head_sum"], t + 1)
                dve.scalar_tensor_tensor(cen_t, bc(gsum[u][:, :], 2, HD), -1.0 / HD, heads, ALU.mult, ALU.add).then_inc(S["cen_ready"], 1)
                dve.wait_ge(S["cen_ready"], t + 1)
                if later(t, 1):
                    dve.wait_ge(S["gvar_ready"], t)
                dve.tensor_tensor(gsq[:, :], cen[:, t, :], cen[:, t, :], ALU.mult).then_inc(S["head_sq"], 1)
                dve.wait_ge(S["head_sq"], t + 1)
                if later(t, 2):
                    dve.wait_ge(S["gvar_ready"], t - 1)
                dve.tensor_reduce(gsum[u][:, :], gsq[:, :].rearrange("p (n d) -> p n d", n=NH), AX.X, ALU.add).then_inc(S["grs_step"], 1)
                dve.wait_ge(S["grs_step"], t + 1)
                dve.tensor_scalar(grs[:, t, :], gsum[u][:, :], 1.0 / HD, EPS, ALU.mult, ALU.add).then_inc(S["gvar_ready"], 1)

            def stage2(s, u):
                loop = not isinstance(s, int)
                if loop or s + 2 < NT:
                    normed(s + 2, u)
                if loop or 0 <= s - 2 < NT:
                    centre(s - 2, u)
                if loop or 0 <= s + 1 < NT:
                    mask_queries(s + 1, 1 - u)
                if loop or 0 <= s < NT:
                    decay_scores(s, u)
                if loop or 0 <= s + 1 < NT:
                    values(s + 1, 1 - u)
            skewed(dve, stage2, lambda: dve.wait_ge(S["norms_ready"], 2))

            dve.wait_ge(S["grs_ready"], NT)
            dve.wait_ge(S["x0b_ready"], NT)
            dve.wait_ge(S["hb_out"], NT)

            def group_normed(p):
                if later(p, 1):
                    dve.wait_ge(S["gnT_done"], p)
                dve.tensor_tensor(gn.rearrange("p a (n d) -> p (a n) d", n=NH),
                                  cen[:, bass.ds(2 * p, 2), :].rearrange("p a (n d) -> p (a n) d", n=NH),
                                  bc(gvar[:, bass.ds(2 * p, 2), :].rearrange("p a n -> p (a n)"), 2, HD), ALU.mult).then_inc(S["gn_ready"], 1)

            def gate_heads(p):
                dve.wait_ge(S["gx_ready"], p + 1)
                if later(p, 1):
                    dve.wait_ge(S["wo_done"], p)
                dve.tensor_tensor(gh, gx, gateT[:, :, bass.ds(2 * p * TP, 2 * TP)], ALU.mult).then_inc(S["gh_ready"], 1)

            def moments(src, st_, mv, p, ready, stats, done):
                settle(dve)
                dve.wait_ge(S[ready], p + 1)
                for u in range(2):
                    ins = dve.bn_stats(st_[:, u, :], src[:, 2 * p + u, :])
                ins.then_inc(S[stats], 1)
                settle(dve)
                dve.wait_ge(S[stats], p + 1)
                for u in range(2):
                    ins = dve.bn_aggr(mv[:, u, :], st_[:, u, :])
                ins.then_inc(S[done], 1)

            def two(a_, p):
                return a_[:, bass.ds(2 * p, 2), :]

            def attended(p):
                dve.wait_ge(S["wo_done"], p + 1)
                dve.tensor_tensor(two(x, p), bank[6][0:TP, :].rearrange("p (a n) -> p a n", a=2), two(x, p), ALU.add).then_inc(S["x1_ready"], 1)
                moments(x, st_x, mv_x, p, "x1_ready", "x1_stats", "x1_moments")
                dve.tensor_tensor(two(h, p), two(h, p), two(x, p), ALU.add).then_inc(S["hx_ready"], 1)

            def normed_by(dst, src, i, mv, rstd, ready):
                for u in range(2):
                    ins = dve.tensor_scalar(dst[:, u, :], src[:, 2 * i + u, :], mv[:, u, 0:1], rstd[:, 1, u:u + 1], ALU.subtract, ALU.mult)
                ins.then_inc(S[ready], 1)

            def x2_normed(p):
                dve.wait_ge(S["rs2_ready"], p + 1)
                if later(p, 1):
                    dve.wait_ge(S["x2T_done"], p)
                normed_by(x2, x, p, mv_x, rstd_x, "x2_ready")

            def hidden(i, j):
                m = MS[j]
                if j == 0 and later(i, 1):
                    dve.wait_ge(S["mlp_done"], i)
                dve.wait_ge(S["su_ready"], NM * i + j + 1)
                dve.scalar_tensor_tensor(hT[0:m, j, :], bank[j % 3][0:m, 2 * TP:4 * TP], col("b_g", j, m),
                                         su[j % 2][0:m, :], ALU.add, ALU.mult).then_inc(S["hid_ready"], 1)

            def mlp_added(q):
                dve.wait_ge(S["mlp_done"], q + 1)
                dve.wait_ge(S["hx_ready"], q + 1)
                dve.tensor_tensor(two(h, q), bank[3][0:TP, :].rearrange("p (a n) -> p a n", a=2), two(h, q), ALU.add).then_inc(S["h1_ready"], 1)
                moments(h, st_h, mv_h, q, "h1_ready", "h1_stats", "h1_moments")

            def last_norm(q):
                dve.wait_ge(S["rs3_ready"], q + 1)
                if later(q, 1):
                    dve.wait_ge(S["xfT_done"], q)
                    dve.wait_ge(xf_stored, 16 * q)
                normed_by(xf, h, q, mv_h, rstd_h, "xf_ready")

            count = {}

            def before_max(name, q, ins):
                ins.then_inc(S[name], 1)
                settle(dve)
                dve.wait_ge(S[name], q + 1)

            def chain(name, total, q, ins):
                ins.then_inc(S[name], 1)
                count[name] = count.get(name, 0) % total + 1
                dve.wait_ge(S[name], total * q + count[name])

            def choose_groups(q):
                def do(ins):
                    chain("choice_step", CHOICE_STEPS, q, ins)
                dve.wait_ge(S["sig_ready"], q + 1)
                do(dve.tensor_tensor(sc[:, :, :], sig[:, :, :], bc(gbias[:, :], 1, 2), ALU.add))
                before_max("gmax_ready", q, dve.tensor_reduce(gmax[:, :, :], sc[:, :, :].rearrange("p a (g e) -> p a g e", g=NG), AX.X, ALU.max))
                for u in range(2):
                    ins = dve.max(top[:, u, :], gmax[:, u, :])
                before_max("top_ready", q, ins)
                for u in range(2):
                    ins = dve.max_index(idx[:, u, :], top[:, u, :], gmax[:, u, :])
                do(ins)
                do(dve.tensor_copy(idf[:, :, :], idx[:, :, :]))
                do(dve.tensor_tensor(geq[:, :, :, :], bc(bc(io64[:, 0:NG], 1, TOPG), 1, 2), bc(idf[:, :, 0:TOPG], 3, NG), ALU.is_equal))
                do(dve.tensor_reduce(gsel[:, :, :], geq[:, :, :, :].rearrange("p a k g -> p a g k"), AX.X, ALU.add))

            def choose_experts(q):
                def do(ins):
                    chain("choice_step", CHOICE_STEPS, q, ins)
                grouped = sc[:, :, :].rearrange("p a (g e) -> p (a g) e", g=NG)
                before_max("masked_ready", q, dve.tensor_tensor(grouped, grouped, bc(gsel[:, :, :].rearrange("p a g -> p (a g)"), 2, EG), ALU.mult))
                for u in range(2):
                    ins = dve.max(etop[:, u, :], sc[:, u, :])
                before_max("etop_ready", q, ins)
                for u in range(2):
                    ins = dve.max_index(idx[:, u, :], etop[:, u, :], sc[:, u, :])
                do(ins)
                do(dve.tensor_copy(idf[:, :, :], idx[:, :, :]))
                dve.tensor_copy(chosen[:, bass.ds(2 * q, 2), :], idf[:, :, 0:TOPK])
                do(dve.tensor_tensor(oh, bc(bc(io64[:, :], 1, TOPK), 1, 2), bc(idf[:, :, 0:TOPK], 3, NE), ALU.is_equal))

            def choice_kept(q):
                def do(ins):
                    chain("choice_step", CHOICE_STEPS, q, ins)
                do(dve.tensor_reduce(smap[:, :, :], oh.rearrange("p a k e -> p a e k"), AX.X, ALU.add))
                dve.tensor_copy(sel[:, :, :], smap[:, :, :])
                do(dve.tensor_tensor(selsum[:, 2 * q + 1, :], selsum[:, 2 * q, :], smap[:, 0, :], ALU.add))
                dve.tensor_tensor(selsum[:, 2 * q + 2, :], selsum[:, 2 * q + 1, :], smap[:, 1, :], ALU.add).then_inc(S["sel_ready"], 1)
                do(dve.tensor_reduce(wsum[:, 0, :], etop[:, :, 0:TOPK], AX.X, ALU.add))
                do(dve.tensor_scalar(wsum[:, 1, :], wsum[:, 0, :], 1e-8, None, ALU.add))
                do(dve.reciprocal(wsum[:, 2, :], wsum[:, 1, :]))
                do(dve.tensor_tensor(wk[:, bass.ds(2 * q, 2), :], etop[:, :, 0:TOPK], bc(wsum[:, 2, :], 2, TOPK), ALU.mult))
                assert count["choice_step"] == CHOICE_STEPS

            def take_slots(q, part):
                def do(ins):
                    chain("slot_step", SLOT_STEPS, q, ins)
                if part == 0:
                    dve.wait_ge(S["pos_done"], q + 1)
                    do(dve.tensor_tensor(smap[:, :, :], bank[7][0:TP, 0:2 * NE].rearrange("p (a e) -> p a e", a=2),
                                         bc(ebase[:, :], 1, 2), ALU.add))
                    do(dve.tensor_tensor(prod, oh, bc(smap[:, :, :], 2, TOPK), ALU.mult))
                else:
                    do(dve.tensor_reduce(slf[:, :, :], prod, AX.X, ALU.add))
                    dve.tensor_copy(slot[:, bass.ds(2 * q, 2), :], slf[:, :, :]).then_inc(S["slots_ready"], 1)
                    assert count["slot_step"] == SLOT_STEPS

            def stages35(s):
                if isinstance(s, int) and s == -1:
                    group_normed(0)
                if has(s, -1):
                    mlp_added(s - 1)
                if has(s, 0):
                    hidden(s, 0)
                if has(s, 1):
                    gate_heads(s + 1)
                if has(s, -1):
                    last_norm(s - 1)
                if has(s, -3):
                    take_slots(s - 3, 0)
                if has(s, 0):
                    hidden(s, 1)
                if has(s, -3):
                    take_slots(s - 3, 1)
                if has(s, 0):
                    hidden(s, 2)
                if has(s, 1):
                    attended(s + 1)
                if has(s, 0):
                    hidden(s, 3)
                    hidden(s, 4)
                if has(s, -2):
                    choose_groups(s - 2)
                if has(s, 0):
                    hidden(s, 5)
                if has(s, 1):
                    x2_normed(s + 1)
                if has(s, 2):
                    group_normed(s + 2)
                if has(s, -2):
                    choose_experts(s - 2)
                    choice_kept(s - 2)
            tower(dve, stages35, lo=3, end=NPAIR - 2, hi=NPAIR + 3)

            n_tb = [0]

            def do(ins):
                ins.then_inc(S["tb"], 1)
                n_tb[0] += 1
                dve.wait_ge(S["tb"], n_tb[0])
            dve.wait_ge(S["count_done"], 1)
            do(dve.tensor_scalar(nbf[:, :], bank[6][:, 0:NE], 127.0, None, ALU.add))
            do(dve.tensor_copy(nbi[:, :], nbf[:, :]))
            do(dve.tensor_scalar(nbi[:, :], nbi[:, :], 7, None, ALU.arith_shift_right))
            do(dve.tensor_copy(nbf[:, :], nbi[:, :]))
            do(dve.tensor_tensor_scan(bend[:, :], ones64[:, :], nbf[:, :], 0.0, ALU.mult, ALU.add))
            do(dve.tensor_tensor(shift[:, :], bend[0:TP, :], nbf[0:TP, :], ALU.subtract))
            do(dve.scalar_tensor_tensor(shift[:, :], shift[:, :], 128.0, ebase[:, :], ALU.mult, ALU.subtract))
            for j in range(2):
                do(dve.tensor_scalar(le[:, j, :], bend[:, :], bcol[:, j:j + 1], None, ALU.is_le))
                do(dve.tensor_tensor(lb[:, j, :], le[:, j, :], bend[:, :], ALU.mult))
            do(dve.tensor_reduce(ecol[:, :], le[:, :, :], AX.X, ALU.add))
            do(dve.tensor_reduce(scol[:, :], lb[:, :, :], AX.X, ALU.max))
            do(dve.tensor_tensor(scol[:, :], bcol[:, :], scol[:, :], ALU.subtract))
            do(dve.scalar_tensor_tensor(scol[:, :], ecol[:, :], float(SLOT_BLOCKS), scol[:, :], ALU.mult, ALU.add))
            do(dve.tensor_scalar(scol[:, :], scol[:, :], float(TAB_BLOCKS - 1), None, ALU.min))
            dve.tensor_copy(scol_i[:, :], scol[:, :]).then_inc(S["blocks_ready"], 1)
            do(dve.tensor_scalar(ecol[:, :], ecol[:, :], float(NE - 1), None, ALU.min))
            for j in range(2):
                ins = dve.tensor_copy(vb[:, j, :], ecol[:, j:j + 1].to_broadcast([128, 128]))
            ins.then_inc(S["vb_ready"], 1)
            dve.wait_ge(S["row_done"], 1)
            dve.tensor_copy(rowi[0:1, :], bank[7][0:1, 0:256]).then_inc(S["rows_ready"], 1)
            dve.wait_ge(S["block_rows_turned"], 1)
            dve.tensor_copy(blk_idx[:, :], bank[6][:, 0:NBLK]).then_inc(S["idx_ready"], 1)

            def product(b, p):
                dve.wait_ge(S["sg_ready"], b + 1)
                if later(b, 2):
                    dve.wait_ge(S["y_done"], b - 1)
                dve.tensor_tensor(hb[p][:, :], bank[2 + p][:, 128:256], sg[p][:, :], ALU.mult).then_inc(S["hb_ready"], 1)

            def rows_out(b, p, n):
                dve.wait_ge(S["y_done"], b + 1)
                if later(b, 2):
                    dve.wait_ge(y_stored[p], 16 * n)
                dve.tensor_copy(ys[p][:, :], bank[6 + p][:, 0:256]).then_inc(S["ys_ready"], 1)

            product(0, 0)
            for b in range(1, 4):
                product(b, b % 2)
                rows_out(b - 1, (b - 1) % 2, (b - 1) // 2)
            with dve.Fori(2, NBLK // 2) as i:
                for u in range(2):
                    product(2 * i + u, u)
                    rows_out(2 * i + u - 1, 1 - u, i + (u - 1))
            rows_out(NBLK - 1, 1, NBLK // 2 - 1)

            def shared_product(i):
                dve.wait_ge(S["sh_silu"], i + 1)
                if later(i, 1):
                    dve.wait_ge(S["sd_done"], 2 * i)
                dve.tensor_tensor(sh_s[1][:, :, :].rearrange("p a b -> p (a b)"), bank[1][:, 0:4 * TP],
                                  sh_s[0][:, :, :].rearrange("p a b -> p (a b)"), ALU.mult).then_inc(S["sh_ready"], 1)

            def result_rows(t, u, n=0):
                dve.tensor_tensor(oh[:, 0], bc(io64[:, :], 1, TOPK), bc(chosen[:, t, :], 2, NE), ALU.is_equal).then_inc(S["yrow_step"], 1)
                dve.wait_ge(S["yrow_step"], 3 * t + 1)
                dve.tensor_tensor(prod[:, 0], oh[:, 0], bc(shift[:, :], 1, TOPK), ALU.mult).then_inc(S["yrow_step"], 1)
                dve.wait_ge(S["yrow_step"], 3 * t + 2)
                dve.tensor_reduce(slf[:, 0, :], prod[:, 0], AX.X, ALU.add).then_inc(S["yrow_step"], 1)
                dve.wait_ge(S["yrow_step"], 3 * t + 3)
                dve.tensor_tensor(yrow[:, t, :], slf[:, 0, :], slot[:, t, :], ALU.add).then_inc(S["yrow_ready"], 1)

            def combine(t, u, n):
                dve.wait_ge(S["sd_done"], t + 1)
                dve.tensor_tensor(h[:, t, :], bank[2 + u][0:TP, 0:D], h[:, t, :], ALU.add).then_inc(S["acc_ready"], 1)
                dve.wait_ge(S["acc_ready"], t + 1)
                dve.wait_ge(cg_loaded[u], 16 * TOPK * (n + 1))
                for k in range(TOPK):
                    ins = dve.scalar_tensor_tensor(h[:, t, :], cg[u][:, k, :], wk[:, t, k:k + 1], h[:, t, :], ALU.mult, ALU.add)
                    if k < TOPK - 1:
                        ins.then_inc(S["acc_step"], 1)
                        dve.wait_ge(S["acc_step"], (TOPK - 1) * t + k + 1)
                ins.then_inc(S["combined"], 1)
            result_rows(0, 0)
            result_rows(1, 1)
            shared_product(0)
            for u in range(2):
                result_rows(2 + u, u)
                combine(u, u, 0)
            with dve.Fori(1, NPAIR - 1) as i:
                shared_product(i)
                for u in range(2):
                    result_rows(2 * i + 2 + u, u)
                    combine(2 * i + u, u, i)
            shared_product(NPAIR - 1)
            combine(NT - 2, 0, NPAIR - 1)
            combine(NT - 1, 1, NPAIR - 1)


def kernel(**inputs):
    import numpy as np
    import concourse.bacc as bacc
    from concourse.bass_utils import run_bass_kernel_spmd

    g = {k: np.asarray(v) for k, v in inputs.items()}
    at, ff = "L0_attn_", "L0_ffn_"
    p = g["x"].reshape(SEQS, 3, 6, 16, 6, 16).transpose(0, 2, 4, 1, 3, 5).reshape(SEQS, 36, KP * 128)
    full = np.zeros((NT * PER, SEQ, KP * 128), np.float32)
    full[:SEQS, 1:] = p
    patches = full.reshape(NT, TP, KP, 128).transpose(0, 3, 2, 1).reshape(NT, 128, KP * TP)

    vec = np.zeros((128, NVEC), np.float32)
    for name, key in (("n1w", "norm1_w"), ("n1b", "norm1_b"), ("bq", "bq"), ("bk", "bk"), ("bg", "bg"),
                      ("gnw", "gn_w"), ("gnb", "gn_b"), ("n2w", "norm2_w"), ("n2b", "norm2_b")):
        vec[:, VEC[name]:VEC[name] + 2] = g[at + key].reshape(2, 128).T
    for s, name in enumerate(("b_u", "b_g")):
        for j, m in enumerate(MS):
            vec[:m, VEC[name] + j] = g[at + "b_in"][s * HID + j * HM:s * HID + j * HM + m]
    eg, eu, ed = (g[ff + n] for n in ("eg_w", "eu_w", "ed_w"))
    gu = np.stack([eg.transpose(0, 2, 1), eu.transpose(0, 2, 1)], 2).reshape(NE, 2, 128, 256).transpose(0, 2, 1, 3)
    moe = np.concatenate([gu.reshape(NE, 128, 512), ed.transpose(0, 2, 1)], 2)

    gamma = (1.0 - np.exp2(-5.0 - np.arange(NH, dtype=np.float32))).astype(np.float32)
    key, query = np.arange(TP)[:, None, None], np.arange(TP)[None, None, :]
    diff = (query - key).astype(np.float32)
    same = (key // SEQ == query // SEQ) & (diff >= 0)
    decay = np.where(same, np.exp(np.log(gamma)[None, :, None] * np.maximum(diff, 0)) * np.float32(HD ** -0.5), 0)
    p128 = np.arange(128)
    arrays = {
        "patches": patches, "w_tok": g["L0_tok_W"], "b_tok": g["L0_tok_b"], "cls": g["cls_tok"].reshape(1, D),
        "wq": g[at + "wq"], "wk": g[at + "wk"], "wg": g[at + "wg"], "wv": g[at + "wv"], "wo": g[at + "wo"],
        "bv": g[at + "bv"], "bo": g[at + "bo"], "b_out": g[at + "b_out"],
        "w_in": g[at + "w_in"], "w_out": g[at + "w_out"],
        "sgT": g[ff + "sg_w"].T, "suT": g[ff + "su_w"].T, "sdT": g[ff + "sd_w"].T, "gateT": g[ff + "gate_w"].T,
        "gate_bias": g[ff + "gate_bias"], "moe": moe, "c_vec": vec,
        "c_ident": np.eye(128), "c_hmask": (p128[:, None] // HD == np.arange(8)[None]),
        "c_tri": np.triu(np.ones((TP, TP)), 1), "c_decay": decay.reshape(TP, NH * TP),
        "c_io64": np.arange(NE), "c_ebase": np.arange(NE) * SLOT_BLOCKS * 128,
        "c_bcol": p128[:, None] + np.array([[0, 128]]),
        "c_tid": np.arange(TP)[:, None] + TP * np.arange(NT)[None],
    }
    arrays = {n: np.ascontiguousarray(v, dtype=np.float32) for n, v in arrays.items()}

    nc = bacc.Bacc("TRN2", target_bir_lowering=False, num_devices=1)
    aps = {n: nc.dram_tensor(f"in_{n}", v.shape, mybir.dt.from_np(v.dtype), kind="ExternalInput").ap() for n, v in arrays.items()}
    out = nc.dram_tensor("out_0", (SEQS * SEQ, D), F32, kind="ExternalOutput").ap()
    build(nc, aps, out)
    r = run_bass_kernel_spmd(nc, [{f"in_{n}": v for n, v in arrays.items()}], core_ids=[0])
    return r.results[0]["out_0"].reshape(SEQS, SEQ, D)
```

```python
from contextlib import ExitStack

import concourse.bass as bass
from concourse import mybir

F32 = mybir.dt.float32
BF16 = mybir.dt.bfloat16
I32 = mybir.dt.int32
U32 = mybir.dt.uint32
ALU = mybir.AluOpType
ACT = mybir.ActivationFunctionType
AX = mybir.AxisListType

SEQS, SEQ, D = 64, 37, 256
PER = 3
TP = PER * SEQ
NT = 22
NPAIR = NT // 2
TALL = NT * TP
KP = 6
NH, HD = 16, 16
HID, HM, NM = 682, 114, 6
MS = [HM] * (NM - 1) + [HID - HM * (NM - 1)]
NE, TOPK, NG, TOPG = 64, 6, 8, 4
EG = NE // NG
SLOT_BLOCKS = -(-TALL // 128)
UNROLL = 6
NREAL = SEQS * SEQ
LAST = NREAL - (NT - 1) * TP
NBLK = (NREAL * TOPK + NE * 127) // 128
LANE = -(-NBLK // UNROLL)
NBLK = LANE * UNROLL
TAB_BLOCKS = NE * SLOT_BLOCKS + 128
EPS = 1e-5
SPLIT = 3
TURNS = 6
FULL, REST = divmod(NREAL, 128)
assert FULL % 2 == 0 and REST and NBLK % 2 == 0
PATS = 4
FIRST = 16
RSTD, MEAN, BOTH = 0, 1, 6
CHOICE_STEPS, SLOT_STEPS = 14, 3

VEC = {}
_at = 0
for _name, _w in (("n1w", 2), ("n1b", 2), ("bq", 2), ("bk", 2), ("bg", 2), ("gnw", 2), ("gnb", 2),
                  ("n2w", 2), ("n2b", 2), ("b_u", NM), ("b_g", NM)):
    VEC[_name] = _at
    _at += _w
NVEC = _at
ROWS = ("bv", "bo", "b_out")


def later(t, k):
    return not isinstance(t, int) or t >= k


def build(nc, a, out):
    with ExitStack() as ctx:
        def sb(name, shape, dt=F32):
            return ctx.enter_context(nc.sbuf_tensor(name, shape, dt))

        def sem(name):
            return ctx.enter_context(nc.semaphore(name))

        x_rows = nc.dram_tensor("x_rows", (TALL, D), F32, kind="Internal").ap()
        slot_token = nc.dram_tensor("slot_token", (TAB_BLOCKS * 128, 1), F32, kind="Internal").ap()
        h_rows = nc.dram_tensor("h_rows", (TALL, D), F32, kind="Internal").ap()
        wk_rows = nc.dram_tensor("wk_rows", (TALL, TOPK), F32, kind="Internal").ap()
        yrow_rows = nc.dram_tensor("yrow_rows", (TALL, TOPK), F32, kind="Internal").ap()
        y_rows = nc.dram_tensor("y_rows", (NBLK * 128, D), F32, kind="Internal").ap()

        h = sb("h", [TP, NT, D])
        x = sb("x", [TP, NT, D])
        cen = sb("cen", [TP, NT, D])
        gateT = sb("gateT", [128, 2, TALL])
        st = sb("st", [TP, NT, 6])
        gvar = sb("gvar", [TP, NT, NH])
        grs = sb("grs", [TP, NT, NH])
        rs = sb("rs", [TP, 7, NT])
        half = sb("half", [TP, NT])

        w_tok = sb("w_tok", [128, KP, D])
        wqk = sb("wqk", [128, 2, 4, D])
        wo = sb("wo", [128, 2, D])
        w_in = sb("w_in", [128, 2, 2 * HID])
        w_out = sb("w_out", [HM, NM, D])
        sgu = sb("sgu", [128, 2, 2, D])
        sdw = sb("sdw", [128, 2, D])
        gw = sb("gw", [128, 2, NE])
        vec = sb("vec", [128, NVEC])
        rows = sb("rows", [TP, len(ROWS), D])
        pos = sb("pos", [TP, D])
        gbias = sb("gbias", [TP, NE])
        decay = sb("decay", [TP, NH, TP])
        hmask = sb("hmask", [128, 8])
        ident = sb("ident", [128, 128])
        tri = sb("tri", [TP, TP])
        trib = sb("trib", [TP, TP], BF16)
        onesb = sb("onesb", [TP, 128], BF16)
        io64 = sb("io64", [TP, NE])
        ebase = sb("ebase", [TP, NE])
        tid = sb("tid", [TP, NT])

        xn_pair = sb("xn_pair", [TP, 2, D])
        xn = [xn_pair[:, u, :] for u in range(2)]
        xT = sb("xT", [128, 2, 2 * TP])
        qT = [sb(f"qT{u}", [128, 2, TP]) for u in range(2)]
        kT = [sb(f"kT{u}", [128, 2, TP]) for u in range(2)]
        qm = [sb(f"qm{u}", [128, NH, TP]) for u in range(2)]
        vv = [sb(f"vv{u}", [TP, D]) for u in range(2)]
        ss = [sb(f"ss{u}", [TP, NH, TP]) for u in range(2)]
        gn = xn_pair
        gsum = [sb(f"gsum{u}", [TP, NH]) for u in range(2)]
        gsq = sb("gsq", [TP, D])
        q0, q1 = (qm[u][:, :, :].rearrange("p a b -> p (a b)") for u in range(2))
        pat = [gateT[:, :, :].rearrange("p a b -> p (a b)")[:, u * KP * TP:(u + 1) * KP * TP].rearrange("p (k t) -> p k t", k=KP)
               for u in range(PATS)]
        tab_zero = q1[:, 0:TAB_BLOCKS]
        su = [q1[:, u * 2 * TP:(u + 1) * 2 * TP] for u in range(2)]
        hT = q0[:, 0:NM * 2 * TP].rearrange("p (j t) -> p j t", j=NM)
        st_x, st_h = (sb(f"st_{n}", [TP, 2, 6]) for n in "xh")
        mv_x, mv_h = (sb(f"mv_{n}", [TP, 2, 2]) for n in "xh")
        rstd_x, rstd_h = (sb(f"rstd_{n}", [TP, 2, 2]) for n in "xh")
        ss0, ss1 = (ss[u][:, :, :].rearrange("p a b -> p (a b)") for u in range(2))
        x2, xf = (ss1[:, j * 2 * D:(j + 1) * 2 * D].rearrange("p (a n) -> p a n", a=2) for j in range(2))
        xfT, gx, gh = (q1[:, j * 4 * TP:(j + 1) * 4 * TP].rearrange("p (k t) -> p k t", k=2) for j in (1, 2, 3))
        eps = sb("eps", [TP, 2])
        sig = sb("sig", [TP, 2, NE])
        sc = sb("sc", [TP, 2, NE])
        gmax = sb("gmax", [TP, 2, NG])
        top = sb("top", [TP, 2, 8])
        idx = sb("idx", [TP, 2, 8], U32)
        idf = sb("idf", [TP, 2, 8])
        geq = sb("geq", [TP, 2, TOPG, NG])
        gsel = sb("gsel", [TP, 2, NG])
        etop = sb("etop", [TP, 2, 8])
        oh, prod = (ss0[:, u * 2 * TOPK * NE:(u + 1) * 2 * TOPK * NE].rearrange("p (a k e) -> p a k e", a=2, k=TOPK) for u in range(2))
        sel = sb("sel", [TP, 2, NE], BF16)
        selsum = sb("selsum", [TP, NT + 1, NE], BF16)
        smap = sb("smap", [TP, 2, NE])
        slf = sb("slf", [TP, 2, TOPK])
        slot = sb("slot", [TP, NT, TOPK])
        chosen = sb("chosen", [TP, NT, TOPK])
        yrow = sb("yrow", [TP, NT, TOPK])
        shift = sb("shift", [TP, NE])
        slc = [sb(f"slc{u}", [128, TOPK], I32) for u in range(2)]
        tic = [sb(f"tic{u}", [TP, 1]) for u in range(2)]
        wk = sb("wk", [TP, NT, TOPK])
        wsum = sb("wsum", [TP, 3, 2])
        nbf = sb("nbf", [128, NE])
        nbi = sb("nbi", [128, NE], I32)
        bend = sb("bend", [128, NE])
        ones64 = sb("ones64", [128, NE])
        le = sb("le", [128, 2, NE])
        lb = sb("lb", [128, 2, NE])
        bcol = sb("bcol", [128, 2])
        ecol = sb("ecol", [128, 2])
        scol = sb("scol", [128, 2])
        scol_i = sb("scol_i", [128, 2], I32)
        vb, blk_rows = (q0[:, j * 256:(j + 1) * 256].rearrange("p (a b) -> p a b", a=2) for j in range(2))
        rowf, same = (q0[0:1, 512 + j * 256:768 + j * 256] for j in range(2))
        rowi = sb("rowi", [1, 256], I32)
        blk_idx = sb("blk_idx", [128, NBLK], I32)

        w_in_f = w_in[:, :, :].rearrange("p a b -> p (a b)")
        wqk_f = wqk[:, :, :, :].rearrange("p a b c -> p (a b c)")
        w_tok_f = w_tok[:, :, :].rearrange("p a b -> p (a b)")
        moe_w = [w_in_f[:, q * 768:(q + 1) * 768] for q in range(3)] + [w_tok_f[:, 0:768]]
        moe_w += [q1[:, q * 768:(q + 1) * 768] for q in range(2)]
        xg = [wqk_f[:, q * D:(q + 1) * D] for q in range(UNROLL)]
        xgT = [wqk_f[:, (6 + q) * D:(7 + q) * D].rearrange("p (a b) -> p a b", a=2) for q in range(2)]
        ys = [q0[:, 1008 + q * D:1008 + (q + 1) * D] for q in range(3)]
        sg, hb = ([w_tok_f[:, 768 + (2 * j + q) * 128:896 + (2 * j + q) * 128] for q in range(2)] for j in range(2))
        icol = [sb(f"icol{q}", [128, 1], I32) for q in range(UNROLL)]
        cg = [r[:, 0:TOPK * D].rearrange("p (k n) -> p k n", k=TOPK) for r in (w_in_f, q1)]
        acc = [wqk_f[:, u * D:(u + 1) * D] for u in range(2)]
        sh_s = [q0[:, 0:512], wqk_f[:, 512:1024]]
        wk_t, yrow_t = (w_tok_f[:, 1280 + j * 128:1280 + j * 128 + (FULL + 1) * TOPK].rearrange("p (t k) -> p t k", k=TOPK)
                        for j in range(2))

        bank = [ctx.enter_context(nc.psum_tensor(f"bank{i}", [128, 512], F32)) for i in range(8)]

        S = {}
        for name in ("weights", "posrow", "table_zero", "table_cleared", "setup",
                     "embedded", "h_ready", "h_stats", "pool_step", "norms_ready",
                     "xn_ready", "x0_ready", "x0b_ready", "hb_out", "xnT_done", "xT_ready", "qk_done", "gate_done",
                     "v_done", "qk_read", "gate_read", "qm0_ready", "qm1_ready", "scores_done", "mask_done",
                     "v_ready", "av_done", "head_sum", "cen_ready", "head_sq", "gvar_ready",
                     "grs_step", "grs_ready", "gn_ready", "gnT_done", "gx_ready", "gh_ready", "wo_done", "x1_ready",
                     "x1_stats", "x1_moments", "hx_ready", "rs2_step", "rs2_ready",
                     "x2_ready", "x2T_done", "x2T_ready", "in_done", "su_ready", "hid_ready", "mlp_done",
                     "h1_ready", "h1_stats", "h1_moments", "rs3_step", "rs3_ready",
                     "xf_ready", "xfT_done", "xfT_ready", "xf_kept", "logits_done", "sig_ready",
                     "choice_step", "fill_step", "h_stored", "wk_stored", "yrow_stored", "wk_loaded", "yrow_loaded",
                     "gmax_ready", "top_ready", "masked_ready", "etop_ready", "sel_ready", "pos_done",
                     "slot_step", "slots_ready",
                     "count_done", "table_step", "blocks_ready", "vb_ready", "row_done", "rows_ready",
                     "block_rows", "block_rows_turned", "idx_ready",
                     "icol_first", "icol_ready", "xgT_done", "xgT_ready", "gu_done", "sg_ready",
                     "hb_ready", "y_done", "ys_ready", "sh_done", "sh_silu", "sh_ready", "sd_done", "acc_ready",
                     "ci_ready", "yrow_step", "yrow_ready", "combined", "acc_step"):
            S[name] = sem(name)
        pat_loaded = [sem(f"pat_loaded{u}") for u in range(PATS)]
        xf_stored = sem("xf_stored")
        indices_ready = [sem(f"indices_ready{u}") for u in range(2)]
        scattered = [sem(f"scattered{u}") for u in range(2)]
        w_loaded = [sem(f"w_loaded{q}") for q in range(UNROLL)]
        gathered = [sem(f"gathered{q}") for q in range(UNROLL)]
        y_stored = [sem(f"y_stored{q}") for q in range(3)]
        h_loaded = [sem(f"h_loaded{u}") for u in range(2)]
        cg_loaded = [sem(f"cg_loaded{u}") for u in range(2)]
        out_stored = [sem(f"out_stored{u}") for u in range(2)]

        def col(name, j=0, n=128):
            return vec[0:n, VEC[name] + j:VEC[name] + j + 1]

        def row(name):
            return rows[:, ROWS.index(name), :]

        def bc(ap, axis, n):
            return ap.unsqueeze(axis).to_broadcast([*ap.shape[:axis], n, *ap.shape[axis:]])

        consts = [(ident[:, :], a["c_ident"]), (vec[:, :], a["c_vec"]), (hmask[:, :], a["c_hmask"]),
                  (tri[:, :], a["c_tri"]), (decay[:, :, :].rearrange("p a b -> p (a b)"), a["c_decay"]),
                  (io64[:, :], a["c_io64"].partition_broadcast(TP)), (ebase[:, :], a["c_ebase"].partition_broadcast(TP)),
                  (bcol[:, :], a["c_bcol"]), (tid[:, :], a["c_tid"]),
                  (gbias[:, :], a["gate_bias"].partition_broadcast(TP)),
                  (row("bv"), a["bv"].partition_broadcast(TP)), (row("bo"), a["bo"].partition_broadcast(TP)),
                  (row("b_out"), a["b_out"].partition_broadcast(TP))]
        kpn = "(k p) n -> p k n"
        weights = [(wqk[:, :, j, :], a[n].rearrange(kpn, p=128)) for j, n in enumerate(("wq", "wk", "wg", "wv"))]
        weights += [(wo[:, :, :], a["wo"].rearrange(kpn, p=128)), (w_in[:, :, :], a["w_in"].rearrange(kpn, p=128)),
                    (w_out[:, 0:NM - 1, :], a["w_out"][0:HM * (NM - 1), :].rearrange(kpn, p=HM)),
                    (w_out[0:MS[-1], NM - 1, :], a["w_out"][HM * (NM - 1):HID, :]),
                    (sgu[:, :, 0, :], a["sgT"].rearrange(kpn, p=128)), (sgu[:, :, 1, :], a["suT"].rearrange(kpn, p=128)),
                    (sdw[:, :, :], a["sdT"].rearrange(kpn, p=128)), (gw[:, :, :], a["gateT"].rearrange(kpn, p=128))]

        def settle(eng):
            eng.wait_ge(S["setup"], 4)

        def pairs(eng, lo, hi, step):
            with eng.Fori(lo, hi) as i:
                for u in range(2):
                    step(2 * i + u, u, i)

        def all_tiles(eng, step):
            step(0, 0, 0)
            step(1, 1, 0)
            pairs(eng, 1, NPAIR, step)

        def has(s, k):
            return not isinstance(s, int) or 0 <= s + k < NPAIR

        def tower(eng, step, lo=2, end=NPAIR - 1, hi=NPAIR + 2):
            for s in range(0, lo):
                step(s)
            with eng.Fori(lo, end) as s:
                step(s)
            for s in range(end, hi):
                step(s)

        def skewed(eng, step, before_last, before_loop=lambda: None):
            for s in range(-2, 4):
                step(s, s % 2)
            before_loop()
            pairs(eng, 2, NPAIR - 1, lambda t, u, n: step(t, u))
            for s in range(NT - 2, NT + 1):
                step(s, s % 2)
            before_last()
            step(NT + 1, (NT + 1) % 2)

        block = ctx.enter_context(nc.Block())

        @block.sync
        def _(sp):
            sp.dma_start(w_tok[:, :, :], a["w_tok"].rearrange(kpn, p=128)).then_inc(S["posrow"], 16)
            sp.dma_start(pos[:, :], a["b_tok"].partition_broadcast(TP)).then_inc(S["posrow"], 16)

            def load_patches(t, u, n):
                if later(t, PATS):
                    sp.wait_ge(S["embedded"], t - PATS + 1)
                sp.dma_start(pat[u].rearrange("p k t -> p (k t)"),
                             a["patches"][bass.ds(t, 1), :, :].rearrange("a p n -> p (a n)")).then_inc(pat_loaded[u], 16)

            for u in range(PATS):
                load_patches(u, u, 0)
            sp.wait_ge(S["posrow"], 32)
            for s in range(PER):
                sp.dma_start(pos[s * SEQ:s * SEQ + 1, :], a["cls"]).then_inc(S["posrow"], 16)
            with sp.Fori(1, NT // PATS) as i:
                for u in range(PATS):
                    load_patches(PATS * i + u, u, i)
            for t in range(NT // PATS * PATS, NT):
                load_patches(t, t % PATS, t // PATS)
            sp.wait_ge(S["table_zero"], 1)
            sp.dma_start(slot_token.rearrange("(p n) a -> p (n a)", p=128), tab_zero).then_inc(S["table_cleared"], 16)

            def pair_rows(a_, q):
                return a_[bass.ds(q * 2 * TP, 2 * TP), :].rearrange("(a p) n -> p a n", a=2)
            with sp.Fori(0, NPAIR) as q:
                sp.wait_ge(S["h1_ready"], q + 1)
                sp.dma_start(pair_rows(h_rows, q), h[:, bass.ds(2 * q, 2), :]).then_inc(S["h_stored"], 16)
                sp.wait_ge(S["xf_ready"], q + 1)
                sp.dma_start(pair_rows(x_rows, q), xf).then_inc(xf_stored, 16)
            sp.wait_ge(S["choice_step"], CHOICE_STEPS * NPAIR)
            sp.dma_start(wk_rows.rearrange("(t p) k -> p t k", p=TP), wk[:, :, :]).then_inc(S["wk_stored"], 16)
            sp.wait_ge(S["rows_ready"], 1)

            def load_w(i, q):
                if later(i, 1):
                    sp.wait_ge(S["y_done"], UNROLL * (i - 1) + q + 1)
                e = sp.value_load(rowi[0:1, bass.ds(LANE * q + i, 1)], min_val=0, max_val=2 * NE - 1)
                sp.dma_start(moe_w[q][:, :], a["moe"][bass.ds(e % NE, 1), :, :].rearrange("a p n -> p (a n)"),
                             cond=(e < NE) if later(i, 1) else None).then_inc(w_loaded[q], 16)

            for q in range(UNROLL):
                load_w(0, q)

            def store_and_load(lo, hi):
                with sp.Fori(lo, hi) as i:
                    for q in range(UNROLL):
                        load_w(i + 1, q)

            def load_tiled(dst, src, name):
                sp.dma_start(dst[:, 0:FULL, :], src[0:FULL * 128, :].rearrange("(t p) k -> p t k", p=128)).then_inc(S[name], 16)
                sp.dma_start(dst[0:REST, FULL, :], src[FULL * 128:NREAL, :]).then_inc(S[name], 16)
            most = -(-(TURNS * NT + 4) // UNROLL) + 1
            store_and_load(0, most)
            sp.wait_ge(S["yrow_ready"], NT)
            sp.dma_start(yrow_rows.rearrange("(t p) k -> p t k", p=TP), yrow[:, :, :]).then_inc(S["yrow_stored"], 16)
            sp.wait_ge(S["wk_stored"], 16)
            load_tiled(wk_t, wk_rows, "wk_loaded")
            store_and_load(most, most + 1)
            sp.wait_ge(S["yrow_stored"], 16)
            load_tiled(yrow_t, yrow_rows, "yrow_loaded")
            store_and_load(most + 1, LANE - 1)
            sp.wait_ge(S["h_stored"], 16 * NPAIR)
            sp.wait_ge(S["y_done"], NBLK)

            def load_h(t, u, n, rows_=128):
                if later(t, 2):
                    sp.wait_ge(out_stored[u], 16 * n)
                sp.dma_start(acc[u][0:rows_, :], h_rows[bass.ds(t * 128, rows_), :]).then_inc(h_loaded[u], 16)

            def store_out(t, u, n, rows_=128):
                sp.wait_ge(S["combined"], t + 1)
                sp.dma_start(out[bass.ds(t * 128, rows_), :], acc[u][0:rows_, :]).then_inc(out_stored[u], 16)
            load_h(0, 0, 0)
            load_h(1, 1, 0)

            def turn(t, u, n):
                store_out(t, u, n)
                load_h(t + 2, u, n + 1)
            pairs(sp, 0, FULL // 2 - 1, turn)
            store_out(FULL - 2, 0, 0)
            load_h(FULL, 0, FULL // 2, REST)
            store_out(FULL - 1, 1, 0)
            store_out(FULL, 0, 0, REST)
            for u in range(2):
                sp.wait_ge(out_stored[u], 16 * (FULL // 2 + 1 - u))

        @block.gpsimd
        def _(pool):
            pool.memset(half[:, :], -0.5).then_inc(S["setup"], 1)
            pool.memset(selsum[:, 0, :], 0.0).then_inc(S["setup"], 1)
            pool.memset(eps[:, :], EPS)
            pool.memset(onesb[:, :], 1.0).then_inc(S["setup"], 1)
            pool.memset(ones64[:, :], 1.0).then_inc(S["setup"], 1)
            pool.memset(tab_zero, 0.0).then_inc(S["table_zero"], 1)

            chain = [0]

            def do(ins):
                ins.then_inc(S["pool_step"], 1)
                chain[0] += 1
                pool.wait_ge(S["pool_step"], chain[0])

            def first_norms(lo, hi):
                mean, r, both, t0, t1, var, t2 = (rs[:, j, lo:hi] for j in (MEAN, RSTD, BOTH, 2, 3, 4, 5))
                s6 = st[:, lo:hi, :]
                pool.tensor_tensor(t0, s6[:, :, 1], s6[:, :, 4], ALU.add)
                pool.tensor_tensor(t2, s6[:, :, 2], s6[:, :, 5], ALU.add)
                do(pool.tensor_tensor(t1, s6[:, :, 1], s6[:, :, 4], ALU.subtract))
                pool.tensor_scalar(mean, t0, 0.5, None, ALU.mult)
                do(pool.tensor_tensor(var, t1, t1, ALU.mult))
                do(pool.tensor_scalar(t0, var, D / 4.0, None, ALU.mult))
                do(pool.tensor_tensor(t1, t0, t2, ALU.add))
                do(pool.tensor_scalar(var, t1, 1.0 / D, None, ALU.mult))
                do(pool.tensor_scalar(t1, var, EPS, None, ALU.add))
                do(pool.tensor_tensor(r, t1, half[:, lo:hi], ALU.pow))
                do(pool.tensor_tensor(t0, r, r, ALU.mult))
                do(pool.tensor_tensor(t1, var, t0, ALU.mult))
                do(pool.tensor_scalar(t0, t1, EPS, None, ALU.add))
                do(pool.tensor_tensor(t2, t0, half[:, lo:hi], ALU.pow))
                pool.tensor_tensor(both, t2, r, ALU.mult).then_inc(S["norms_ready"], 1)

            pool.wait_ge(S["setup"], 4)
            pool.wait_ge(S["h_stats"], FIRST)
            first_norms(0, FIRST)
            pool.wait_ge(S["h_stats"], NT)
            first_norms(FIRST, NT)

            pool.wait_ge(S["weights"], 16 * (len(weights) + len(consts)))
            pool.wait_ge(S["table_cleared"], 16)

            def mask_queries(t, u):
                pool.wait_ge(S["qk_read"], t + 1)
                if later(t, 2):
                    pool.wait_ge(S["scores_done"], 4 * (t - 1))
                pool.tensor_tensor(qm[u][:, 8:16, :], bc(qT[u][:, 1, :], 1, 8), bc(hmask[:, :], 2, TP),
                                   ALU.mult).then_inc(S["qm1_ready"], 1)

            def residual_bias(t, u):
                settle(pool)
                pool.wait_ge(S["x0_ready"], t + 1)
                pool.tensor_tensor(x[:, t, :], x[:, t, :], row("bo"), ALU.add).then_inc(S["x0b_ready"], 1)
                settle(pool)
                pool.wait_ge(S["xn_ready"], t + 1)
                pool.tensor_tensor(h[:, t, :], h[:, t, :], row("b_out"), ALU.add).then_inc(S["hb_out"], 1)

            def head_factors(t, u):
                settle(pool)
                pool.wait_ge(S["gvar_ready"], t + 1)
                pool.tensor_tensor(gvar[:, t, :], grs[:, t, :], half[:, 0:NH], ALU.pow).then_inc(S["grs_ready"], 1)

            def stage2(s, u):
                loop = not isinstance(s, int)
                if loop or 0 <= s + 1 < NT:
                    mask_queries(s + 1, 1 - u)
                if loop or s + 2 < NT:
                    residual_bias(s + 2, u)
                if loop or 0 <= s - 2 < NT:
                    head_factors(s - 2, u)

            def factors(mv, rstd, i, moments, step, ready):
                pool.wait_ge(S[moments], i + 1)
                pool.tensor_tensor(rstd[:, 0, :], mv[:, :, 1], eps[:, :], ALU.add).then_inc(S[step], 1)
                pool.wait_ge(S[step], i + 1)
                pool.tensor_tensor(rstd[:, 1, :], rstd[:, 0, :], half[:, 0:2], ALU.pow).then_inc(S[ready], 1)

            def scatter(n, u, first=0, end=TOPK):
                if first == 0:
                    scatter_set_up(n, u)
                n_rows = LAST if isinstance(n, int) and 2 * n + u == NT - 1 else TP
                for k in range(first, end):
                    pool.indirect_dma_start(slot_token, bass.IndirectOffsetOnAxis(ap=slc[u][0:n_rows, k:k + 1], axis=0),
                                            tic[u][0:n_rows, :], None).then_inc(scattered[u], 16)

            def scatter_set_up(n, u):
                if later(n, 1):
                    pool.wait_ge(scattered[u], 16 * TOPK * n)
                pool.wait_ge(S["slots_ready"], n + 1)
                pool.tensor_copy(slc[u][0:TP, :], slot[:, 2 * n + u, :])
                pool.tensor_copy(tic[u][:, :], tid[:, bass.ds(2 * n + u, 1)]).then_inc(indices_ready[u], 1)
                settle(pool)
                pool.wait_ge(indices_ready[u], n + 1)

            def stages35(s):
                if has(s, -1):
                    factors(mv_h, rstd_h, s - 1, "h1_moments", "rs3_step", "rs3_ready")
                if has(s, -4) and not (isinstance(s, int) and s >= NPAIR):
                    scatter(s - 4, 1, SPLIT)
                if has(s, 1):
                    factors(mv_x, rstd_x, s + 1, "x1_moments", "rs2_step", "rs2_ready")
                if has(s, -3):
                    scatter(s - 3, 0)
                    scatter(s - 3, 1, 0, TOPK if isinstance(s, int) and s >= NPAIR - 1 else SPLIT)
            skewed(pool, stage2, lambda: stages35(-1))
            pool.wait_ge(S["grs_ready"], NT)
            tower(pool, stages35, lo=4, hi=NPAIR + 4)

            pool.wait_ge(S["blocks_ready"], 1)
            pool.wait_ge(S["mlp_done"], NPAIR)
            for u in range(2):
                pool.wait_ge(scattered[u], 16 * TOPK * NPAIR)
            for j in range(2):
                pool.indirect_dma_start(blk_rows[:, j, :], None, slot_token.rearrange("(b c) a -> b (c a)", c=128),
                                        bass.IndirectOffsetOnAxis(ap=scol_i[:, j:j + 1], axis=0)).then_inc(S["block_rows"], 16)

            pool.wait_ge(S["idx_ready"], 1)
            pool.wait_ge(xf_stored, 16 * NPAIR)

            def gather(b, q, n):
                if later(b, UNROLL):
                    pool.wait_ge(gathered[q], 16 * n)
                    pool.wait_ge(S["xgT_done"], b - UNROLL + 1)
                first = not later(b, UNROLL)
                pool.tensor_copy(icol[q][:, :], blk_idx[:, bass.ds(LANE * q + n, 1)]).then_inc(S["icol_first" if first else "icol_ready"], 1)
                if first:
                    pool.wait_ge(S["icol_first"], b + 1)
                else:
                    settle(pool)
                    pool.wait_ge(S["icol_ready"], b - UNROLL + 1)
                pool.indirect_dma_start(xg[q][:, :], None, x_rows, bass.IndirectOffsetOnAxis(ap=icol[q][:, 0:1], axis=0)
                                        ).then_inc(gathered[q], 16)
            for q in range(UNROLL):
                gather(q, q, 0)
            with pool.Fori(1, NBLK // UNROLL) as i:
                for q in range(UNROLL):
                    gather(UNROLL * i + q, q, i)

            for q in range(3):
                pool.wait_ge(y_stored[q], 16 * NBLK // 3)
            pool.wait_ge(S["yrow_loaded"], 32)

            def collect(t, u, n=0, n_rows=128):
                if later(t, 2):
                    pool.wait_ge(cg_loaded[u], 16 * TOPK * n)
                    pool.wait_ge(S["combined"], t - 1)
                pool.wait_ge(S["yrow_ready"], t + 1)
                pool.tensor_copy(slc[u][0:n_rows, :], yrow_t[0:n_rows, t, :]).then_inc(S["ci_ready"], 1)
                settle(pool)
                pool.wait_ge(S["ci_ready"], t + 1)
                for k in range(TOPK):
                    pool.indirect_dma_start(cg[u][0:n_rows, k, :], None, y_rows,
                                            bass.IndirectOffsetOnAxis(ap=slc[u][0:n_rows, k:k + 1], axis=0)).then_inc(cg_loaded[u], 16)
            collect(0, 0)
            collect(1, 1)
            pairs(pool, 1, FULL // 2, collect)
            collect(FULL, 0, FULL // 2, REST)

        @block.scalar
        def _(act):
            for dst, src in consts + weights:
                act.dma_start(dst, src).then_inc(S["weights"], 16)
            act.wait_ge(S["weights"], 16 * (len(weights) + len(consts)))

            def turned(t, u):
                act.wait_ge(S["xnT_done"], t + 1)
                if later(t, 1):
                    act.wait_ge(S["v_done"], t)
                for k in range(2):
                    ins = act.activation(xT[:, k, 0:TP], bank[3][:, k * TP:(k + 1) * TP], ACT.Identity,
                                         bias=col("n1b", k), scale=col("n1w", k))
                ins.then_inc(S["xT_ready"], 1)

            def projected(t, u):
                act.wait_ge(S["qk_done"], t + 1)
                if later(t, 2):
                    act.wait_ge(S["qm0_ready"], t - 1)
                    act.wait_ge(S["qm1_ready"], t - 1)
                    act.wait_ge(S["scores_done"], 4 * (t - 1))
                for k in range(2):
                    act.activation(qT[u][:, k, :], bank[5][:, k * TP:(k + 1) * TP], ACT.Identity, bias=col("bq", k))
                for k in range(2):
                    ins = act.activation(kT[u][:, k, :], bank[5][:, (2 + k) * TP:(3 + k) * TP], ACT.Identity, bias=col("bk", k))
                ins.then_inc(S["qk_read"], 1)
                act.wait_ge(S["gate_done"], t + 1)
                for k in range(2):
                    ins = act.activation(gateT[:, k, bass.ds(t * TP, TP)], bank[4][:, k * TP:(k + 1) * TP], ACT.Silu, bias=col("bg", k))
                ins.then_inc(S["gate_read"], 1)

            def stage2(s, u):
                loop = not isinstance(s, int)
                if loop or 0 <= s + 1 < NT:
                    projected(s + 1, 1 - u)
                if loop or s + 2 < NT:
                    turned(s + 2, u)

            def turned_pair(dst, src, scale, bias):
                for k in range(2):
                    ins = act.activation(dst[:, k, :], src[:, k * 2 * TP:(k + 1) * 2 * TP], ACT.Identity,
                                         bias=col(bias, k), scale=col(scale, k))
                return ins

            def heads_turned(p):
                act.wait_ge(S["gnT_done"], p + 1)
                if later(p, 1):
                    act.wait_ge(S["gh_ready"], p)
                turned_pair(gx, bank[5], "gnw", "gnb").then_inc(S["gx_ready"], 1)

            def x2_turned(p):
                act.wait_ge(S["x2T_done"], p + 1)
                if later(p, 1):
                    act.wait_ge(S["in_done"], NM * p)
                turned_pair(xT, bank[5], "n2w", "n2b").then_inc(S["x2T_ready"], 1)

            def hidden(i, j):
                m = MS[j]
                act.wait_ge(S["in_done"], NM * i + j + 1)
                if later(i, 1) or j >= 2:
                    act.wait_ge(S["hid_ready"], NM * i + j - 1)
                act.activation(su[j % 2][0:m, :], bank[j % 3][0:m, 0:2 * TP], ACT.Silu,
                               bias=col("b_u", j, m)).then_inc(S["su_ready"], 1)

            def xf_turned(q):
                act.wait_ge(S["xfT_done"], q + 1)
                if later(q, 1):
                    act.wait_ge(S["logits_done"], q)
                act.activation(xfT.rearrange("p a b -> p (a b)"), bank[7][:, 0:4 * TP], ACT.Copy).then_inc(S["xfT_ready"], 1)
                act.activation(gateT[:, :, bass.ds(q * 2 * TP, 2 * TP)], bank[7][:, 0:4 * TP].rearrange("p (k t) -> p k t", k=2),
                               ACT.Copy).then_inc(S["xf_kept"], 1)

            def scored(q):
                act.wait_ge(S["logits_done"], q + 1)
                if later(q, 1):
                    act.wait_ge(S["choice_step"], CHOICE_STEPS * (q - 1) + 1)
                act.activation(sig[:, :, :].rearrange("p a b -> p (a b)"), bank[4][0:TP, 0:2 * NE], ACT.Sigmoid).then_inc(S["sig_ready"], 1)

            def stages35(s):
                if has(s, 0):
                    hidden(s, 0)
                if has(s, 1):
                    heads_turned(s + 1)
                if has(s, 0):
                    hidden(s, 1)
                    hidden(s, 2)
                if has(s, -1):
                    xf_turned(s - 1)
                if has(s, 0):
                    for j in range(3, NM):
                        hidden(s, j)
                if has(s, 1):
                    x2_turned(s + 1)
                if has(s, -1):
                    scored(s - 1)
            def start():
                act.wait_ge(S["scores_done"], 4 * NT)
                stages35(-1)
            skewed(act, stage2, start)
            tower(act, stages35, hi=NPAIR + 1)

            def rows_turned(b, p):
                act.wait_ge(S["xgT_done"], b + 1)
                if later(b, 2):
                    act.wait_ge(S["gu_done"], b - 1)
                act.activation(xgT[p][:, :, :].rearrange("p a b -> p (a b)"), bank[p][:, 0:256], ACT.Copy).then_inc(S["xgT_ready"], 1)

            def gate_silu(b, p):
                act.wait_ge(S["gu_done"], b + 1)
                if later(b, 2):
                    act.wait_ge(S["hb_ready"], b - 1)
                act.activation(sg[p][:, :], bank[2 + p][:, 0:128], ACT.Silu).then_inc(S["sg_ready"], 1)

            def store_y(i, q):
                act.wait_ge(S["ys_ready"], UNROLL * i + q + 1)
                act.dma_start(y_rows[bass.ds((LANE * q + i) * 128, 128), :], ys[q % 3]).then_inc(y_stored[q % 3], 16)

            def blocks(i, first=0, ahead=UNROLL):
                for q in range(UNROLL):
                    gate_silu(UNROLL * i + q, q % 2)
                    if q < ahead:
                        rows_turned(UNROLL * i + q + 2, q % 2)
                    if q >= first:
                        store_y(i if q >= 2 else i - 1, (q - 2) % UNROLL)
            rows_turned(0, 0)
            rows_turned(1, 1)
            blocks(0, first=2)
            with act.Fori(1, LANE - 1) as i:
                blocks(i)
            blocks(LANE - 1, ahead=UNROLL - 2)
            store_y(LANE - 1, UNROLL - 2)
            store_y(LANE - 1, UNROLL - 1)

            def shared_silu(i):
                act.wait_ge(S["sh_done"], i + 1)
                if later(i, 1):
                    act.wait_ge(S["sh_ready"], i)
                act.activation(sh_s[0], bank[0][:, :], ACT.Silu).then_inc(S["sh_silu"], 1)
            shared_silu(0)
            with act.Fori(1, FULL // 2 + 1) as i:
                shared_silu(i)

        @block.tensor
        def _(pe):
            def mm(out_, lhsT, rhs, start, stop):
                return pe.matmul(out_, lhsT, rhs, start=start, stop=stop)

            pe.wait_ge(S["posrow"], 32)

            def embed(t, u, n):
                pe.wait_ge(pat_loaded[u], 16 * (n + 1))
                if later(t, 2):
                    pe.wait_ge(S["h_ready"], t - 1)
                for k in range(KP):
                    ins = mm(bank[u % 2][0:TP, 0:D], pat[u][:, k, :], w_tok[:, k, :], k == 0, k == KP - 1)
                ins.then_inc(S["embedded"], 1)
            for t in range(PATS):
                embed(t, t, 0)
            with pe.Fori(1, NT // PATS) as i:
                for u in range(PATS):
                    embed(PATS * i + u, u, i)
            for t in range(NT // PATS * PATS, NT):
                embed(t, t % PATS, t // PATS)

            pe.wait_ge(S["weights"], 16 * (len(weights) + len(consts)))

            def turn_norm(t, u):
                pe.wait_ge(S["xn_ready"], t + 1)
                if later(t, 1):
                    pe.wait_ge(S["xT_ready"], t)
                for k in range(2):
                    ins = pe.transpose(bank[3][:, k * TP:(k + 1) * TP], xn[u][:, k * 128:(k + 1) * 128], ident[0:TP, 0:TP])
                ins.then_inc(S["xnT_done"], 1)

            def project(t, u):
                pe.wait_ge(S["xT_ready"], t + 1)
                if later(t, 1):
                    pe.wait_ge(S["qk_read"], t)
                for j in range(2):
                    for m in range(2):
                        for k in range(2):
                            ins = mm(bank[5][:, (2 * j + m) * TP:(2 * j + m + 1) * TP], wqk[:, k, j, m * 128:(m + 1) * 128],
                                     xT[:, k, 0:TP], k == 0, k == 1)
                ins.then_inc(S["qk_done"], 1)
                if later(t, 1):
                    pe.wait_ge(S["gate_read"], t)
                for m in range(2):
                    for k in range(2):
                        ins = mm(bank[4][:, m * TP:(m + 1) * TP], wqk[:, k, 2, m * 128:(m + 1) * 128], xT[:, k, 0:TP], k == 0, k == 1)
                ins.then_inc(S["gate_done"], 1)
                if later(t, 1):
                    pe.wait_ge(S["v_ready"], t)
                for k in range(2):
                    ins = mm(bank[6][0:TP, 0:D], xT[:, k, 0:TP], wqk[:, k, 3, :], k == 0, k == 1)
                ins.then_inc(S["v_done"], 1)

            def scores(t, u, j):
                if j == 0:
                    pe.wait_ge(S["qm0_ready"], t + 1)
                    pe.wait_ge(S["qm1_ready"], t + 1)
                    if later(t, 1):
                        pe.wait_ge(S["mask_done"], 4 * t)
                if j == 3:
                    pe.wait_ge(S["mask_done"], 4 * t + 1)
                mm(bank[j % 3][0:TP, 0:4 * TP], kT[u][:, j // 2, :], qm[u][:, 4 * j:4 * j + 4, :].rearrange("p a b -> p (a b)"),
                   True, True).then_inc(S["scores_done"], 1)

            def retain(t, u, j):
                pe.wait_ge(S["mask_done"], 4 * t + j + 1)
                if j == 0:
                    pe.wait_ge(S["v_ready"], t + 1)
                    if later(t, 1):
                        pe.wait_ge(S["cen_ready"], t)
                for n in range(4 * j, 4 * j + 4):
                    ins = mm(bank[7][0:TP, n * HD:(n + 1) * HD], ss[u][:, n, :], vv[u][:, n * HD:(n + 1) * HD], True, True)
                if j == 3:
                    ins.then_inc(S["av_done"], 1)

            def stage2(s, u):
                loop = not isinstance(s, int)
                if loop or 0 <= s + 1 < NT:
                    project(s + 1, 1 - u)
                if loop or s + 2 < NT:
                    turn_norm(s + 2, u)
                for j in range(4):
                    if loop or 0 <= s < NT:
                        scores(s, u, j)
                    if loop or 0 <= s - 1 < NT:
                        retain(s - 1, 1 - u, j)


            def turn(dst, src):
                for k in range(2):
                    for u in range(2):
                        at = (2 * k + u) * TP
                        ins = pe.transpose(dst[:, at:at + TP], src[:, u, k * 128:(k + 1) * 128], ident[0:TP, 0:TP])
                return ins

            def turn_heads(p):
                pe.wait_ge(S["gn_ready"], p + 1)
                if later(p, 1):
                    pe.wait_ge(S["x2T_ready"], p)
                turn(bank[5], gn).then_inc(S["gnT_done"], 1)

            def attn_out(p):
                pe.wait_ge(S["gh_ready"], p + 1)
                if later(p, 1):
                    pe.wait_ge(S["x1_ready"], p)
                for u in range(2):
                    for k in range(2):
                        ins = mm(bank[6][0:TP, u * D:(u + 1) * D], gh[:, k, u * TP:(u + 1) * TP], wo[:, k, :], k == 0, k == 1)
                ins.then_inc(S["wo_done"], 1)

            def turn_x2(p):
                pe.wait_ge(S["x2_ready"], p + 1)
                turn(bank[5], x2).then_inc(S["x2T_done"], 1)

            def mlp_in(i, j):
                m = MS[j]
                if j == 0:
                    pe.wait_ge(S["x2T_ready"], i + 1)
                if later(i, 1) or j >= 3:
                    pe.wait_ge(S["hid_ready"], NM * i + j - 2)
                for s in range(2):
                    for k in range(2):
                        at = s * HID + j * HM
                        ins = mm(bank[j % 3][0:m, s * 2 * TP:(s + 1) * 2 * TP], w_in[:, k, at:at + m], xT[:, k, :], k == 0, k == 1)
                ins.then_inc(S["in_done"], 1)

            def mlp_out(i, u):
                if u == 0 and later(i, 1):
                    pe.wait_ge(S["h1_ready"], i)
                for j, m in enumerate(MS):
                    if u == 0:
                        pe.wait_ge(S["hid_ready"], NM * i + j + 1)
                    ins = mm(bank[3][0:TP, u * D:(u + 1) * D], hT[0:m, j, u * TP:(u + 1) * TP], w_out[0:m, j, :], j == 0, j == NM - 1)
                if u == 1:
                    ins.then_inc(S["mlp_done"], 1)

            def turn_xf(q):
                pe.wait_ge(S["xf_ready"], q + 1)
                if later(q, 2):
                    pe.wait_ge(S["slot_step"], SLOT_STEPS * (q - 2) + 1)
                turn(bank[7], xf).then_inc(S["xfT_done"], 1)

            def route(q):
                if later(q, 1):
                    pe.wait_ge(S["sig_ready"], q)
                pe.wait_ge(S["xfT_ready"], q + 1)
                for u in range(2):
                    for k in range(2):
                        ins = mm(bank[4][0:TP, u * NE:(u + 1) * NE], xfT[:, k, u * TP:(u + 1) * TP], gw[:, k, :], k == 0, k == 1)
                ins.then_inc(S["logits_done"], 1)

            def place(q):
                pe.wait_ge(S["sel_ready"], q + 1)
                pe.wait_ge(S["xf_kept"], min(q + 2, NPAIR) if isinstance(q, int) else q + 2)
                for u in range(2):
                    at = u * NE
                    mm(bank[7][0:TP, at:at + NE], trib[:, :], sel[:, u, :], True, False)
                    ins = mm(bank[7][0:TP, at:at + NE], onesb[:, 0:TP], selsum[:, 2 * q + u, :], False, True)
                ins.then_inc(S["pos_done"], 1)

            def stages35(s):
                if has(s, 0):
                    mlp_in(s, 0)
                if has(s, -3):
                    place(s - 3)
                if has(s, 1):
                    turn_heads(s + 1)
                if has(s, 0):
                    mlp_in(s, 1)
                    mlp_in(s, 2)
                if has(s, 1):
                    attn_out(s + 1)
                if has(s, -1):
                    turn_xf(s - 1)
                if has(s, 0):
                    for j in range(3, NM):
                        mlp_in(s, j)
                if has(s, -1):
                    route(s - 1)
                if has(s, 0):
                    mlp_out(s, 0)
                if has(s, 1):
                    turn_x2(s + 1)
                if has(s, 0):
                    mlp_out(s, 1)
            def start():
                pe.wait_ge(S["gate_read"], NT)
                pe.wait_ge(S["qk_read"], NT)
                stages35(-1)
            skewed(pe, stage2, start)
            tower(pe, stages35, lo=3, hi=NPAIR + 3)

            pe.wait_ge(S["sel_ready"], NPAIR)
            mm(bank[6][:, 0:NE], onesb[:, :], selsum[:, NT, :], True, True).then_inc(S["count_done"], 1)
            pe.wait_ge(S["vb_ready"], 1)
            for j in range(2):
                ins = mm(bank[7][:, j * 128:(j + 1) * 128], vb[:, j, :], ident[:, :], True, True)
            ins.then_inc(S["row_done"], 1)
            pe.wait_ge(S["block_rows"], 32)
            for j in range(2):
                ins = pe.transpose(bank[6][:, j * 128:(j + 1) * 128], blk_rows[:, j, :], ident[:, :])
            ins.then_inc(S["block_rows_turned"], 1)

            def turn_rows(b, q, p, n):
                pe.wait_ge(gathered[q], 16 * (n + 1))
                if later(b, 2):
                    pe.wait_ge(S["xgT_ready"], b - 1)
                for k in range(2):
                    ins = pe.transpose(bank[p][:, k * 128:(k + 1) * 128], xg[q][:, k * 128:(k + 1) * 128], ident[:, :])
                ins.then_inc(S["xgT_done"], 1)

            def gate_up(b, q, p, n):
                pe.wait_ge(w_loaded[q], 16 * (n + 1))
                pe.wait_ge(S["xgT_ready"], b + 1)
                if later(b, 2):
                    pe.wait_ge(S["hb_ready"], b - 1)
                for s in range(2):
                    for k in range(2):
                        at = k * 256 + s * 128
                        ins = mm(bank[2 + p][:, s * 128:(s + 1) * 128], moe_w[q][:, at:at + 128], xgT[p][:, k, :], k == 0, k == 1)
                ins.then_inc(S["gu_done"], 1)

            def down(b, q, p):
                pe.wait_ge(S["hb_ready"], b + 1)
                if later(b, 2):
                    pe.wait_ge(S["ys_ready"], b - 1)
                mm(bank[6 + p][:, 0:256], hb[p][:, :], moe_w[q][:, 512:768], True, True).then_inc(S["y_done"], 1)

            def stage6(i, q, first=False, ahead=True):
                b, p, m = UNROLL * i + q, q % 2, (q - 1) % UNROLL
                gate_up(b, q, p, i)
                if ahead:
                    turn_rows(b + 2, (q + 2) % UNROLL, p, i + (q + 2) // UNROLL)
                if not first:
                    down(b - 1, m, 1 - p)

            pe.wait_ge(S["idx_ready"], 1)
            turn_rows(0, 0, 0, 0)
            turn_rows(1, 1, 1, 0)
            for q in range(UNROLL):
                stage6(0, q, first=q == 0)
            with pe.Fori(1, NBLK // UNROLL - 1) as i:
                for q in range(UNROLL):
                    stage6(i, q)
            for q in range(UNROLL):
                stage6(NBLK // UNROLL - 1, q, ahead=q < UNROLL - 2)
            down(NBLK - 1, UNROLL - 1, 1)

            pe.wait_ge(S["ys_ready"], NBLK)
            pe.wait_ge(S["xf_kept"], NPAIR)

            def shared_in(i, n=256):
                for s in range(2):
                    if later(i, 1):
                        pe.wait_ge(S["sh_silu" if s == 0 else "sh_ready"], i)
                    for m in range(2):
                        for k in range(2):
                            ins = mm(bank[s][:, m * 256:m * 256 + n], sgu[:, k, s, m * 128:(m + 1) * 128],
                                     gateT[:, k, bass.ds(i * 256, n)], k == 0, k == 1)
                ins.then_inc(S["sh_done"], 1)

            def shared_out(i, tiles=((0, 128), (1, 128))):
                pe.wait_ge(S["sh_ready"], i + 1)
                for u, n in tiles:
                    if later(i, 1):
                        pe.wait_ge(S["acc_ready"], 2 * i + u - 1)
                    for k in range(2):
                        at = k * 256 + u * 128
                        ins = mm(bank[2 + u][0:n, 0:D], sh_s[1][:, at:at + n], sdw[:, k, :], k == 0, k == 1)
                    ins.then_inc(S["sd_done"], 1)
            shared_in(0)
            shared_out(0)
            with pe.Fori(1, FULL // 2) as i:
                shared_in(i)
                shared_out(i)
            shared_in(FULL // 2, REST)
            shared_out(FULL // 2, ((0, REST),))

        @block.vector
        def _(dve):
            dve.wait_ge(S["posrow"], 16 * (2 + PER))

            def embedded(t, u, n=0):
                dve.wait_ge(S["embedded"], t + 1)
                dve.tensor_tensor(h[:, t, :], bank[u][0:TP, 0:D], pos[:, :], ALU.add).then_inc(S["h_ready"], 1)
                dve.wait_ge(S["h_ready"], t + 1)
                dve.bn_stats(st[:, t, :], h[:, t, :]).then_inc(S["h_stats"], 1)
            pairs(dve, 0, NPAIR, embedded)

            dve.wait_ge(S["table_cleared"], 16)
            dve.wait_ge(S["norms_ready"], 1)
            dve.wait_ge(S["weights"], 16 * (len(weights) + len(consts)))
            dve.tensor_copy(trib[:, :], tri[:, :]).then_inc(S["setup"], 1)

            def normed(t, u):
                dve.tensor_scalar(x[:, t, :], h[:, t, :], rs[:, MEAN, bass.ds(t, 1)], rs[:, RSTD, bass.ds(t, 1)],
                                  ALU.subtract, ALU.mult).then_inc(S["x0_ready"], 1)
                if later(t, 2):
                    dve.wait_ge(S["xnT_done"], t - 1)
                dve.tensor_scalar(xn[u], h[:, t, :], rs[:, MEAN, bass.ds(t, 1)], rs[:, BOTH, bass.ds(t, 1)],
                                  ALU.subtract, ALU.mult).then_inc(S["xn_ready"], 1)

            def mask_queries(t, u, n=0):
                dve.wait_ge(S["qk_read"], t + 1)
                if later(t, 2):
                    dve.wait_ge(S["scores_done"], 4 * (t - 1))
                dve.tensor_tensor(qm[u][:, 0:8, :], bc(qT[u][:, 0, :], 1, 8), bc(hmask[:, :], 2, TP),
                                  ALU.mult).then_inc(S["qm0_ready"], 1)

            def decay_scores(t, u):
                if later(t, 2):
                    dve.wait_ge(S["av_done"], t - 1)
                for j in range(4):
                    dve.wait_ge(S["scores_done"], 4 * t + j + 1)
                    dve.tensor_tensor(ss[u][:, 4 * j:4 * j + 4, :], bank[j % 3][0:TP, 0:4 * TP].rearrange("p (a b) -> p a b", a=4),
                                      decay[:, 4 * j:4 * j + 4, :], ALU.mult).then_inc(S["mask_done"], 1)

            def values(t, u):
                dve.wait_ge(S["v_done"], t + 1)
                if later(t, 2):
                    dve.wait_ge(S["av_done"], t - 1)
                dve.tensor_tensor(vv[u][:, :], bank[6][0:TP, 0:D], row("bv"), ALU.add).then_inc(S["v_ready"], 1)

            def centre(t, u):
                heads = bank[7][0:TP, 0:D].rearrange("p (n d) -> p n d", n=NH)
                cen_t = cen[:, t, :].rearrange("p (n d) -> p n d", n=NH)
                dve.wait_ge(S["av_done"], t + 1)
                if later(t, 2):
                    dve.wait_ge(S["cen_ready"], t - 1)
                dve.tensor_reduce(gsum[u][:, :], heads, AX.X, ALU.add).then_inc(S["head_sum"], 1)
                dve.wait_ge(S["head_sum"], t + 1)
                dve.scalar_tensor_tensor(cen_t, bc(gsum[u][:, :], 2, HD), -1.0 / HD, heads, ALU.mult, ALU.add).then_inc(S["cen_ready"], 1)
                dve.wait_ge(S["cen_ready"], t + 1)
                if later(t, 1):
                    dve.wait_ge(S["gvar_ready"], t)
                dve.tensor_tensor(gsq[:, :], cen[:, t, :], cen[:, t, :], ALU.mult).then_inc(S["head_sq"], 1)
                dve.wait_ge(S["head_sq"], t + 1)
                if later(t, 2):
                    dve.wait_ge(S["gvar_ready"], t - 1)
                dve.tensor_reduce(gsum[u][:, :], gsq[:, :].rearrange("p (n d) -> p n d", n=NH), AX.X, ALU.add).then_inc(S["grs_step"], 1)
                dve.wait_ge(S["grs_step"], t + 1)
                dve.tensor_scalar(grs[:, t, :], gsum[u][:, :], 1.0 / HD, EPS, ALU.mult, ALU.add).then_inc(S["gvar_ready"], 1)

            def stage2(s, u):
                loop = not isinstance(s, int)
                if loop or s + 2 < NT:
                    normed(s + 2, u)
                if loop or 0 <= s - 2 < NT:
                    centre(s - 2, u)
                if loop or 0 <= s + 1 < NT:
                    mask_queries(s + 1, 1 - u)
                if loop or 0 <= s < NT:
                    decay_scores(s, u)
                if loop or 0 <= s + 1 < NT:
                    values(s + 1, 1 - u)


            def group_normed(p):
                dve.wait_ge(S["grs_ready"], 2 * p + 2)
                if later(p, 1):
                    dve.wait_ge(S["gnT_done"], p)
                dve.tensor_tensor(gn[:, :, :].rearrange("p a (n d) -> p (a n) d", n=NH),
                                  cen[:, bass.ds(2 * p, 2), :].rearrange("p a (n d) -> p (a n) d", n=NH),
                                  bc(gvar[:, bass.ds(2 * p, 2), :].rearrange("p a n -> p (a n)"), 2, HD), ALU.mult).then_inc(S["gn_ready"], 1)

            def gate_heads(p):
                dve.wait_ge(S["gx_ready"], p + 1)
                if later(p, 1):
                    dve.wait_ge(S["wo_done"], p)
                dve.tensor_tensor(gh, gx, gateT[:, :, bass.ds(2 * p * TP, 2 * TP)], ALU.mult).then_inc(S["gh_ready"], 1)

            def moments(src, st_, mv, p, ready, stats, done):
                settle(dve)
                dve.wait_ge(S[ready], p + 1)
                for u in range(2):
                    ins = dve.bn_stats(st_[:, u, :], src[:, 2 * p + u, :])
                ins.then_inc(S[stats], 1)
                settle(dve)
                dve.wait_ge(S[stats], p + 1)
                for u in range(2):
                    ins = dve.bn_aggr(mv[:, u, :], st_[:, u, :])
                ins.then_inc(S[done], 1)

            def two(a_, p):
                return a_[:, bass.ds(2 * p, 2), :]

            def attended(p):
                dve.wait_ge(S["wo_done"], p + 1)
                dve.tensor_tensor(two(x, p), bank[6][0:TP, :].rearrange("p (a n) -> p a n", a=2), two(x, p), ALU.add).then_inc(S["x1_ready"], 1)
                moments(x, st_x, mv_x, p, "x1_ready", "x1_stats", "x1_moments")
                dve.tensor_tensor(two(h, p), two(h, p), two(x, p), ALU.add).then_inc(S["hx_ready"], 1)

            def normed_by(dst, src, i, mv, rstd, ready):
                for u in range(2):
                    ins = dve.tensor_scalar(dst[:, u, :], src[:, 2 * i + u, :], mv[:, u, 0:1], rstd[:, 1, u:u + 1], ALU.subtract, ALU.mult)
                ins.then_inc(S[ready], 1)

            def x2_normed(p):
                dve.wait_ge(S["rs2_ready"], p + 1)
                if later(p, 1):
                    dve.wait_ge(S["x2T_done"], p)
                normed_by(x2, x, p, mv_x, rstd_x, "x2_ready")

            def hidden(i, j):
                m = MS[j]
                if j == 0 and later(i, 1):
                    dve.wait_ge(S["mlp_done"], i)
                dve.wait_ge(S["su_ready"], NM * i + j + 1)
                dve.scalar_tensor_tensor(hT[0:m, j, :], bank[j % 3][0:m, 2 * TP:4 * TP], col("b_g", j, m),
                                         su[j % 2][0:m, :], ALU.add, ALU.mult).then_inc(S["hid_ready"], 1)

            def mlp_added(q):
                dve.wait_ge(S["mlp_done"], q + 1)
                dve.wait_ge(S["hx_ready"], q + 1)
                dve.tensor_tensor(two(h, q), bank[3][0:TP, :].rearrange("p (a n) -> p a n", a=2), two(h, q), ALU.add).then_inc(S["h1_ready"], 1)
                moments(h, st_h, mv_h, q, "h1_ready", "h1_stats", "h1_moments")

            def last_norm(q):
                dve.wait_ge(S["rs3_ready"], q + 1)
                if later(q, 1):
                    dve.wait_ge(S["xfT_done"], q)
                    dve.wait_ge(xf_stored, 16 * q)
                normed_by(xf, h, q, mv_h, rstd_h, "xf_ready")

            count = {}

            def before_max(name, q, ins):
                ins.then_inc(S[name], 1)
                settle(dve)
                dve.wait_ge(S[name], q + 1)

            def chain(name, total, q, ins):
                ins.then_inc(S[name], 1)
                count[name] = count.get(name, 0) % total + 1
                dve.wait_ge(S[name], total * q + count[name])

            def choose_groups(q):
                def do(ins):
                    chain("choice_step", CHOICE_STEPS, q, ins)
                dve.wait_ge(S["sig_ready"], q + 1)
                do(dve.tensor_tensor(sc[:, :, :], sig[:, :, :], bc(gbias[:, :], 1, 2), ALU.add))
                before_max("gmax_ready", q, dve.tensor_reduce(gmax[:, :, :], sc[:, :, :].rearrange("p a (g e) -> p a g e", g=NG), AX.X, ALU.max))
                for u in range(2):
                    ins = dve.max(top[:, u, :], gmax[:, u, :])
                before_max("top_ready", q, ins)
                for u in range(2):
                    ins = dve.max_index(idx[:, u, :], top[:, u, :], gmax[:, u, :])
                do(ins)
                do(dve.tensor_copy(idf[:, :, :], idx[:, :, :]))
                do(dve.tensor_tensor(geq[:, :, :, :], bc(bc(io64[:, 0:NG], 1, TOPG), 1, 2), bc(idf[:, :, 0:TOPG], 3, NG), ALU.is_equal))
                do(dve.tensor_reduce(gsel[:, :, :], geq[:, :, :, :].rearrange("p a k g -> p a g k"), AX.X, ALU.add))

            def choose_experts(q):
                def do(ins):
                    chain("choice_step", CHOICE_STEPS, q, ins)
                grouped = sc[:, :, :].rearrange("p a (g e) -> p (a g) e", g=NG)
                before_max("masked_ready", q, dve.tensor_tensor(grouped, grouped, bc(gsel[:, :, :].rearrange("p a g -> p (a g)"), 2, EG), ALU.mult))
                for u in range(2):
                    ins = dve.max(etop[:, u, :], sc[:, u, :])
                before_max("etop_ready", q, ins)
                for u in range(2):
                    ins = dve.max_index(idx[:, u, :], etop[:, u, :], sc[:, u, :])
                do(ins)
                do(dve.tensor_copy(idf[:, :, :], idx[:, :, :]))
                dve.tensor_copy(chosen[:, bass.ds(2 * q, 2), :], idf[:, :, 0:TOPK])
                do(dve.tensor_tensor(oh, bc(bc(io64[:, :], 1, TOPK), 1, 2), bc(idf[:, :, 0:TOPK], 3, NE), ALU.is_equal))

            def choice_kept(q):
                def do(ins):
                    chain("choice_step", CHOICE_STEPS, q, ins)
                do(dve.tensor_reduce(smap[:, :, :], oh.rearrange("p a k e -> p a e k"), AX.X, ALU.add))
                if isinstance(q, int) and q == NPAIR - 1:
                    dve.tensor_scalar(wsum[:, 0, 0:1], tid[:, NT - 1:NT], float(NREAL), None, ALU.is_lt).then_inc(S["fill_step"], 1)
                    dve.wait_ge(S["fill_step"], 1)
                    dve.tensor_scalar(smap[:, 1, :], smap[:, 1, :], wsum[:, 0, 0:1], None, ALU.mult).then_inc(S["fill_step"], 1)
                    dve.wait_ge(S["fill_step"], 2)
                dve.tensor_copy(sel[:, :, :], smap[:, :, :])
                do(dve.tensor_tensor(selsum[:, 2 * q + 1, :], selsum[:, 2 * q, :], smap[:, 0, :], ALU.add))
                dve.tensor_tensor(selsum[:, 2 * q + 2, :], selsum[:, 2 * q + 1, :], smap[:, 1, :], ALU.add).then_inc(S["sel_ready"], 1)
                do(dve.tensor_reduce(wsum[:, 0, :], etop[:, :, 0:TOPK], AX.X, ALU.add))
                do(dve.tensor_scalar(wsum[:, 1, :], wsum[:, 0, :], 1e-8, None, ALU.add))
                do(dve.reciprocal(wsum[:, 2, :], wsum[:, 1, :]))
                do(dve.tensor_tensor(wk[:, bass.ds(2 * q, 2), :], etop[:, :, 0:TOPK], bc(wsum[:, 2, :], 2, TOPK), ALU.mult))
                assert count["choice_step"] == CHOICE_STEPS

            def take_slots(q, part):
                def do(ins):
                    chain("slot_step", SLOT_STEPS, q, ins)
                if part == 0:
                    dve.wait_ge(S["pos_done"], q + 1)
                    do(dve.tensor_tensor(smap[:, :, :], bank[7][0:TP, 0:2 * NE].rearrange("p (a e) -> p a e", a=2),
                                         bc(ebase[:, :], 1, 2), ALU.add))
                    do(dve.tensor_tensor(prod, oh, bc(smap[:, :, :], 2, TOPK), ALU.mult))
                else:
                    do(dve.tensor_reduce(slf[:, :, :], prod, AX.X, ALU.add))
                    dve.tensor_copy(slot[:, bass.ds(2 * q, 2), :], slf[:, :, :]).then_inc(S["slots_ready"], 1)
                    assert count["slot_step"] == SLOT_STEPS

            def stages35(s):
                if isinstance(s, int) and s == -1:
                    group_normed(0)
                if has(s, -1):
                    mlp_added(s - 1)
                if has(s, 0):
                    hidden(s, 0)
                if has(s, 1):
                    gate_heads(s + 1)
                if has(s, -1):
                    last_norm(s - 1)
                if has(s, -3):
                    take_slots(s - 3, 0)
                if has(s, 0):
                    hidden(s, 1)
                if has(s, -3):
                    take_slots(s - 3, 1)
                if has(s, 0):
                    hidden(s, 2)
                if has(s, 1):
                    attended(s + 1)
                if has(s, 0):
                    hidden(s, 3)
                    hidden(s, 4)
                if has(s, -2):
                    choose_groups(s - 2)
                if has(s, 0):
                    hidden(s, 5)
                if has(s, 1):
                    x2_normed(s + 1)
                if has(s, 2):
                    group_normed(s + 2)
                if has(s, -2):
                    choose_experts(s - 2)
                    choice_kept(s - 2)
            def start():
                dve.wait_ge(S["x0b_ready"], NT)
                dve.wait_ge(S["hb_out"], NT)
                stages35(-1)
            skewed(dve, stage2, start, lambda: dve.wait_ge(S["norms_ready"], 2))
            tower(dve, stages35, lo=3, end=NPAIR - 2, hi=NPAIR + 3)

            table_steps = [0]

            def do(ins):
                ins.then_inc(S["table_step"], 1)
                table_steps[0] += 1
                dve.wait_ge(S["table_step"], table_steps[0])
            dve.wait_ge(S["count_done"], 1)
            do(dve.tensor_scalar(nbf[:, :], bank[6][:, 0:NE], 127.0, None, ALU.add))
            do(dve.tensor_copy(nbi[:, :], nbf[:, :]))
            do(dve.tensor_scalar(nbi[:, :], nbi[:, :], 7, None, ALU.arith_shift_right))
            do(dve.tensor_copy(nbf[:, :], nbi[:, :]))
            do(dve.tensor_tensor_scan(bend[:, :], ones64[:, :], nbf[:, :], 0.0, ALU.mult, ALU.add))
            do(dve.tensor_tensor(shift[:, :], bend[0:TP, :], nbf[0:TP, :], ALU.subtract))
            do(dve.scalar_tensor_tensor(shift[:, :], shift[:, :], 128.0, ebase[:, :], ALU.mult, ALU.subtract))
            for j in range(2):
                do(dve.tensor_scalar(le[:, j, :], bend[:, :], bcol[:, j:j + 1], None, ALU.is_le))
                do(dve.tensor_tensor(lb[:, j, :], le[:, j, :], bend[:, :], ALU.mult))
            do(dve.tensor_reduce(ecol[:, :], le[:, :, :], AX.X, ALU.add))
            do(dve.tensor_reduce(scol[:, :], lb[:, :, :], AX.X, ALU.max))
            do(dve.tensor_tensor(scol[:, :], bcol[:, :], scol[:, :], ALU.subtract))
            do(dve.scalar_tensor_tensor(scol[:, :], ecol[:, :], float(SLOT_BLOCKS), scol[:, :], ALU.mult, ALU.add))
            do(dve.tensor_scalar(scol[:, :], scol[:, :], float(TAB_BLOCKS - 1), None, ALU.min))
            dve.tensor_copy(scol_i[:, :], scol[:, :]).then_inc(S["blocks_ready"], 1)
            do(dve.tensor_scalar(ecol[:, :], ecol[:, :], float(NE - 1), None, ALU.min))
            for j in range(2):
                ins = dve.tensor_copy(vb[:, j, :], ecol[:, j:j + 1].to_broadcast([128, 128]))
            ins.then_inc(S["vb_ready"], 1)
            dve.wait_ge(S["row_done"], 1)
            do(dve.tensor_copy(rowf, bank[7][0:1, 0:256]))
            do(dve.memset(same[:, 0:1], 0.0))
            do(dve.tensor_tensor(same[:, 1:256], rowf[:, 1:256], rowf[:, 0:255], ALU.is_equal))
            dve.scalar_tensor_tensor(rowi[0:1, :], same, float(NE), rowf, ALU.mult, ALU.add).then_inc(S["rows_ready"], 1)
            dve.wait_ge(S["block_rows_turned"], 1)
            dve.tensor_copy(blk_idx[:, :], bank[6][:, 0:NBLK]).then_inc(S["idx_ready"], 1)

            def result_rows(t, step):
                if step:
                    dve.wait_ge(S["yrow_step"], 3 * t + step)
                if step == 0:
                    ins = dve.tensor_tensor(oh[:, 0], bc(io64[:, :], 1, TOPK), bc(chosen[:, t, :], 2, NE), ALU.is_equal)
                elif step == 1:
                    ins = dve.tensor_tensor(prod[:, 0], oh[:, 0], bc(shift[:, :], 1, TOPK), ALU.mult)
                elif step == 2:
                    ins = dve.tensor_reduce(slf[:, 0, :], prod[:, 0], AX.X, ALU.add)
                else:
                    ins = dve.tensor_tensor(yrow[:, t, :], slf[:, 0, :], slot[:, t, :], ALU.add)
                ins.then_inc(S["yrow_step" if step < 3 else "yrow_ready"], 1)

            def product(b, p):
                dve.wait_ge(S["sg_ready"], b + 1)
                if later(b, 2):
                    dve.wait_ge(S["y_done"], b - 1)
                dve.tensor_tensor(hb[p][:, :], bank[2 + p][:, 128:256], sg[p][:, :], ALU.mult).then_inc(S["hb_ready"], 1)

            def rows_out(b, k, n):
                dve.wait_ge(S["y_done"], b + 1)
                if later(b, 3):
                    dve.wait_ge(y_stored[k % 3], 16 * n)
                dve.tensor_copy(ys[k % 3], bank[6 + k % 2][:, 0:256]).then_inc(S["ys_ready"], 1)

            product(0, 0)
            for b in range(1, 4):
                product(b, b % 2)
                rows_out(b - 1, b - 1, 0)

            def turns(base, n, steps=lambda k: None):
                for k in range(6):
                    product(6 * n + base + k, k % 2)
                    rows_out(6 * n + base + k - 1, (3 + k) % 6, 2 * n + (base + k - 1) // 3)
                    steps(k)
            with dve.Fori(0, NT) as t:
                turns(4, t, lambda k: result_rows(t, k) if k < 4 else None)
            rest, last = 4 + TURNS * NT, (NBLK - 4) % 6
            with dve.Fori(0, (NBLK - rest) // 6) as i:
                turns(rest, i)
            for b in range(NBLK - last, NBLK):
                product(b, b % 2)
                rows_out(b - 1, (b - 1) % 6, (b - 1) // 3)
            rows_out(NBLK - 1, (NBLK - 1) % 6, (NBLK - 1) // 3)

            def shared_product(i):
                dve.wait_ge(S["sh_silu"], i + 1)
                if later(i, 1):
                    dve.wait_ge(S["sd_done"], 2 * i)
                dve.tensor_tensor(sh_s[1], bank[1][:, :], sh_s[0], ALU.mult).then_inc(S["sh_ready"], 1)

            def combine(t, u, n, n_rows=128):
                sum_ = acc[u][0:n_rows, :]
                dve.wait_ge(h_loaded[u], 16 * (n + 1))
                dve.wait_ge(S["sd_done"], t + 1)
                dve.tensor_tensor(sum_, bank[2 + u][0:n_rows, 0:D], sum_, ALU.add).then_inc(S["acc_ready"], 1)
                dve.wait_ge(S["acc_ready"], t + 1)
                dve.wait_ge(cg_loaded[u], 16 * TOPK * (n + 1))
                for k in range(TOPK):
                    ins = dve.scalar_tensor_tensor(sum_, cg[u][0:n_rows, k, :], wk_t[0:n_rows, t, k:k + 1], sum_, ALU.mult, ALU.add)
                    if k < TOPK - 1:
                        ins.then_inc(S["acc_step"], 1)
                        dve.wait_ge(S["acc_step"], (TOPK - 1) * t + k + 1)
                ins.then_inc(S["combined"], 1)
            dve.wait_ge(S["wk_loaded"], 32)
            shared_product(0)
            combine(0, 0, 0)
            combine(1, 1, 0)
            with dve.Fori(1, FULL // 2) as i:
                shared_product(i)
                for u in range(2):
                    combine(2 * i + u, u, i)
            shared_product(FULL // 2)
            combine(FULL, 0, FULL // 2, REST)


def kernel(**inputs):
    import numpy as np
    import concourse.bacc as bacc
    from concourse.bass_utils import run_bass_kernel_spmd

    g = {k: np.asarray(v) for k, v in inputs.items()}
    at, ff = "L0_attn_", "L0_ffn_"
    p = g["x"].reshape(SEQS, 3, 6, 16, 6, 16).transpose(0, 2, 4, 1, 3, 5).reshape(SEQS, 36, KP * 128)
    full = np.zeros((NT * PER, SEQ, KP * 128), np.float32)
    full[:SEQS, 1:] = p
    patches = full.reshape(NT, TP, KP, 128).transpose(0, 3, 2, 1).reshape(NT, 128, KP * TP)

    vec = np.zeros((128, NVEC), np.float32)
    for name, key in (("n1w", "norm1_w"), ("n1b", "norm1_b"), ("bq", "bq"), ("bk", "bk"), ("bg", "bg"),
                      ("gnw", "gn_w"), ("gnb", "gn_b"), ("n2w", "norm2_w"), ("n2b", "norm2_b")):
        vec[:, VEC[name]:VEC[name] + 2] = g[at + key].reshape(2, 128).T
    for s, name in enumerate(("b_u", "b_g")):
        for j, m in enumerate(MS):
            vec[:m, VEC[name] + j] = g[at + "b_in"][s * HID + j * HM:s * HID + j * HM + m]
    eg, eu, ed = (g[ff + n] for n in ("eg_w", "eu_w", "ed_w"))
    gu = np.stack([eg.transpose(0, 2, 1), eu.transpose(0, 2, 1)], 2).reshape(NE, 2, 128, 256).transpose(0, 2, 1, 3)
    moe = np.concatenate([gu.reshape(NE, 128, 512), ed.transpose(0, 2, 1)], 2)

    gamma = (1.0 - np.exp2(-5.0 - np.arange(NH, dtype=np.float32))).astype(np.float32)
    key, query = np.arange(TP)[:, None, None], np.arange(TP)[None, None, :]
    diff = (query - key).astype(np.float32)
    same = (key // SEQ == query // SEQ) & (diff >= 0)
    decay = np.where(same, np.exp(np.log(gamma)[None, :, None] * np.maximum(diff, 0)) * np.float32(HD ** -0.5), 0)
    p128 = np.arange(128)
    arrays = {
        "patches": patches, "w_tok": g["L0_tok_W"], "b_tok": g["L0_tok_b"], "cls": g["cls_tok"].reshape(1, D),
        "wq": g[at + "wq"], "wk": g[at + "wk"], "wg": g[at + "wg"], "wv": g[at + "wv"], "wo": g[at + "wo"],
        "bv": g[at + "bv"], "bo": g[at + "bo"], "b_out": g[at + "b_out"],
        "w_in": g[at + "w_in"], "w_out": g[at + "w_out"],
        "sgT": g[ff + "sg_w"].T, "suT": g[ff + "su_w"].T, "sdT": g[ff + "sd_w"].T, "gateT": g[ff + "gate_w"].T,
        "gate_bias": g[ff + "gate_bias"], "moe": moe, "c_vec": vec,
        "c_ident": np.eye(128), "c_hmask": (p128[:, None] // HD == np.arange(8)[None]),
        "c_tri": np.triu(np.ones((TP, TP)), 1), "c_decay": decay.reshape(TP, NH * TP),
        "c_io64": np.arange(NE), "c_ebase": np.arange(NE) * SLOT_BLOCKS * 128,
        "c_bcol": p128[:, None] + np.array([[0, 128]]),
        "c_tid": np.arange(TP)[:, None] + TP * np.arange(NT)[None],
    }
    arrays = {n: np.ascontiguousarray(v, dtype=np.float32) for n, v in arrays.items()}

    nc = bacc.Bacc("TRN2", target_bir_lowering=False, num_devices=1)
    aps = {n: nc.dram_tensor(f"in_{n}", v.shape, mybir.dt.from_np(v.dtype), kind="ExternalInput").ap() for n, v in arrays.items()}
    out = nc.dram_tensor("out_0", (SEQS * SEQ, D), F32, kind="ExternalOutput").ap()
    build(nc, aps, out)
    r = run_bass_kernel_spmd(nc, [{f"in_{n}": v for n, v in arrays.items()}], core_ids=[0])
    return r.results[0]["out_0"].reshape(SEQS, SEQ, D)
```
